# Optimizing a Trainium2 kernel written in Bass

```python
import numpy as np
import jax
import jax.numpy as jnp

def _softmax(x, axis=-1):
    return jax.nn.softmax(x, axis=axis)

def _gelu(x):
    return jax.nn.gelu(x, approximate=True)

def _silu(x):
    return jax.nn.silu(x)

def _sigmoid(x):
    return jax.nn.sigmoid(x)

def _layernorm(x, axis=-1, eps=1e-05):
    m = jnp.mean(x, axis=axis, keepdims=True)
    v = jnp.var(x, axis=axis, keepdims=True)
    return (x - m) / jnp.sqrt(v + eps)

def _scatter_add(tgt, idx, src, axis=0):
    return tgt.at[idx].add(src)

def _segment_sum(src, seg, n):
    return jax.ops.segment_sum(src, seg, n)
kernel_name = 'mk_flamingo_gated_d2_seqx_r4_58bee1'

def setup_inputs(seed: int=0):
    np.random.seed(seed)
    _w = jnp.asarray

    def _rec_inputs():
        import jax
        import jax.numpy as jnp
        _rk = jax.random.key(seed)
        x = -0.000125 + 0.9999 * jax.random.normal(jax.random.fold_in(_rk, 1), (16, 100, 512), jnp.float32)
        _lenS = 100 - jax.random.randint(jax.random.fold_in(_rk, 7), (16,), 0, max(1, 100 // 4) + 1, jnp.int32)
        _lenS2 = 361 - jax.random.randint(jax.random.fold_in(_rk, 8), (16,), 0, max(1, 361 // 4) + 1, jnp.int32)
        _ctx_2048P = jax.random.normal(jax.random.fold_in(_rk, 11), (16, 16, 512), jnp.float32)
        _ctx_2048c = jax.random.dirichlet(jax.random.fold_in(_rk, 511), 0.3 * jnp.ones((16,), jnp.float32), (16, 361))
        _ctx_2048t = jnp.einsum('bsk,bkd->bsd', _ctx_2048c, _ctx_2048P)
        _ctx_2048t = _ctx_2048t * jax.lax.rsqrt(jnp.mean(jnp.square(_ctx_2048t)) + 1e-12) * 0.953939
        ctx_2048 = -1.52775e-05 + 0.999936 * (_ctx_2048t + 0.3 * jax.random.normal(jax.random.fold_in(_rk, 611), (16, 361, 512), jnp.float32))
        _validS = jnp.arange(100)[None, :] < _lenS[:, None]
        _validS2 = jnp.arange(361)[None, :] < _lenS2[:, None]
        _causal = jnp.tril(jnp.ones((100, 100), dtype=bool))
        mask_BxS2_ff1 = jnp.where(jnp.ones((16, 361), dtype=bool), 1.0, 0.0).astype(jnp.float32)
        mask_BxS2_bf1 = jnp.ones((16, 361), dtype=bool)
        _g = jax.random.normal(jax.random.fold_in(_rk, 9001), (2, 2), jnp.float32)
        _g = jnp.sign(_g) * jnp.maximum(jnp.abs(_g), 1.0) + (_g == 0) * 1.0
        g_xattn = _g[0]
        g_ffn = _g[1]
        return (x, ctx_2048, mask_BxS2_ff1, mask_BxS2_bf1, g_xattn, g_ffn)
    x, ctx_2048, mask_BxS2_ff1, mask_BxS2_bf1, g_xattn, g_ffn = _rec_inputs()

    def _L0_xattn_setup():
        import jax, jax.numpy as jnp
        import numpy as np
        H = 512
        NH = 16
        HD = H // NH
        FD = 64
        key = jax.random.key(seed)
        ks = jax.random.split(key, 12)
        B, S = (4, 1024)
        s = 1.0 / np.sqrt(H)
        sf = 1.0 / np.sqrt(HD)
        return {'query': jax.random.normal(ks[0], (B, S, H), jnp.float32), 'key': jax.random.normal(ks[1], (B, S, H), jnp.float32), 'value': jax.random.normal(ks[2], (B, S, H), jnp.float32), 'attention_mask': jnp.ones((B, S), jnp.float32), 'Wq': jax.random.normal(ks[3], (H, H), jnp.float32) * s, 'bq': jnp.zeros((H,), jnp.float32), 'Wk': jax.random.normal(ks[4], (H, H), jnp.float32) * s, 'bk': jnp.zeros((H,), jnp.float32), 'Wv': jax.random.normal(ks[5], (H, H), jnp.float32) * s, 'bv': jnp.zeros((H,), jnp.float32), 'Wqf': jax.random.normal(ks[6], (FD, HD), jnp.float32) * sf, 'Wkf': jax.random.normal(ks[7], (FD, HD), jnp.float32) * sf, 'Wo': jax.random.normal(ks[8], (H, H), jnp.float32) * s, 'bo': jnp.zeros((H,), jnp.float32)}
    _L0_xattn_all = _L0_xattn_setup()
    _L0_xattn_in = {k: v for k, v in _L0_xattn_all.items() if k in ('Wq', 'bq', 'Wk', 'bk', 'Wv', 'bv', 'Wqf', 'Wkf', 'Wo', 'bo')}
    del _L0_xattn_all

    def _L0_ffn_setup():
        import jax, jax.numpy as jnp
        import numpy as np
        B, S, H = (2, 256, 512)
        E, K = (8, 2)
        I = 352
        IS = 1408
        WSCALE = 0.02
        key = jax.random.key(seed)
        ks = jax.random.split(key, 9)
        f32 = jnp.float32
        return {'hidden_states': jax.random.normal(ks[0], (B, S, H), dtype=f32), 'gate_w': jax.random.normal(ks[1], (E, H), dtype=f32) * WSCALE, 'w_gate': jax.random.normal(ks[2], (E, H, I), dtype=f32) * WSCALE, 'w_up': jax.random.normal(ks[3], (E, H, I), dtype=f32) * WSCALE, 'w_down': jax.random.normal(ks[4], (E, I, H), dtype=f32) * WSCALE, 'sw_gate': jax.random.normal(ks[5], (H, IS), dtype=f32) * WSCALE, 'sw_up': jax.random.normal(ks[6], (H, IS), dtype=f32) * WSCALE, 'sw_down': jax.random.normal(ks[7], (IS, H), dtype=f32) * WSCALE, 'shared_gate_w': jax.random.normal(ks[8], (H, 1), dtype=f32) * WSCALE}
    _L0_ffn_all = _L0_ffn_setup()
    _L0_ffn_in = {k: v for k, v in _L0_ffn_all.items() if k in ('gate_w', 'w_gate', 'w_up', 'w_down', 'sw_gate', 'sw_up', 'sw_down', 'shared_gate_w')}
    del _L0_ffn_all

    def _L1_xattn_setup():
        import jax, jax.numpy as jnp
        import numpy as np
        import math
        D_MODEL = 512
        N_Q_HEADS = 16
        N_KV_HEADS = 4
        HEAD_DIM = D_MODEL // N_Q_HEADS
        B = 4
        S = 256

        def _alibi_slopes(num_heads):
            n = 2 ** int(math.floor(math.log2(num_heads)))
            m0 = 2.0 ** (-8.0 / n)
            return m0 ** jnp.arange(1, n + 1, dtype=jnp.float32)
        key = jax.random.key(seed)
        ks = jax.random.split(key, 8)
        xavier = lambda k, fi, fo: jax.random.normal(k, (fi, fo), jnp.float32) * math.sqrt(2.0 / (fi + fo))
        return {'query': jax.random.normal(ks[0], (B, S, D_MODEL), jnp.float32), 'key': jax.random.normal(ks[1], (B, S, D_MODEL), jnp.float32), 'value': jax.random.normal(ks[2], (B, S, D_MODEL), jnp.float32), 'mask': jnp.ones((B, S), dtype=bool), 'Wq': xavier(ks[3], D_MODEL, N_Q_HEADS * HEAD_DIM), 'Wk': xavier(ks[4], D_MODEL, N_KV_HEADS * HEAD_DIM), 'Wv': xavier(ks[5], D_MODEL, N_KV_HEADS * HEAD_DIM), 'Wo': xavier(ks[6], D_MODEL, D_MODEL)}
    _L1_xattn_all = _L1_xattn_setup()
    _L1_xattn_in = {k: v for k, v in _L1_xattn_all.items() if k in ('Wq', 'Wk', 'Wv', 'Wo')}
    del _L1_xattn_all

    def _L1_ffn_setup():
        import jax, jax.numpy as jnp
        import numpy as np
        B, S, H, I, E, TOP_K, NS = (2, 512, 512, 352, 8, 2, 2)
        SI = I * NS
        INIT = 0.02
        key = jax.random.key(seed)
        ks = jax.random.split(key, 9)
        f32 = jnp.float32
        return {'hidden_states': jax.random.normal(ks[0], (B, S, H), f32), 'router_w': jax.random.normal(ks[1], (E, H), f32) * INIT, 'gate_w': jax.random.normal(ks[2], (E, H, I), f32) * INIT, 'up_w': jax.random.normal(ks[3], (E, H, I), f32) * INIT, 'down_w': jax.random.normal(ks[4], (E, I, H), f32) * INIT, 's_gate_w': jax.random.normal(ks[5], (H, SI), f32) * INIT, 's_gate_b': jnp.zeros((SI,), f32), 's_up_w': jax.random.normal(ks[6], (H, SI), f32) * INIT, 's_up_b': jnp.zeros((SI,), f32), 's_down_w': jax.random.normal(ks[7], (SI, H), f32) * INIT, 's_down_b': jnp.zeros((H,), f32)}
    _L1_ffn_all = _L1_ffn_setup()
    _L1_ffn_in = {k: v for k, v in _L1_ffn_all.items() if k in ('router_w', 'gate_w', 'up_w', 'down_w', 's_gate_w', 's_gate_b', 's_up_w', 's_up_b', 's_down_w', 's_down_b')}
    del _L1_ffn_all
    return {'x': x, 'ctx_2048': ctx_2048, 'mask_BxS2_ff1': mask_BxS2_ff1, 'mask_BxS2_bf1': mask_BxS2_bf1, 'g_xattn': g_xattn, 'g_ffn': g_ffn, 'L0_xattn_Wq': _L0_xattn_in['Wq'], 'L0_xattn_bq': _L0_xattn_in['bq'], 'L0_xattn_Wk': _L0_xattn_in['Wk'], 'L0_xattn_bk': _L0_xattn_in['bk'], 'L0_xattn_Wv': _L0_xattn_in['Wv'], 'L0_xattn_bv': _L0_xattn_in['bv'], 'L0_xattn_Wqf': _L0_xattn_in['Wqf'], 'L0_xattn_Wkf': _L0_xattn_in['Wkf'], 'L0_xattn_Wo': _L0_xattn_in['Wo'], 'L0_xattn_bo': _L0_xattn_in['bo'], 'L0_ffn_gate_w': _L0_ffn_in['gate_w'], 'L0_ffn_w_gate': _L0_ffn_in['w_gate'], 'L0_ffn_w_up': _L0_ffn_in['w_up'], 'L0_ffn_w_down': _L0_ffn_in['w_down'], 'L0_ffn_sw_gate': _L0_ffn_in['sw_gate'], 'L0_ffn_sw_up': _L0_ffn_in['sw_up'], 'L0_ffn_sw_down': _L0_ffn_in['sw_down'], 'L0_ffn_shared_gate_w': _L0_ffn_in['shared_gate_w'], 'L1_xattn_Wq': _L1_xattn_in['Wq'], 'L1_xattn_Wk': _L1_xattn_in['Wk'], 'L1_xattn_Wv': _L1_xattn_in['Wv'], 'L1_xattn_Wo': _L1_xattn_in['Wo'], 'L1_ffn_router_w': _L1_ffn_in['router_w'], 'L1_ffn_gate_w': _L1_ffn_in['gate_w'], 'L1_ffn_up_w': _L1_ffn_in['up_w'], 'L1_ffn_down_w': _L1_ffn_in['down_w'], 'L1_ffn_s_gate_w': _L1_ffn_in['s_gate_w'], 'L1_ffn_s_gate_b': _L1_ffn_in['s_gate_b'], 'L1_ffn_s_up_w': _L1_ffn_in['s_up_w'], 'L1_ffn_s_up_b': _L1_ffn_in['s_up_b'], 'L1_ffn_s_down_w': _L1_ffn_in['s_down_w'], 'L1_ffn_s_down_b': _L1_ffn_in['s_down_b']}

def reference(x, ctx_2048, mask_BxS2_ff1, mask_BxS2_bf1, g_xattn, g_ffn, L0_xattn_Wq, L0_xattn_bq, L0_xattn_Wk, L0_xattn_bk, L0_xattn_Wv, L0_xattn_bv, L0_xattn_Wqf, L0_xattn_Wkf, L0_xattn_Wo, L0_xattn_bo, L0_ffn_gate_w, L0_ffn_w_gate, L0_ffn_w_up, L0_ffn_w_down, L0_ffn_sw_gate, L0_ffn_sw_up, L0_ffn_sw_down, L0_ffn_shared_gate_w, L1_xattn_Wq, L1_xattn_Wk, L1_xattn_Wv, L1_xattn_Wo, L1_ffn_router_w, L1_ffn_gate_w, L1_ffn_up_w, L1_ffn_down_w, L1_ffn_s_gate_w, L1_ffn_s_gate_b, L1_ffn_s_up_w, L1_ffn_s_up_b, L1_ffn_s_down_w, L1_ffn_s_down_b):
    import jax
    import jax.numpy as jnp

    def _L0_xattn_ref(query, key, value, attention_mask, Wq, bq, Wk, bk, Wv, bv, Wqf, Wkf, Wo, bo):
        import jax, jax.numpy as jnp
        import numpy as np
        H = 512
        NH = 16
        HD = H // NH
        FD = 64
        B, Sq, _ = query.shape
        Sk = key.shape[1]

        def heads(x, W, b, S):
            return (x @ W.T + b).reshape(B, S, NH, HD).transpose(0, 2, 1, 3)
        q = heads(query, Wq, bq, Sq)
        k = heads(key, Wk, bk, Sk)
        v = heads(value, Wv, bv, Sk)
        q_prime = jax.nn.relu(jnp.einsum('bhnd,fd->bhnf', q, Wqf))
        k_prime = jax.nn.relu(jnp.einsum('bhnd,fd->bhnf', k, Wkf))
        k_prime = k_prime * attention_mask[:, None, :, None]
        kv = jnp.einsum('bhnf,bhne->bhfe', k_prime, v)
        qkv = jnp.einsum('bhmf,bhfe->bhme', q_prime, kv)
        k_sum = jnp.sum(k_prime, axis=2)
        qk_sum = jnp.einsum('bhmf,bhf->bhm', q_prime, k_sum)[..., None]
        out = qkv / (qk_sum + 1e-08)
        out = out.transpose(0, 2, 1, 3).reshape(B, Sq, H)
        return out @ Wo.T + bo

    def _L0_ffn_ref(hidden_states, gate_w, w_gate, w_up, w_down, sw_gate, sw_up, sw_down, shared_gate_w):
        import jax, jax.numpy as jnp
        import numpy as np
        B, S, H = (2, 256, 512)
        E, K = (8, 2)
        I = 352
        IS = 1408
        WSCALE = 0.02
        x = hidden_states
        logits = jnp.einsum('bsh,eh->bse', x, gate_w)
        probs = jax.nn.softmax(logits, axis=-1)
        top_w, top_i = jax.lax.top_k(probs, K)
        top_w = top_w / jnp.sum(top_w, axis=-1, keepdims=True)
        onehot = jax.nn.one_hot(top_i, E, dtype=x.dtype)
        combine = jnp.einsum('bsk,bske->bse', top_w, onehot)
        g = jnp.einsum('bsh,ehi->besi', x, w_gate)
        u = jnp.einsum('bsh,ehi->besi', x, w_up)
        h = jax.nn.silu(g) * u
        expert_out = jnp.einsum('besi,eih->besh', h, w_down)
        moe_out = jnp.einsum('besh,bse->bsh', expert_out, combine)
        sh = jax.nn.silu(x @ sw_gate) * (x @ sw_up)
        shared_out = sh @ sw_down
        shared_gate = jax.nn.sigmoid(x @ shared_gate_w)
        return moe_out + shared_out * shared_gate

    def _L1_xattn_ref(query, key, value, mask, Wq, Wk, Wv, Wo):
        import jax, jax.numpy as jnp
        import numpy as np
        import math
        D_MODEL = 512
        N_Q_HEADS = 16
        N_KV_HEADS = 4
        HEAD_DIM = D_MODEL // N_Q_HEADS
        B = 4
        S = 256

        def _alibi_slopes(num_heads):
            n = 2 ** int(math.floor(math.log2(num_heads)))
            m0 = 2.0 ** (-8.0 / n)
            return m0 ** jnp.arange(1, n + 1, dtype=jnp.float32)
        b, q_len, d = query.shape
        kv_len = key.shape[1]
        G = N_KV_HEADS
        Hpg = N_Q_HEADS // G
        dh = HEAD_DIM
        Q = (query @ Wq).reshape(b, q_len, G, Hpg, dh)
        K = (key @ Wk).reshape(b, kv_len, G, dh)
        V = (value @ Wv).reshape(b, kv_len, G, dh)
        Q = Q / math.sqrt(dh)
        scores = jnp.einsum('bqghd,bkgd->bghqk', Q, K)
        rel = jnp.arange(kv_len, dtype=jnp.float32)[None, :] - jnp.arange(q_len, dtype=jnp.float32)[:, None]
        m = _alibi_slopes(N_Q_HEADS).reshape(1, G, Hpg, 1, 1)
        scores = scores + m * rel[None, None, None]
        neg = jnp.finfo(scores.dtype).min
        scores = jnp.where(mask[:, None, None, None, :], scores, neg)
        w = jax.nn.softmax(scores, axis=-1)
        out = jnp.einsum('bghqk,bkgd->bqghd', w, V)
        out = out.reshape(b, q_len, G * Hpg * dh)
        return out @ Wo

    def _L1_ffn_ref(hidden_states, router_w, gate_w, up_w, down_w, s_gate_w, s_gate_b, s_up_w, s_up_b, s_down_w, s_down_b):
        import jax, jax.numpy as jnp
        import numpy as np
        B, S, H, I, E, TOP_K, NS = (2, 512, 512, 352, 8, 2, 2)
        SI = I * NS
        INIT = 0.02
        b, s, h = hidden_states.shape
        x = hidden_states.reshape(-1, h)
        T = x.shape[0]
        num_experts = router_w.shape[0]
        logits = x @ router_w.T
        probs = jax.nn.softmax(logits.astype(jnp.float32), axis=-1)
        topk_w, topk_idx = jax.lax.top_k(probs, TOP_K)
        topk_w = topk_w / jnp.sum(topk_w, axis=-1, keepdims=True)
        combine = jnp.zeros((T, num_experts), probs.dtype)
        combine = combine.at[jnp.arange(T)[:, None], topk_idx].add(topk_w)

        def expert_step(acc, ws):
            gw, uw, dw, ce = ws
            out = jax.nn.silu(x @ gw) * (x @ uw) @ dw
            return (acc + ce[:, None].astype(out.dtype) * out, None)
        moe_out, _ = jax.lax.scan(expert_step, jnp.zeros_like(x), (gate_w, up_w, down_w, combine.T))
        shared = jax.nn.silu(x @ s_gate_w + s_gate_b) * (x @ s_up_w + s_up_b) @ s_down_w + s_down_b
        return (moe_out + shared).reshape(b, s, h)
    x = x + jnp.tanh(g_xattn[0]) * _L0_xattn_ref(_layernorm(x, axis=-1), ctx_2048, ctx_2048, mask_BxS2_ff1, L0_xattn_Wq, L0_xattn_bq, L0_xattn_Wk, L0_xattn_bk, L0_xattn_Wv, L0_xattn_bv, L0_xattn_Wqf, L0_xattn_Wkf, L0_xattn_Wo, L0_xattn_bo)
    x = x + jnp.tanh(g_ffn[0]) * _L0_ffn_ref(_layernorm(x, axis=-1), L0_ffn_gate_w, L0_ffn_w_gate, L0_ffn_w_up, L0_ffn_w_down, L0_ffn_sw_gate, L0_ffn_sw_up, L0_ffn_sw_down, L0_ffn_shared_gate_w)
    x = x + jnp.tanh(g_xattn[1]) * _L1_xattn_ref(_layernorm(x, axis=-1), ctx_2048, ctx_2048, mask_BxS2_bf1, L1_xattn_Wq, L1_xattn_Wk, L1_xattn_Wv, L1_xattn_Wo)
    x = x + jnp.tanh(g_ffn[1]) * _L1_ffn_ref(_layernorm(x, axis=-1), L1_ffn_router_w, L1_ffn_gate_w, L1_ffn_up_w, L1_ffn_down_w, L1_ffn_s_gate_w, L1_ffn_s_gate_b, L1_ffn_s_up_w, L1_ffn_s_up_b, L1_ffn_s_down_w, L1_ffn_s_down_b)
    return x

_drawn_inputs = setup_inputs


def setup_inputs(seed=0):
    import zlib

    import numpy as np

    out = dict(_drawn_inputs(seed))
    spreads = {'g_ffn': (-1.0, 0.6),
     'L0_xattn_bq': (0.0, 0.8),
     'L0_xattn_bk': (0.0, 0.8),
     'L0_xattn_bv': (0.0, 0.1),
     'L0_xattn_bo': (0.0, 0.1),
     'L1_ffn_s_gate_b': (0.0, 0.8),
     'L1_ffn_s_up_b': (0.0, 0.8),
     'L1_ffn_s_down_b': (0.0, 0.1)}
    factors = {'L0_ffn_gate_w': 3.635,
     'L0_ffn_w_gate': 3.187,
     'L0_ffn_w_up': 3.123,
     'L0_ffn_w_down': 3.126,
     'L0_ffn_shared_gate_w': 8.0,
     'L1_ffn_router_w': 3.573,
     'L1_ffn_gate_w': 3.166,
     'L1_ffn_up_w': 3.094,
     'L1_ffn_down_w': 3.093}
    for name, (base, spread) in spreads.items():
        noise = np.random.default_rng([zlib.crc32(name.encode()), seed]).standard_normal(out[name].shape)
        drawn = base * np.exp(spread * noise) if base else spread * noise
        out[name] = jnp.asarray(drawn.astype(out[name].dtype))
    for name, factor in factors.items():
        out[name] = (out[name] * factor).astype(out[name].dtype)
    return out
```

```python
from contextlib import ExitStack

import concourse.bass as bass
from concourse import mybir

F32 = mybir.dt.float32
F16 = mybir.dt.float16
U8 = mybir.dt.uint8
U32 = mybir.dt.uint32
ALU = mybir.AluOpType
ACT = mybir.ActivationFunctionType
AX_X = mybir.AxisListType.X

P = 128
B, S, D = 16, 100, 512
SK = 361
KC = D // P
T = B * S
TT = (T + P - 1) // P
TP = TT * P
LAST = T - (TT - 1) * P
PAIRS = TT // 2
NCH = 4
CW = TP // NCH
KT = [(0, P), (P, P), (2 * P, SK - 2 * P)]
NH, HD, FD = 16, 32, 64
NG = 4
NPAIR = NH // 2
VW = HD + 1
E = 8
I = 352
IT = [(0, P), (P, P), (2 * P, I - 2 * P)]
IH = len(IT)
UNITS = NCH * IH
NBLK = (12, 10)
WS = 64.0
KVS = 256.0
PASSES = ((0, 0), (0, 1), (1, 0))
EPS_LN = 1e-5
EPS_DEN = 1e-8
NEG = -1e30
NAUG = HD + 3


class Count:

    def __init__(self, sem, first=0):
        self.sem, self.base, self.first, self.per = sem, 0, first, 0
        self.total = 0

    def span(self, times, per=1):
        new = Count(self.sem, self.first)
        new.base, new.per = self.total, per
        self.total += times * per
        return new

    def at(self, n=0, k=0):
        return n * self.per + (self.base + k + 1)

    def before(self, n=0, k=0):
        return n * self.per + (self.base + k + self.first)


class Banks:

    def __init__(self, full, free, uses, times, other=()):
        per = {}
        self.place = {}
        for name, bank in uses:
            self.place[name] = (bank, per.get(bank, 0))
            per[bank] = per.get(bank, 0) + 1
        self.f = {b: full[b].span(times, n) for b, n in per.items()}
        self.r = {b: free[b].span(times, n) for b, n in per.items() if b not in other}

    def bank(self, name):
        return self.place[name][0]

    def written(self, eng, name, n=0):
        b, k = self.place[name]
        eng.wait_ge(self.f[b].sem, self.f[b].at(n, k))

    def free(self, eng, name, n=0):
        b, k = self.place[name]
        eng.wait_ge(self.r[b].sem, self.r[b].before(n, k))

    def full_sem(self, name):
        return self.f[self.place[name][0]].sem

    def free_sem(self, name):
        return self.r[self.place[name][0]].sem


def build(nc, a, out, stop=4):
    with ExitStack() as ctx:
        def sb(name, shape, dt=F32):
            return ctx.enter_context(nc.sbuf_tensor(name, shape, dt))

        x = sb("x", [P, TT, D])
        nT = [sb("nT_hi", [P, KC, TP], F16), sb("nT_lo", [P, KC, TP], F16)]
        big = sb("big", [P, NPAIR * TP])
        work_words = 3 * (2 * KC * I + IH * D)
        work = sb("work", [P, work_words])
        wq, wk, wv, wo = ([sb(f"{w}_{h}", [P, KC, D], F16) for h in ("hi", "lo")] for w in ("wq", "wk", "wv", "wo"))
        norm = [sb(f"norm{i}", [P, D]) for i in range(2)]
        ident = sb("ident", [P, P])
        cols = sb("cols", [P, 64])
        stats = sb("stats", [P, TT, 6])
        mv = sb("mv", [P, TT, 2])
        rstd = sb("rstd", [P, TT])
        mhalf = sb("mhalf", [P, TT])
        mask_c = sb("mask_c", [P, B, 3])
        route_s = [sb(f"route_s{i}", [P, KC, 16]) for i in range(2)]
        route_w = [[sb(f"route_w{i}{h}", [P, KC, 16], F16) for h in range(2)] for i in range(2)]
        logit = sb("logit", [P, TT, 16])
        top = sb("top", [P, TT, 8])
        topi = sb("topi", [P, TT, 8], U32)
        comb = sb("comb", [P, TT, 12])
        iota8 = sb("iota8", [P, E])
        rt = sb("rt", [P, 8, TT])
        oh = sb("oh", [P, 2, TT, E])
        bias_gu = sb("bias_gu", [P, NBLK[1], IH, 2])
        bias_now = sb("bias_now", [P, 2, IH, 2])
        bias_v = sb("bias_v", [P, D])
        bias_o = sb("bias_o", [P, D])
        bias_d = sb("bias_d", [P, D])
        psum = ctx.enter_context(nc.psum_tensor("psum", [P, 8, 512], F32))

        bq, bk = cols[:, 0:4], cols[:, 4:8]
        gate, gate_in = cols[:, 8:12], cols[:, 12:16]
        den, rden = cols[:, 16:32], cols[:, 32:48]
        gate_s = cols[:, 48:52]
        tick = cols[:, 52:53]
        nmax = cols[:, 53:55]

        used = [0]

        def carve(n, dt, pattern=None, rows=slice(0, P), **dims):
            v = work[rows, used[0]:used[0] + n]
            used[0] += n
            if dt != F32:
                v = v.bitcast(dt)
            return v.rearrange(pattern, **dims) if pattern else v

        CT = KC * SK
        ctx_f = carve(CT, F32, "p (k s) -> p k s", k=KC)
        ctx_s = [carve(CT // 2, F16, "p (k s) -> p k s", k=KC) for _ in range(2)]
        shared_end = used[0]
        kT = [carve(CT // 2, F16, "p (k s) -> p k s", k=KC) for _ in range(2)]
        kf = carve(3 * NH * FD, F32, "p (t f) -> p t f", t=3)
        va = carve(3 * NH * VW, F32, "p (t h c) -> p t h c", t=3, h=NH)
        kv32 = carve(NH * VW, F32, "p (a c) -> p a c", a=NPAIR)
        kvb = [carve(NH * VW // 2, F16, "p (a c) -> p a c", a=NPAIR) for _ in range(2)]
        bd_k = [carve(128, F16) for _ in range(2)]
        bd_q = [carve(128, F16) for _ in range(2)]
        assert KC * CW <= 3 * NH * FD
        qh = [kf.rearrange("p t f -> p (t f)")[:, h * KC * CW // 2:(h + 1) * KC * CW // 2].bitcast(F16)
              .rearrange("p (m t) -> p m t", m=KC) for h in range(2)]
        qf = [big[:, h * NPAIR * TP // 2:(h + 1) * NPAIR * TP // 2].bitcast(F16)
              .rearrange("p (m t) -> p m t", m=NPAIR) for h in range(2)]
        stage = big[:, 0:KC * D].rearrange("p (k n) -> p k n", k=KC)
        bd_f = [big[:, KC * D + 256 * i:KC * D + 256 * (i + 1)] for i in range(2)]

        used[0] = shared_end
        aug = slice(0, NAUG)
        k1 = carve(NG * SK, F32, "p (g s) -> p g s", rows=aug, g=NG)
        q1 = carve(NH * S, F32, "p (h s) -> p h s", rows=aug, h=NH)
        v1 = carve(3 * P, F32, "p (t c) -> p t c", t=3)
        pr = [carve(3 * P, F32) for _ in range(2)]
        pT = [carve(3 * S, F32, "p (t s) -> p t s", t=3) for _ in range(2)]
        mask8 = carve(B * SK // 4, U8, "p (b s) -> p b s", rows=slice(HD, HD + 1), b=B)
        q1T = big[:, 0:KC * TP].rearrange("p (m t) -> p m t", m=KC)
        stage1 = [big[:, KC * TP + i * KC * D:KC * TP + (i + 1) * KC * D].rearrange("p (k n) -> p k n", k=KC)
                  for i in range(2)]

        hT = [big[:, h * IH * TP // 2:(h + 1) * IH * TP // 2].bitcast(F16)
              .rearrange("p (m t) -> p m t", m=IH) for h in range(2)]
        sil = [big[:, IH * TP + i * CW:IH * TP + (i + 1) * CW] for i in range(2)]
        h32 = [big[:, IH * TP + (2 + i) * CW:IH * TP + (3 + i) * CW] for i in range(2)]
        used[0] = 0
        GN = KC * I
        WN = 2 * GN + IH * D
        wst = carve(WN, F32)
        wsp = [[carve(WN // 2, F16) for h in range(2)] for s in range(2)]

        sems = {}

        def sem(name):
            sems[name] = ctx.enter_context(nc.semaphore(name))
            return sems[name]

        psum_full = [Count(sem(f"psum_full{b}")) for b in range(8)]
        psum_free = [Count(sem(f"psum_free{b}"), 1) for b in range(8)]
        hi_done = Count(sem("hi_done"))
        att_hi = Count(sem("att_hi"))
        x_loaded, const_loaded = sem("x_loaded"), sem("const_loaded")
        stage_full, stage_hi, stage_used = sem("stage_full"), sem("stage_hi"), sem("stage_used")
        dve_chain = Count(sem("dve_chain"))
        gates_ready = sem("gates_ready")
        phase = sem("phase")
        stats_ready, rstd_ready = sem("stats_ready"), sem("rstd_ready")
        norm_ready = Count(sem("norm_ready"))
        q_split = sem("q_split")
        ctx_loaded, ctx_hi = sem("ctx_loaded"), sem("ctx_hi")
        ctx_split = sem("ctx_split")
        kT_ready, va_ready, kf_ready = sem("kT_ready"), sem("va_ready"), sem("kf_ready")
        kv32_ready, kv_hi, kv_ready = sem("kv32_ready"), sem("kv_hi"), sem("kv_ready")
        den_ready, rden_ready = sem("den_ready"), sem("rden_ready")
        w_loaded, w_hi, w_split = sem("w_loaded"), sem("w_hi"), sem("w_split")
        sil_ready, h_ready, h_hi, hT_ready = sem("sil_ready"), sem("h_ready"), sem("h_hi"), sem("hT_ready")
        logits_ready, top_ready, route_exp = sem("logits_ready"), sem("top_ready"), sem("route_exp")
        mask_loaded, kv1_ready, nmax_ready = sem("mask_loaded"), sem("kv1_ready"), sem("nmax_ready")
        exp_done, pT_ready = sem("exp_done"), sem("pT_ready")
        x_ready = sem("x_ready")
        stored = sem("stored")

        def banks(uses, times, other=()):
            return Banks(psum_full, psum_free, uses, times, other)

        def pair_banks(name):
            return [banks([(name, par)], PAIRS + 1 - par) for par in range(2)]

        plan = {}
        LINEAR = ([(f"kT{m}", m % 2) for m in range(KC)] + [("v0", 2), ("v1", 3), ("v2", 2)]
                  + [(f"kf{t}{h}", 4 + h) for t in range(3) for h in range(2)]
                  + [("kv0", 6), ("kv1", 7), ("o0", 6), ("o1", 7), ("oT", 6)])
        SOFTMAX = ([(f"s{h}", h % 2) for h in range(NH)] + [(f"pT{h}", 2 + h % 2) for h in range(NH)]
                   + [("k", 7), ("v", 6), ("o", 4), ("oT", 5)])
        BLOCK = ([(f"{w}{u}", 2 * (u % 2) + n) for u in range(UNITS) for n, w in enumerate("gu")]
                 + [(f"d{t}", 4 + t % 4) for t in range(TT)])
        for layer in range(2):
            plan["ln", 2 * layer] = pair_banks("n")
            plan["q", layer] = banks([(f"q{m}", m) for m in range(KC)]
                                     + [(f"f{p}", 4 + p % 4) for p in range(NPAIR)] * (layer == 0), NCH)
            plan["att", layer] = banks((LINEAR, SOFTMAX)[layer], B, other=((), range(4))[layer])
            plan["out", layer] = pair_banks("w")
            plan["ln", 2 * layer + 1] = pair_banks("n")
            plan["route", layer] = banks([("l", 7)], 1)
            plan["ffn", layer] = banks(BLOCK, NBLK[layer], other=range(4))
        hi = {}
        for layer in range(2):
            hi["ln", 2 * layer] = hi_done.span(TT)
            hi["q", layer] = hi_done.span(NCH, (KC + NPAIR) * (layer == 0))
            hi["kT", layer] = hi_done.span(B, KC * (layer == 0))
            hi["oT", layer] = att_hi.span(B)
            hi["ln", 2 * layer + 1] = hi_done.span(TT)
        norms = {}
        for layer in range(2):
            norms["ln", 2 * layer] = norm_ready.span(TT)
            norms["att", layer] = norm_ready.span(B)
            norms["ln", 2 * layer + 1] = norm_ready.span(TT)

        def col(v, t, n=P):
            return v[:, :, bass.ds(t * n, n)]

        def row(v, t):
            return v[:, bass.ds(t, 1), :].rearrange("p o d -> p (o d)")

        def at1(v, t):
            return v[:, bass.ds(t, 1)]

        def in_pairs(eng, body):
            with eng.Fori(0, PAIRS) as j:
                body(j * 2, j, 0)
                body(j * 2 + 1, j, 1)
            body(TT - 1, PAIRS, 0)

        block = ctx.enter_context(nc.Block())
        CONSTS = [(ident[:], a["ident"]), (bq, a["bq"]), (bk, a["bk"]), (gate_in, a["gates"]),
                  (mask_c[:], a["mask_f"]), (iota8[:], a["iota8"]), (bias_gu[:], a["bias_gu"]),
                  (bias_v[:], a["bv"].partition_broadcast(P)), (bias_o[:], a["bo"].partition_broadcast(P)),
                  (bias_d[:], a["bd"].partition_broadcast(P)),
                  (route_s[0][:, :, 0:E + 1], a["route0"]), (route_s[1][:, :, 0:E], a["route1"])]
        N_CONST = len(CONSTS) + 2 * 4

        @block.sync
        def _(sp):
            for n in range(4):
                if n:
                    sp.wait_ge(stage_used, n)
                sp.dma_start(stage, a["w_attn0"][n]).then_inc(stage_full, 16)
                if n == 0:
                    sp.dma_start(x[:, 0:TT - 1, :], a["x"][0:(TT - 1) * P, :].rearrange("(t p) d -> p t d", p=P)).then_inc(x_loaded, 16)
                    sp.wait_ge(phase, 1)
                    sp.dma_start(x[0:LAST, TT - 1, :], a["x"][(TT - 1) * P:T, :]).then_inc(x_loaded, 16)
            sp.dma_start(ctx_f, a["ctxT"][0]).then_inc(ctx_loaded, 16)
            with sp.Fori(1, B) as b:
                sp.wait_ge(ctx_split, b)
                sp.dma_start(ctx_f, a["ctxT"][b]).then_inc(ctx_loaded, 16)

            def ffn_loads(layer):
                sp.wait_ge(phase, (3, 7)[layer])
                first = NBLK[0] * layer
                sp.dma_start(wst, a[f"w_blk{layer}"][0]).then_inc(w_loaded, 16)
                with sp.Fori(1, NBLK[layer]) as k:
                    sp.wait_ge(w_split, k + first)
                    sp.dma_start(wst, a[f"w_blk{layer}"][k]).then_inc(w_loaded, 16)

            if stop >= 2:
                ffn_loads(0)
            if stop >= 3:
                sp.wait_ge(phase, 5)
                sp.dma_start(stage1[0], a["w_attn1"][0]).then_inc(stage_full, 16)
                sp.dma_start(stage1[1], a["w_attn1"][1]).then_inc(stage_full, 16)
                sp.dma_start(q1[HD:NAUG], a["q_aug"]).then_inc(mask_loaded, 16)
                sp.dma_start(k1[HD + 1:NAUG], a["k_aug"]).then_inc(mask_loaded, 16)
                sp.dma_start(mask8, a["mask_b"]).then_inc(mask_loaded, 16)
                sp.wait_ge(stage_used, 7)
                sp.dma_start(stage1[0][:, :, 0:2 * P], a["w_kv1"]).then_inc(stage_full, 16)
                sp.dma_start(ctx_f, a["ctxT"][0]).then_inc(ctx_loaded, 16)
                with sp.Fori(1, B) as b:
                    sp.wait_ge(ctx_split, b + B)
                    sp.dma_start(ctx_f, a["ctxT"][b]).then_inc(ctx_loaded, 16)
            if stop >= 4:
                ffn_loads(1)
            sp.wait_ge(phase, {1: 3, 2: 5, 3: 7, 4: 9}[stop])
            sp.dma_start(out[0:(TT - 1) * P, :].rearrange("(t p) d -> p t d", p=P), x[:, 0:TT - 1, :]).then_inc(stored, 16)
            sp.dma_start(out[(TT - 1) * P:T, :], x[0:LAST, TT - 1, :]).then_inc(stored, 16)
            sp.wait_ge(stored, 32)

        @block.gpsimd
        def _(pool):
            pool.wait_ge(phase, 1)
            for dst, src in CONSTS:
                pool.dma_start(dst, src).then_inc(const_loaded, 16)
            for n, w in enumerate(("wkf", "wqf")):
                for j in range(4):
                    pool.dma_start(bd_f[n][HD * j:HD * (j + 1), FD * j:FD * (j + 1)], a[w]).then_inc(const_loaded, 16)
            for n in range(stop):
                pool.wait_ge(stats_ready, n + 1)
                nc.gpsimd.tensor_tensor(rstd[:], rstd[:], mhalf[:], ALU.pow).then_inc(rstd_ready, 1)

        @block.scalar
        def _(act):
            def layernorm_hi(n):
                def tile(t, j, par):
                    pl = plan["ln", n][par]
                    pl.written(act, "n", j)
                    nc.scalar.activation(col(nT[0], t), psum[:, par, :].rearrange("p (k t) -> p k t", k=KC),
                                         ACT.Copy).then_inc(hi_done.sem, 1)
                in_pairs(act, tile)

            act.wait_ge(const_loaded, 16 * N_CONST)
            nc.scalar.activation(gate, gate_in, ACT.Tanh).then_inc(gates_ready, 1)
            for n, dst in enumerate((wq, wk, wv, wo)):
                act.wait_ge(stage_full, 16 * (n + 1))
                nc.scalar.activation(dst[0][:], stage, ACT.Copy, scale=WS).then_inc(stage_hi, 1)
            for n, dst in enumerate((bd_k, bd_q)):
                nc.scalar.activation(dst[0], bd_f[n], ACT.Copy).then_inc(stage_hi, 1)
            for n in range(2):
                nc.scalar.activation(route_w[n][0][:], route_s[n][:], ACT.Copy, scale=WS).then_inc(stage_hi, 1)

            layernorm_hi(0)

            pl = plan["q", 0]
            with act.Fori(0, NCH) as c:
                act.wait_ge(phase, 2)
                for m in range(KC):
                    pl.written(act, f"q{m}", c)
                    nc.scalar.activation(qh[0][:, m, :], psum[:, m, 0:CW], ACT.Identity, bias=bq[:, m:m + 1]).then_inc(hi_done.sem, 1)
                for p in range(NPAIR):
                    pl.written(act, f"f{p}", c)
                    nc.scalar.activation(col(qf[0], c, CW)[:, p, :], psum[:, pl.bank(f"f{p}"), 0:CW], ACT.Relu).then_inc(hi_done.sem, 1)

            pl = plan["att", 0]

            def context(b):
                act.wait_ge(ctx_loaded, b * 16 + 16)
                nc.scalar.activation(ctx_s[0], ctx_f, ACT.Copy).then_inc(ctx_hi, 1)

            def keys(b):
                for m in range(KC):
                    pl.written(act, f"kT{m}", b)
                    nc.scalar.activation(kT[0][:, m, :], psum[:, m % 2, 0:SK], ACT.Identity, bias=bk[:, m:m + 1]).then_inc(hi_done.sem, 1)

            def split_kv(b):
                act.wait_ge(kv32_ready, b + 1)
                nc.scalar.activation(kvb[0], kv32, ACT.Copy).then_inc(kv_hi, 1)

            def att_columns(pl, b):
                pl.written(act, "oT", b)
                nc.scalar.activation(col(nT[0], b, S), psum[:, pl.bank("oT"), 0:KC * S].rearrange("p (k t) -> p k t", k=KC),
                                     ACT.Copy).then_inc(att_hi.sem, 1)

            act.wait_ge(phase, 3 - 1)
            context(0)
            keys(0)
            split_kv(0)
            with act.Fori(0, B - 1) as b:
                pl.written(act, "v2", b)
                context(b + 1)
                keys(b + 1)
                att_columns(pl, b)
                split_kv(b + 1)
            att_columns(pl, B - 1)

            def ffn(layer):
                layernorm_hi(2 * layer + 1)
                pl = plan["ffn", layer]
                first = NBLK[0] * layer
                act.wait_ge(top_ready, layer + 1)
                nc.scalar.activation(rt[:, 1, :], rt[:, 0, :], ACT.Exp, scale=1.0 / WS).then_inc(route_exp, 1)
                if layer == 0:
                    nc.scalar.activation(rt[:, 5, :], rt[:, 4, :], ACT.Sigmoid, scale=1.0 / WS).then_inc(route_exp, 1)

                def split_hi(k, par, reuse=None):
                    act.wait_ge(w_loaded, (k + first) * 16 + 16)
                    if reuse is not None:
                        pl.written(act, f"d{TT - 1}", reuse)
                    nc.scalar.activation(wsp[par][0], wst, ACT.Copy, scale=WS).then_inc(w_hi, 1)

                def units(k, par):
                    def unit_hi(u):
                        s, (c, m) = u % 2, divmod(u, IH)
                        mn = IT[m][1]
                        act.wait_ge(h_ready, (k + first) * UNITS + u + 1)
                        nc.scalar.activation(hT[0][0:mn, m, c * CW:(c + 1) * CW], h32[s][0:mn, :], ACT.Copy).then_inc(h_hi, 1)

                    for u in range(UNITS):
                        s, m = u % 2, u % IH
                        mn = IT[m][1]
                        pl.written(act, f"g{u}", k)
                        bias = bias_now[0:mn, par, m, 0:1] if layer else 0.0
                        nc.scalar.activation(sil[s][0:mn, :], psum[0:mn, 2 * s, 0:CW], ACT.Silu, bias=bias,
                                             scale=1.0 / WS).then_inc(sil_ready, 1)
                        if u:
                            unit_hi(u - 1)
                    unit_hi(UNITS - 1)

                split_hi(0, 0)
                units(0, 0)
                split_hi(1, 1)
                with act.Fori(0, NBLK[layer] // 2 - 1) as j:
                    for par in range(2):
                        k = j * 2 + 1 + par
                        units(k, 1 - par)
                        split_hi(k + 1, par, k - 1)
                units(NBLK[layer] - 1, 1)

            if stop >= 2:
                ffn(0)
            if stop >= 3:
                for n, dst in enumerate((wq, wo)):
                    act.wait_ge(stage_full, 16 * 6)
                    nc.scalar.activation(dst[0][:], stage1[n], ACT.Copy, scale=WS).then_inc(stage_hi, 1)
                act.wait_ge(stage_full, 16 * 7)
                nc.scalar.activation(wk[0][:, :, 0:2 * P], stage1[0][:, :, 0:2 * P], ACT.Copy, scale=WS).then_inc(stage_hi, 1)
                layernorm_hi(2)
                pl = plan["att", 1]

                def context1(b):
                    act.wait_ge(ctx_loaded, b * 16 + (16 + 16 * B))
                    nc.scalar.activation(ctx_s[0], ctx_f, ACT.Copy).then_inc(ctx_hi, 1)

                def heads(b):
                    for h in range(NH):
                        act.wait_ge(nmax_ready, b * NH + h + 1)
                        if h >= 2:
                            pl.written(act, f"pT{h - 2}", b)
                        nc.scalar.activation(pr[h % 2][0:S, 0:SK], psum[0:S, pl.bank(f"s{h}"), 0:SK], ACT.Exp,
                                             bias=nmax[0:S, h % 2:h % 2 + 1], accum_out=den[0:S, h:h + 1]).then_inc(exp_done, 1)

                context1(0)
                with act.Fori(0, B - 1) as b:
                    heads(b)
                    context1(b + 1)
                    att_columns(pl, b)
                heads(B - 1)
                att_columns(pl, B - 1)
            if stop >= 4:
                ffn(1)

        @block.vector
        def _(dve):
            chained = [0]

            def link(ins):
                chained[0] += 1
                ins.then_inc(dve_chain.sem, 1)
                dve.wait_ge(dve_chain.sem, chained[0])

            def end_phase():
                nc.vector.engine_nop().then_inc(phase, 1)

            for v in (x[:, TT - 1, :], bd_f[0], bd_f[1], route_s[0][:], route_s[1][:]):
                nc.vector.memset(v, 0.0)
            nc.vector.memset(mhalf[:], -0.5)
            for c in psum_free:
                nc.vector.engine_nop().then_inc(c.sem, 1)
            link(nc.vector.memset(comb[:], 1.0))
            end_phase()
            dve.wait_ge(const_loaded, 16 * N_CONST)
            for v in (bq, bk, bias_v[:]):
                link(nc.vector.tensor_scalar(v, v, WS, None, ALU.mult))
            link(nc.vector.tensor_scalar(mask_c[:], mask_c[:], 1.0 / WS, None, ALU.mult))
            dve.wait_ge(gates_ready, 1)
            link(nc.vector.tensor_scalar(gate_s[:, 0:2], gate[:, 0:2], 1.0 / WS, None, ALU.mult))
            link(nc.vector.tensor_scalar(gate_s[:, 2:4], gate[:, 2:4], 1.0 / (WS * WS), None, ALU.mult))
            for n, dst in enumerate((wq, wk, wv, wo)):
                dve.wait_ge(stage_hi, n + 1)
                nc.vector.scalar_tensor_tensor(out=dst[1][:], in0=stage, scalar=WS, in1=dst[0][:],
                                               op0=ALU.mult, op1=ALU.subtract).then_inc(stage_used, 1)
            dve.wait_ge(stage_hi, 8)
            for n, dst in enumerate((bd_k, bd_q)):
                nc.vector.tensor_tensor(dst[1], bd_f[n], dst[0], ALU.subtract)
            for n in range(2):
                ins = nc.vector.scalar_tensor_tensor(out=route_w[n][1][:], in0=route_s[n][:], scalar=WS, in1=route_w[n][0][:],
                                                     op0=ALU.mult, op1=ALU.subtract)
            ins.then_inc(stage_used, 1)
            nc.vector.memset(kv32, 0.0)
            dve.wait_ge(x_loaded, 32)

            def layernorm(n):
                for t in range(TT):
                    ins = nc.vector.bn_stats(stats[:, t, :], x[:, t, :])
                link(ins)
                for t in range(TT):
                    ins = nc.vector.bn_aggr(mv[:, t, :], stats[:, t, :])
                link(ins)
                nc.vector.tensor_scalar(rstd[:], mv[:, :, 1:2].rearrange("p t o -> p (t o)"), EPS_LN, None, ALU.add).then_inc(stats_ready, 1)
                dve.wait_ge(rstd_ready, n + 1)

                def normalise(t, j, par, reuse=True):
                    if reuse:
                        plan["ln", n][par].written(dve, "n", j - 1)
                    nc.vector.tensor_scalar(norm[par][:], row(x, t), mv[:, bass.ds(t, 1), 0:1].rearrange("p o s -> p (o s)"),
                                            at1(rstd, t), ALU.subtract, ALU.mult).then_inc(norm_ready.sem, 1)

                def low(t, j, par):
                    dve.wait_ge(hi_done.sem, hi["ln", n].at(t))
                    nc.vector.tensor_tensor(col(nT[1], t), psum[:, par, :].rearrange("p (k t) -> p k t", k=KC),
                                            col(nT[0], t), ALU.subtract).then_inc(psum_free[par].sem, 1)

                normalise(0, 0, 0, False)
                normalise(1, 0, 1, False)
                with dve.Fori(0, PAIRS - 1) as j:
                    normalise(j * 2 + 2, j + 1, 0)
                    low(j * 2, j, 0)
                    normalise(j * 2 + 3, j + 1, 1)
                    low(j * 2 + 1, j, 1)
                normalise(TT - 1, PAIRS, 0)
                for t in range(TT - 3, TT):
                    low(t, t // 2, t % 2)
                end_phase()

            layernorm(0)
            pl = plan["q", 0]
            with dve.Fori(0, NCH) as c:
                for m in range(KC):
                    dve.wait_ge(hi_done.sem, hi["q", 0].at(c, m))
                    nc.vector.scalar_tensor_tensor(out=qh[1][:, m, :], in0=psum[:, m, 0:CW], scalar=bq[:, m:m + 1],
                                                   in1=qh[0][:, m, :], op0=ALU.add, op1=ALU.subtract).then_inc(psum_free[m].sem, 1)
                for p in range(NPAIR):
                    dve.wait_ge(hi_done.sem, hi["q", 0].at(c, KC + p))
                    nc.vector.scalar_tensor_tensor(out=col(qf[1], c, CW)[:, p, :], in0=psum[:, pl.bank(f"f{p}"), 0:CW], scalar=0.0,
                                                   in1=col(qf[0], c, CW)[:, p, :], op0=ALU.max, op1=ALU.subtract).then_inc(pl.free_sem(f"f{p}"), 1)
            nc.vector.memset(va, WS).then_inc(q_split, 1)
            dve.wait_ge(q_split, 1)

            pl = plan["att", 0]

            def context(b):
                dve.wait_ge(ctx_hi, b + 1)
                nc.vector.tensor_tensor(ctx_s[1], ctx_f, ctx_s[0], ALU.subtract).then_inc(ctx_split, 1)

            def keys(b):
                for m in range(KC):
                    dve.wait_ge(hi_done.sem, hi["kT", 0].at(b, m))
                    nc.vector.scalar_tensor_tensor(out=kT[1][:, m, :], in0=psum[:, m % 2, 0:SK], scalar=bk[:, m:m + 1],
                                                   in1=kT[0][:, m, :], op0=ALU.add, op1=ALU.subtract).then_inc(psum_free[m % 2].sem, 1)

            def values(b):
                for t, (t0, tn) in enumerate(KT):
                    pl.written(dve, f"v{t}", b)
                    nc.vector.tensor_tensor(va[0:tn, t, :, 0:HD], psum[0:tn, pl.bank(f"v{t}"), :].rearrange("p (h c) -> p h c", h=NH),
                                            bias_v[0:tn, :].rearrange("p (h c) -> p h c", h=NH), ALU.add).then_inc(pl.free_sem(f"v{t}"), 1)

            def features(b):
                for t, (t0, tn) in enumerate(KT):
                    for half in range(2):
                        pl.written(dve, f"kf{t}{half}", b)
                        nc.vector.tensor_scalar(kf[0:tn, t, half * 512:(half + 1) * 512], psum[0:tn, 4 + half, :], 0.0,
                                                mask_c[0:tn, bass.ds(b, 1), t:t + 1].rearrange("p a c -> p (a c)"),
                                                ALU.max, ALU.mult).then_inc(psum_free[4 + half].sem, 1)

            def diagonal(b):
                for q in range(2):
                    pl.written(dve, f"kv{q}", b)
                    src = psum[:, 6 + q, 0:4 * 2 * VW].rearrange("p (a c) -> p a c", a=4)
                    nc.vector.tensor_scalar(kv32[0:64, 4 * q:4 * q + 4, 0:VW], src[0:64, :, 0:VW], 1.0 / KVS, None, ALU.mult)
                    nc.vector.tensor_scalar(kv32[64:128, 4 * q:4 * q + 4, VW:2 * VW], src[64:128, :, VW:2 * VW],
                                            1.0 / KVS, None, ALU.mult).then_inc(psum_free[6 + q].sem, 1)
                nc.vector.engine_nop().then_inc(kv32_ready, 1)
                dve.wait_ge(kv_hi, b + 1)
                nc.vector.tensor_tensor(kvb[1], kv32, kvb[0], ALU.subtract).then_inc(kv_ready, 1)

            def quotient(b, reuse=None):
                for q in range(2):
                    pl.written(dve, f"o{q}", b)
                    src = psum[0:S, 6 + q, 0:8 * VW].rearrange("p (h c) -> p h c", h=8)
                    ins = nc.vector.tensor_scalar(den[0:S, 8 * q:8 * q + 8], src[:, :, HD:VW].rearrange("p h c -> p (h c)"),
                                                  EPS_DEN * WS * WS * WS / (KVS * WS), None, ALU.add)
                ins.then_inc(den_ready, 1)
                dve.wait_ge(den_ready, b + 1)
                nc.vector.reciprocal(rden[0:S, :], den[0:S, :]).then_inc(rden_ready, 1)
                dve.wait_ge(rden_ready, b + 1)
                for q in range(2):
                    src = psum[0:S, 6 + q, 0:8 * VW].rearrange("p (h c) -> p h c", h=8)
                    ins = nc.vector.tensor_tensor(norm[0][0:S, 256 * q:256 * (q + 1)].rearrange("p (h c) -> p h c", h=8), src[:, :, 0:HD],
                                                  rden[0:S, 8 * q:8 * q + 8].unsqueeze(2).to_broadcast([S, 8, HD]), ALU.mult)
                    ins.then_inc(psum_free[6 + q].sem, 1)
                nc.vector.engine_nop().then_inc(norm_ready.sem, 1)

            def att_columns(layer, pl, b):
                dve.wait_ge(att_hi.sem, hi["oT", layer].at(b))
                nc.vector.tensor_tensor(col(nT[1], b, S), psum[:, pl.bank("oT"), 0:KC * S].rearrange("p (k t) -> p k t", k=KC),
                                        col(nT[0], b, S), ALU.subtract).then_inc(pl.free_sem("oT"), 1)

            context(0)
            keys(0)
            values(0)
            features(0)
            diagonal(0)
            with dve.Fori(0, B - 1) as b:
                context(b + 1)
                keys(b + 1)
                values(b + 1)
                quotient(b)
                features(b + 1)
                att_columns(0, pl, b)
                diagonal(b + 1)
            quotient(B - 1)
            att_columns(0, pl, B - 1)

            def project_out(layer):
                if layer == 0:
                    link(nc.vector.scalar_tensor_tensor(out=x[:], in0=bias_o[:].unsqueeze(1).to_broadcast([P, TT, D]), scalar=gate[:, 0:1],
                                                        in1=x[:], op0=ALU.mult, op1=ALU.add))
                nc.vector.engine_nop().then_inc(x_ready, 1)

                def tile(t, j, par):
                    pl = plan["out", layer][par]
                    pl.written(dve, "w", j)
                    nc.vector.scalar_tensor_tensor(out=row(x, t), in0=psum[:, par, :], scalar=gate_s[:, layer:layer + 1], in1=row(x, t),
                                                   op0=ALU.mult, op1=ALU.add).then_inc(psum_free[par].sem, 1)
                in_pairs(dve, tile)
                link(nc.vector.engine_nop())
                end_phase()

            project_out(0)

            def ffn(layer):
                layernorm(2 * layer + 1)
                first = NBLK[0] * layer
                plan["route", layer].written(dve, "l")
                link(nc.vector.tensor_copy(logit[:], psum[:, 7, 0:TT * 16].rearrange("p (t e) -> p t e", t=TT)))
                psum_free_tick = nc.vector.engine_nop().then_inc(psum_free[7].sem, 1)
                for t in range(TT):
                    ins = nc.vector.max(top[:, t, :], logit[:, t, 0:E])
                link(ins)
                for t in range(TT):
                    ins = nc.vector.max_index(topi[:, t, :], top[:, t, :], logit[:, t, 0:E])
                link(ins)

                def pick(v, n):
                    return v[:, :, n:n + 1].rearrange("p t o -> p (t o)")
                if layer == 0:
                    link(nc.vector.tensor_copy(rt[:, 4, :], pick(logit, E)))
                nc.vector.tensor_tensor(rt[:, 0, :], pick(top, 1), pick(top, 0), ALU.subtract).then_inc(top_ready, 1)
                nc.vector.tensor_copy(rt[:, 6, :], pick(topi, 0))
                link(nc.vector.tensor_copy(rt[:, 7, :], pick(topi, 1)))
                dve.wait_ge(route_exp, (2, 3)[layer])
                link(nc.vector.tensor_scalar(rt[:, 2, :], rt[:, 1, :], 1.0, None, ALU.add))
                link(nc.vector.reciprocal(rt[:, 2, :], rt[:, 2, :]))
                link(nc.vector.tensor_tensor(rt[:, 3, :], rt[:, 1, :], rt[:, 2, :], ALU.mult))
                ids = iota8[:].unsqueeze(1).to_broadcast([P, TT, E])
                for n in range(2):
                    link(nc.vector.tensor_tensor(oh[:, n], ids, rt[:, 6 + n, :].unsqueeze(2).to_broadcast([P, TT, E]), ALU.is_equal))
                    link(nc.vector.tensor_tensor(oh[:, n], oh[:, n], rt[:, 2 + n, :].unsqueeze(2).to_broadcast([P, TT, E]), ALU.mult))
                link(nc.vector.tensor_tensor(comb[:, :, 0:E], oh[:, 0], oh[:, 1], ALU.add))
                if layer == 0:
                    link(nc.vector.tensor_copy(comb[:, :, E:12], rt[:, 5, :].unsqueeze(2).to_broadcast([P, TT, 4])))
                else:
                    link(nc.vector.memset(comb[:, :, E:12], 1.0))
                    link(nc.vector.scalar_tensor_tensor(out=x[:], in0=bias_d[:].unsqueeze(1).to_broadcast([P, TT, D]), scalar=gate[:, 3:4],
                                                        in1=x[:], op0=ALU.mult, op1=ALU.add))
                link(nc.vector.tensor_scalar(comb[:], comb[:], gate_s[:, 2 + layer:3 + layer], None, ALU.mult))

                pl = plan["ffn", layer]

                def split_low(k, par):
                    dve.wait_ge(w_hi, k + first + 1)
                    if layer:
                        nc.vector.tensor_copy(bias_now[:, par], bias_gu[:, bass.ds(k, 1)].rearrange("p o m n -> p (o m) n"))
                    nc.vector.scalar_tensor_tensor(out=wsp[par][1], in0=wst, scalar=WS, in1=wsp[par][0],
                                                   op0=ALU.mult, op1=ALU.subtract).then_inc(w_split, 1)

                def units(k, par):
                    def unit_low(u):
                        s, (c, m) = u % 2, divmod(u, IH)
                        mn = IT[m][1]
                        dve.wait_ge(h_hi, (k + first) * UNITS + u + 1)
                        nc.vector.tensor_tensor(hT[1][0:mn, m, c * CW:(c + 1) * CW], h32[s][0:mn, :],
                                                hT[0][0:mn, m, c * CW:(c + 1) * CW], ALU.subtract).then_inc(hT_ready, 1)

                    for u in range(UNITS):
                        s, m = u % 2, u % IH
                        mn = IT[m][1]
                        pl.written(dve, f"u{u}", k)
                        dve.wait_ge(sil_ready, (k + first) * UNITS + u + 1)
                        if u >= 2 or not isinstance(k, int) or k > 0:
                            dve.wait_ge(hT_ready, (k + first) * UNITS + u - 1)
                        up = psum[0:mn, 2 * s + 1, 0:CW]
                        if layer:
                            ins = nc.vector.scalar_tensor_tensor(out=h32[s][0:mn, :], in0=up,
                                                                 scalar=bias_now[0:mn, par, m, 1:2],
                                                                 in1=sil[s][0:mn, :], op0=ALU.add, op1=ALU.mult)
                        else:
                            ins = nc.vector.tensor_tensor(h32[s][0:mn, :], up, sil[s][0:mn, :], ALU.mult)
                        ins.then_inc(h_ready, 1)
                        if u:
                            unit_low(u - 1)
                    unit_low(UNITS - 1)

                def combine(k):
                    for t in range(TT):
                        pl.written(dve, f"d{t}", k)
                        nc.vector.scalar_tensor_tensor(out=x[:, t, :], in0=psum[:, 4 + t % 4, :],
                                                       scalar=comb[:, t, bass.ds(k, 1)], in1=x[:, t, :],
                                                       op0=ALU.mult, op1=ALU.add).then_inc(psum_free[4 + t % 4].sem, 1)

                split_low(0, 0)
                units(0, 0)
                split_low(1, 1)
                combine(0)
                with dve.Fori(0, NBLK[layer] // 2 - 1) as j:
                    for par in range(2):
                        k = j * 2 + 1 + par
                        units(k, 1 - par)
                        split_low(k + 1, par)
                        combine(k)
                units(NBLK[layer] - 1, 1)
                combine(NBLK[layer] - 1)
                link(nc.vector.engine_nop())
                end_phase()

            if stop >= 2:
                ffn(0)
            if stop >= 3:
                for n, dst in enumerate((wq, wo)):
                    dve.wait_ge(stage_hi, 9 + n)
                    nc.vector.scalar_tensor_tensor(out=dst[1][:], in0=stage1[n], scalar=WS, in1=dst[0][:],
                                                   op0=ALU.mult, op1=ALU.subtract).then_inc(stage_used, 1)
                dve.wait_ge(stage_hi, 11)
                nc.vector.scalar_tensor_tensor(out=wk[1][:, :, 0:2 * P], in0=stage1[0][:, :, 0:2 * P], scalar=WS, in1=wk[0][:, :, 0:2 * P],
                                               op0=ALU.mult, op1=ALU.subtract).then_inc(stage_used, 1)
                link(nc.vector.tensor_scalar(bias_gu[:, :, :, 1:2], bias_gu[:, :, :, 1:2], WS, None, ALU.mult))
                for v in pr:
                    link(nc.vector.memset(v, 0.0))
                layernorm(2)
                pl = plan["q", 1]
                with dve.Fori(0, NCH) as c:
                    for m in range(KC):
                        pl.written(dve, f"q{m}", c)
                        nc.vector.tensor_scalar(col(q1T, c, CW)[:, m, :], psum[:, m, 0:CW], 1.0 / (WS * HD ** 0.5), None,
                                                ALU.mult).then_inc(psum_free[m].sem, 1)
                link(nc.vector.engine_nop())
                pl = plan["att", 1]
                dve.wait_ge(mask_loaded, 48)

                def context1(b):
                    dve.wait_ge(ctx_hi, b + B + 1)
                    nc.vector.tensor_tensor(ctx_s[1], ctx_f, ctx_s[0], ALU.subtract).then_inc(ctx_split, 1)

                def keys1(b):
                    pl.written(dve, "k", b)
                    for g in range(NG):
                        nc.vector.tensor_scalar(k1[0:HD, g, :], psum[HD * g:HD * (g + 1), 7, 0:SK], 1.0 / WS, None, ALU.mult)
                        nc.vector.tensor_scalar(k1[HD:HD + 1, g, :], row(mask8, b), -1.0, -NEG, ALU.add, ALU.mult)
                        ins = nc.vector.tensor_copy(q1[0:HD].rearrange("p (m j) s -> p m j s", j=4)[:, :, g, :],
                                                    q1T[HD * g:HD * (g + 1), :, bass.ds(b * S, S)])
                    ins.then_inc(psum_free[7].sem, 1)
                    pl.written(dve, "v", b)
                    nc.vector.tensor_scalar(v1[:, 0:2, :], psum[:, 6, 0:2 * P].rearrange("p (t c) -> p t c", t=2), 1.0 / WS, None, ALU.mult)
                    ins = nc.vector.tensor_scalar(v1[0:KT[2][1], 2, :], psum[0:KT[2][1], 6, 2 * P:3 * P], 1.0 / WS, None, ALU.mult)
                    ins.then_inc(psum_free[6].sem, 1)
                    nc.vector.engine_nop().then_inc(kv1_ready, 1)

                def heads(b):
                    def transposed(h):
                        pl.written(dve, f"pT{h}", b)
                        nc.vector.tensor_copy(pT[h % 2], psum[:, 2 + h % 2, 0:3 * S].rearrange("p (t s) -> p t s", t=3)).then_inc(pT_ready, 1)

                    for h in range(NH):
                        pl.written(dve, f"s{h}", b)
                        if h >= 2:
                            dve.wait_ge(exp_done, b * NH + h - 1)
                        nc.vector.reduce_max(nmax[0:S, h % 2:h % 2 + 1], psum[0:S, h % 2, 0:SK], AX_X, negate=True).then_inc(nmax_ready, 1)
                        if h:
                            transposed(h - 1)
                    transposed(NH - 1)

                def quotient1(b):
                    dve.wait_ge(exp_done, b * NH + NH)
                    nc.vector.reciprocal(rden[0:S, :], den[0:S, :]).then_inc(rden_ready, 1)
                    dve.wait_ge(rden_ready, b + B + 1)
                    pl.written(dve, "o", b)
                    nc.vector.tensor_tensor(norm[0][0:S, :].rearrange("p (h c) -> p h c", h=NH), psum[0:S, 4, :].rearrange("p (h c) -> p h c", h=NH),
                                            rden[0:S, :].unsqueeze(2).to_broadcast([S, NH, HD]), ALU.mult).then_inc(psum_free[4].sem, 1)
                    nc.vector.engine_nop().then_inc(norm_ready.sem, 1)

                context1(0)
                keys1(0)
                with dve.Fori(0, B - 1) as b:
                    heads(b)
                    context1(b + 1)
                    quotient1(b)
                    keys1(b + 1)
                    att_columns(1, pl, b)
                heads(B - 1)
                quotient1(B - 1)
                att_columns(1, pl, B - 1)
                project_out(1)
            if stop >= 4:
                ffn(1)

        @block.tensor
        def _(pe):
            def product(dst, stationary, moving, last=None):
                n, total = 0, 3 * KC
                for sh, mh in PASSES:
                    for k in range(KC):
                        ins = nc.tensor.matmul(dst, stationary(sh, k), moving(mh, k), start=n == 0, stop=n == total - 1)
                        n += 1
                if last is not None:
                    ins.then_inc(last, 1)
                return ins

            def transposes(n):
                def tile(t, j, par):
                    pl = plan["ln", n][par]
                    pe.wait_ge(norm_ready.sem, norms["ln", n].at(t))
                    pl.free(pe, "n", j)
                    for k in range(KC):
                        ins = nc.tensor.transpose(psum[:, par, k * P:(k + 1) * P], norm[par][:, k * P:(k + 1) * P], ident[:])
                    ins.then_inc(psum_full[par].sem, 1)
                in_pairs(pe, tile)

            def att_transposes(layer, pl, b):
                pe.wait_ge(norm_ready.sem, norms["att", layer].at(b))
                pl.free(pe, "oT", b)
                for k in range(KC):
                    ins = nc.tensor.transpose(psum[:, pl.bank("oT"), k * S:(k + 1) * S], norm[0][0:S, k * P:(k + 1) * P], ident[0:S, 0:S])
                ins.then_inc(pl.full_sem("oT"), 1)

            def project_out(layer):
                pe.wait_ge(x_ready, layer + 1)

                def tile(t, j, par):
                    pl = plan["out", layer][par]
                    pl.free(pe, "w", j)
                    product(psum[:, par, :], lambda h, k: col(nT[h], t)[:, k, :], lambda h, k: wo[h][:, k, :], psum_full[par].sem)
                in_pairs(pe, tile)

            pe.wait_ge(stage_used, 5)
            transposes(0)
            pe.wait_ge(phase, 2)
            pl = plan["q", 0]
            with pe.Fori(0, NCH) as c:
                for m in range(KC):
                    pl.free(pe, f"q{m}", c)
                    product(psum[:, m, 0:CW], lambda h, k: wq[h][:, k, m * P:(m + 1) * P], lambda h, k: col(nT[h], c, CW)[:, k, :],
                            psum_full[m].sem)
                for p in range(NPAIR):
                    m, half = divmod(p, 2)
                    pl.free(pe, f"f{p}", c)
                    if half == 0:
                        pe.wait_ge(psum_free[m].sem, pl.r[m].before(c + 1))
                    for n, (sh, mh) in enumerate(PASSES):
                        ins = nc.tensor.matmul(psum[:, 4 + p % 4, 0:CW], bd_q[sh][:, half * P:(half + 1) * P], qh[mh][:, m, :],
                                               start=n == 0, stop=n == 2)
                    ins.then_inc(pl.full_sem(f"f{p}"), 1)

            pl = plan["att", 0]

            def keys(b):
                pe.wait_ge(ctx_split, b + 1)
                for m in range(KC):
                    pl.free(pe, f"kT{m}", b)
                    product(psum[:, m % 2, 0:SK], lambda h, k: wk[h][:, k, m * P:(m + 1) * P], lambda h, k: ctx_s[h][:, k, :],
                            psum_full[m % 2].sem)

            def values(b):
                for t, (t0, tn) in enumerate(KT):
                    pl.free(pe, f"v{t}", b)
                    product(psum[0:tn, pl.bank(f"v{t}"), :], lambda h, k: ctx_s[h][:, k, t0:t0 + tn], lambda h, k: wv[h][:, k, :],
                            pl.full_sem(f"v{t}"))

            def features(b):
                pe.wait_ge(psum_free[0].sem, pl.r[0].before(b + 1))
                pe.wait_ge(psum_free[1].sem, pl.r[1].before(b + 1))
                for t, (t0, tn) in enumerate(KT):
                    for half in range(2):
                        pl.free(pe, f"kf{t}{half}", b)
                        for m in (2 * half, 2 * half + 1):
                            for n, (sh, mh) in enumerate(PASSES):
                                ins = nc.tensor.matmul(psum[0:tn, 4 + half, (m % 2) * 256:(m % 2 + 1) * 256], kT[sh][:, m, t0:t0 + tn],
                                                       bd_k[mh], start=n == 0, stop=n == 2)
                        ins.then_inc(psum_full[4 + half].sem, 1)

            def sums(b):
                for bank in (2, 3, 4, 5):
                    pe.wait_ge(psum_free[bank].sem, pl.r[bank].before(b + 1))
                for q in range(2):
                    pl.free(pe, f"kv{q}", b)
                    for p in range(4 * q, 4 * q + 4):
                        for t, (t0, tn) in enumerate(KT):
                            ins = nc.tensor.matmul(psum[:, 6 + q, (p % 4) * 2 * VW:(p % 4 + 1) * 2 * VW], kf[0:tn, t, p * P:(p + 1) * P],
                                                   va[0:tn, t, 2 * p:2 * p + 2, :].rearrange("p h c -> p (h c)"),
                                                   start=t == 0, stop=t == len(KT) - 1)
                    ins.then_inc(psum_full[6 + q].sem, 1)

            def outputs(b):
                pe.wait_ge(kv_ready, b + 1)
                for q in range(2):
                    pl.free(pe, f"o{q}", b)
                    for p in range(4 * q, 4 * q + 4):
                        for n, (sh, mh) in enumerate(PASSES):
                            ins = nc.tensor.matmul(psum[0:S, 6 + q, (p % 4) * 2 * VW:(p % 4 + 1) * 2 * VW], col(qf[sh], b, S)[:, p, :],
                                                   kvb[mh][:, p, :], start=n == 0, stop=n == 2)
                    ins.then_inc(psum_full[6 + q].sem, 1)

            for bank in (4, 5, 6, 7):
                pe.wait_ge(psum_free[bank].sem, plan["q", 0].r[bank].before(NCH))
            pe.wait_ge(q_split, 1)
            keys(0)
            values(0)
            features(0)
            sums(0)
            with pe.Fori(0, B - 1) as b:
                keys(b + 1)
                values(b + 1)
                outputs(b)
                features(b + 1)
                att_transposes(0, pl, b)
                sums(b + 1)
            outputs(B - 1)
            att_transposes(0, pl, B - 1)
            project_out(0)

            def ffn(layer):
                transposes(2 * layer + 1)
                pe.wait_ge(phase, (4, 8)[layer])
                plan["route", layer].free(pe, "l")
                for t in range(TT):
                    for n, (sh, mh) in enumerate(PASSES):
                        for k in range(KC):
                            ins = nc.tensor.matmul(psum[:, 7, t * 16:(t + 1) * 16], nT[sh][:, k, t * P:(t + 1) * P], route_w[layer][mh][:, k, :],
                                                   start=n == 0 and k == 0, stop=n == 2 and k == KC - 1)
                ins.then_inc(psum_full[7].sem, 1)
                pl = plan["ffn", layer]
                first = NBLK[0] * layer

                def blk(k, par):
                    pe.wait_ge(w_split, k + first + 1)
                    for u in range(UNITS):
                        c, m = divmod(u, IH)
                        m0, mn = IT[m]
                        if u >= 2 or not isinstance(k, int) or k > 0:
                            pe.wait_ge(h_ready, (k + first) * UNITS + u - 1)
                        for n, w in enumerate("gu"):
                            product(psum[0:mn, 2 * (u % 2) + n, 0:CW],
                                    lambda h, kc: wsp[par][h][:, n * GN + kc * I + m0:n * GN + kc * I + m0 + mn],
                                    lambda h, kc: nT[h][:, kc, c * CW:(c + 1) * CW], pl.full_sem(f"{w}{u}"))
                    for t in range(TT):
                        c = (t * P + P - 1) // CW
                        pe.wait_ge(hT_ready, (k + first) * UNITS + IH * (c + 1))
                        pl.free(pe, f"d{t}", k)
                        n = 0
                        for sh, mh in PASSES:
                            for m, (m0, mn) in enumerate(IT):
                                ins = nc.tensor.matmul(psum[:, 4 + t % 4, :], hT[sh][0:mn, m, t * P:(t + 1) * P],
                                                       wsp[par][mh][0:mn, 2 * GN + m * D:2 * GN + (m + 1) * D],
                                                       start=n == 0, stop=n == 3 * IH - 1)
                                n += 1
                        ins.then_inc(pl.full_sem(f"d{t}"), 1)

                blk(0, 0)
                with pe.Fori(0, NBLK[layer] // 2 - 1) as j:
                    for par in range(2):
                        blk(j * 2 + 1 + par, (1 + par) % 2)
                blk(NBLK[layer] - 1, 1)

            if stop >= 2:
                ffn(0)
            if stop >= 3:
                pe.wait_ge(stage_used, 8)
                transposes(2)
                pe.wait_ge(phase, 6)
                pl = plan["q", 1]
                with pe.Fori(0, NCH) as c:
                    for m in range(KC):
                        pl.free(pe, f"q{m}", c)
                        product(psum[:, m, 0:CW], lambda h, k: wq[h][:, k, m * P:(m + 1) * P], lambda h, k: col(nT[h], c, CW)[:, k, :],
                                psum_full[m].sem)
                pl = plan["att", 1]

                def keys1(b):
                    pe.wait_ge(ctx_split, b + B + 1)
                    pl.free(pe, "k", b)
                    product(psum[:, 7, 0:SK], lambda h, k: wk[h][:, k, 0:P], lambda h, k: ctx_s[h][:, k, :], psum_full[7].sem)
                    pl.free(pe, "v", b)
                    for t, (t0, tn) in enumerate(KT):
                        product(psum[0:tn, 6, t * P:(t + 1) * P], lambda h, k: ctx_s[h][:, k, t0:t0 + tn], lambda h, k: wk[h][:, k, P:2 * P],
                                psum_full[6].sem if t == 2 else None)

                def heads(b):
                    pe.wait_ge(kv1_ready, b + 1)

                    def scores(h):
                        if h >= 2:
                            pe.wait_ge(exp_done, b * NH + h - 1)
                        nc.tensor.matmul(psum[0:S, h % 2, 0:SK], q1[:, h, :], k1[:, h // 4, :], start=True, stop=True).then_inc(psum_full[h % 2].sem, 1)

                    def turn(h):
                        pe.wait_ge(exp_done, b * NH + h + 1)
                        for t in range(3):
                            ins = nc.tensor.transpose(psum[:, 2 + h % 2, t * S:(t + 1) * S], pr[h % 2][0:S, t * P:(t + 1) * P], ident[0:S, 0:S])
                        ins.then_inc(psum_full[2 + h % 2].sem, 1)

                    def weigh(h):
                        pe.wait_ge(pT_ready, b * NH + h + 1)
                        if h == 0:
                            pl.free(pe, "o", b)
                        for t, (t0, tn) in enumerate(KT):
                            ins = nc.tensor.matmul(psum[0:S, 4, h * HD:(h + 1) * HD], pT[h % 2][0:tn, t, :], v1[0:tn, t, (h // 4) * HD:(h // 4 + 1) * HD],
                                                   start=t == 0, stop=t == 2)
                        if h == NH - 1:
                            ins.then_inc(psum_full[4].sem, 1)

                    scores(0)
                    for h in range(NH):
                        if h + 1 < NH:
                            scores(h + 1)
                        turn(h)
                        if h:
                            weigh(h - 1)
                    weigh(NH - 1)

                keys1(0)
                with pe.Fori(0, B - 1) as b:
                    heads(b)
                    keys1(b + 1)
                    att_transposes(1, pl, b)
                heads(B - 1)
                att_transposes(1, pl, B - 1)
                project_out(1)
            if stop >= 4:
                ffn(1)


STOP = 4


def kernel(**inputs):
    import numpy as np
    import concourse.bacc as bacc
    from concourse.bass_utils import run_bass_kernel_spmd

    v = {k: np.asarray(t) for k, t in inputs.items()}

    def chunks(w):
        return w.reshape(KC, P, -1).transpose(1, 0, 2)

    def per_part(b):
        return b.reshape(KC, P).T

    def block_weights(gate, up, down):
        n = gate.shape[0]
        g, u = (w.reshape(n, KC, P, I).transpose(0, 2, 1, 3).reshape(n, P, KC * I) for w in (gate, up))
        d = np.zeros((n, IH * P, D), np.float32)
        d[:, 0:I] = down
        d = d.reshape(n, IH, P, D).transpose(0, 2, 1, 3).reshape(n, P, IH * D)
        return np.concatenate([g, u, d], axis=2)

    def cut(w, axis):
        n = w.shape[axis] // I
        return w.reshape(n, I, D) if axis == 0 else w.reshape(D, n, I).transpose(1, 0, 2)

    mask_f = np.zeros((P, B, 3), np.float32)
    mask_t = v["mask_BxS2_ff1"].T
    for t, (t0, tn) in enumerate(KT):
        mask_f[0:tn, :, t] = mask_t[t0:t0 + tn]
    bias_gu = np.zeros((P, NBLK[1], IH, 2), np.float32)
    for n, name in enumerate(("L1_ffn_s_gate_b", "L1_ffn_s_up_b")):
        for k in range(NBLK[1] - E):
            for m, (m0, mn) in enumerate(IT):
                bias_gu[0:mn, E + k, m, n] = v[name][k * I + m0:k * I + m0 + mn]
    slopes = (2.0 ** (-8.0 / NH)) ** np.arange(1, NH + 1, dtype=np.float32)
    slopes = slopes.astype(np.float32)
    q_aug = np.stack([np.ones((NH, S), np.float32), np.repeat(slopes[:, None], S, 1),
                      -slopes[:, None] * np.arange(S, dtype=np.float32)[None, :]]).astype(np.float32)
    k_aug = np.stack([np.repeat(np.arange(SK, dtype=np.float32)[None], NG, 0), np.ones((NG, SK), np.float32)])
    arrays = {
        "x": v["x"].reshape(T, D),
        "ctxT": v["ctx_2048"].transpose(0, 2, 1).reshape(B, KC, P, SK).transpose(0, 2, 1, 3),
        "mask_f": mask_f,
        "mask_b": v["mask_BxS2_bf1"].view(np.uint8).reshape(1, B, SK),
        "gates": np.concatenate([v["g_xattn"], v["g_ffn"]])[None].repeat(P, 0),
        "w_attn0": np.stack([chunks(v[f"L0_xattn_{w}"].T) for w in ("Wq", "Wk", "Wv", "Wo")]),
        "w_attn1": np.stack([chunks(v[f"L1_xattn_{w}"]) for w in ("Wq", "Wo")]),
        "w_kv1": chunks(np.concatenate([v["L1_xattn_Wk"], v["L1_xattn_Wv"]], axis=1)),
        "wqf": v["L0_xattn_Wqf"].T, "wkf": v["L0_xattn_Wkf"].T,
        "bq": per_part(v["L0_xattn_bq"]), "bk": per_part(v["L0_xattn_bk"]),
        "bv": v["L0_xattn_bv"], "bo": v["L0_xattn_bo"], "bd": v["L1_ffn_s_down_b"],
        "route0": chunks(np.concatenate([v["L0_ffn_gate_w"].T, v["L0_ffn_shared_gate_w"]], axis=1)),
        "route1": chunks(v["L1_ffn_router_w"].T),
        "w_blk0": block_weights(np.concatenate([v["L0_ffn_w_gate"], cut(v["L0_ffn_sw_gate"], 1)]),
                                np.concatenate([v["L0_ffn_w_up"], cut(v["L0_ffn_sw_up"], 1)]),
                                np.concatenate([v["L0_ffn_w_down"], cut(v["L0_ffn_sw_down"], 0)])),
        "w_blk1": block_weights(np.concatenate([v["L1_ffn_gate_w"], cut(v["L1_ffn_s_gate_w"], 1)]),
                                np.concatenate([v["L1_ffn_up_w"], cut(v["L1_ffn_s_up_w"], 1)]),
                                np.concatenate([v["L1_ffn_down_w"], cut(v["L1_ffn_s_down_w"], 0)])),
        "bias_gu": bias_gu,
        "ident": np.eye(P, dtype=np.float32),
        "iota8": np.arange(E, dtype=np.float32)[None].repeat(P, 0),
        "q_aug": q_aug, "k_aug": k_aug,
    }
    arrays = {f"in_{k}": np.ascontiguousarray(t) for k, t in arrays.items()}
    nc = bacc.Bacc("TRN2", target_bir_lowering=False, num_devices=1)
    aps = {k[3:]: nc.dram_tensor(k, t.shape, mybir.dt.from_np(t.dtype), kind="ExternalInput").ap() for k, t in arrays.items()}
    out = nc.dram_tensor("out", (T, D), F32, kind="ExternalOutput").ap()
    build(nc, aps, out, STOP)
    r = run_bass_kernel_spmd(nc, [arrays], core_ids=[0])
    return r.results[0]["out"].reshape(B, S, D)
```

```python
from contextlib import ExitStack

import concourse.bass as bass
from concourse import mybir

F32 = mybir.dt.float32
F16 = mybir.dt.float16
U8 = mybir.dt.uint8
U32 = mybir.dt.uint32
ALU = mybir.AluOpType
ACT = mybir.ActivationFunctionType
AX_X = mybir.AxisListType.X

P = 128
B, S, D = 16, 100, 512
SK = 361
KC = D // P
T = B * S
TT = (T + P - 1) // P
TP = TT * P
LAST = T - (TT - 1) * P
PAIRS = TT // 2
NCH = 4
CW = TP // NCH
KT = [(0, P), (P, P), (2 * P, SK - 2 * P)]
NH, HD, FD = 16, 32, 64
NG = 4
NPAIR = NH // 2
VW = HD + 1
E = 8
I = 352
IT = [(0, P), (P, P), (2 * P, I - 2 * P)]
IH = len(IT)
UNITS = NCH * IH
NBLK = (12, 10)
WS = 64.0
KVS = 256.0
PASSES = ((0, 0), (0, 1), (1, 0))
EPS_LN = 1e-5
EPS_DEN = 1e-8
ALIBI, MASKED, NMASK, FAR = HD, 64, 32, 60000.0
QS = 1.0 / (WS * HD ** 0.5)
K_AT, V_AT = 4, 11
NS = 3


class Count:

    def __init__(self, sem, first=0):
        self.sem, self.base, self.first, self.per = sem, 0, first, 0
        self.total = 0

    def span(self, times, per=1):
        new = Count(self.sem, self.first)
        new.base, new.per = self.total, per
        self.total += times * per
        return new

    def at(self, n=0, k=0):
        return n * self.per + (self.base + k + 1)

    def before(self, n=0, k=0):
        return n * self.per + (self.base + k + self.first)


class Banks:

    def __init__(self, full, free, uses, times, other=()):
        per = {}
        self.place = {}
        for name, bank in uses:
            self.place[name] = (bank, per.get(bank, 0))
            per[bank] = per.get(bank, 0) + 1
        self.f = {b: full[b].span(times, n) for b, n in per.items()}
        self.r = {b: free[b].span(times, n) for b, n in per.items() if b not in other}

    def bank(self, name):
        return self.place[name][0]

    def written(self, eng, name, n=0):
        b, k = self.place[name]
        eng.wait_ge(self.f[b].sem, self.f[b].at(n, k))

    def free(self, eng, name, n=0):
        b, k = self.place[name]
        eng.wait_ge(self.r[b].sem, self.r[b].before(n, k))

    def full_sem(self, name):
        return self.f[self.place[name][0]].sem

    def free_sem(self, name):
        return self.r[self.place[name][0]].sem


def build(nc, a, out, stop=4):
    with ExitStack() as ctx:
        def sb(name, shape, dt=F32):
            return ctx.enter_context(nc.sbuf_tensor(name, shape, dt))

        x = sb("x", [P, TT, D])
        nT = [sb("nT_hi", [P, KC, TP], F16), sb("nT_lo", [P, KC, TP], F16)]
        big = sb("big", [P, NPAIR * TP])
        work_words = 3 * (2 * KC * I + IH * D)
        work = sb("work", [P, work_words])
        wq, wk, wv, wo = ([sb(f"{w}_{h}", [P, KC, D], F16) for h in ("hi", "lo")] for w in ("wq", "wk", "wv", "wo"))
        norm = [sb(f"norm{i}", [P, D]) for i in range(2)]
        ident = sb("ident", [P, P])
        cols = sb("cols", [P, 80])
        stats = sb("stats", [P, TT, 6])
        mv = sb("mv", [P, TT, 2])
        rstd = sb("rstd", [P, TT])
        mhalf = sb("mhalf", [P, TT])
        mask_c = sb("mask_c", [P, B, 3])
        route_s = [sb(f"route_s{i}", [P, KC, 16]) for i in range(2)]
        route_w = [[sb(f"route_w{i}{h}", [P, KC, 16], F16) for h in range(2)] for i in range(2)]
        logit = sb("logit", [P, TT, 16])
        top = sb("top", [P, TT, 8])
        topi = sb("topi", [P, TT, 8], U32)
        comb = sb("comb", [P, TT, 12])
        iota8 = sb("iota8", [P, E])
        rt = sb("rt", [P, 8, TT])
        oh = sb("oh", [P, 2, TT, E])
        bias_gu = sb("bias_gu", [P, NBLK[1], IH, 2])
        bias_now = sb("bias_now", [P, 2, IH, 2])
        bias_v = sb("bias_v", [P, D])
        bias_o = sb("bias_o", [P, D])
        bias_d = sb("bias_d", [P, D])
        psum = ctx.enter_context(nc.psum_tensor("psum", [P, 8, 512], F32))

        bq, bk = cols[:, 0:4], cols[:, 4:8]
        gate, gate_in = cols[:, 8:12], cols[:, 12:16]
        den, rden = cols[:, 16:32], cols[:, 32:48]
        gate_s = cols[:, 48:52]
        tick = cols[:, 52:53]
        nmax = cols[:, 53:53 + NS]
        den1 = [cols[:, 16:32], cols[:, 56:72]]

        used = [0]

        def carve(n, dt, pattern=None, rows=slice(0, P), **dims):
            v = work[rows, used[0]:used[0] + n]
            used[0] += n
            if dt != F32:
                v = v.bitcast(dt)
            return v.rearrange(pattern, **dims) if pattern else v

        CT = KC * SK
        ctx_f = carve(CT, F32, "p (k s) -> p k s", k=KC)
        ctx_s = [carve(CT // 2, F16, "p (k s) -> p k s", k=KC) for _ in range(2)]
        shared_end = used[0]
        kT = [carve(CT // 2, F16, "p (k s) -> p k s", k=KC) for _ in range(2)]
        kf = carve(3 * NH * FD, F32, "p (t f) -> p t f", t=3)
        va = carve(3 * NH * VW, F32, "p (t h c) -> p t h c", t=3, h=NH)
        kv32 = carve(NH * VW, F32, "p (a c) -> p a c", a=NPAIR)
        kvb = [carve(NH * VW // 2, F16, "p (a c) -> p a c", a=NPAIR) for _ in range(2)]
        bd_k = [carve(128, F16) for _ in range(2)]
        bd_q = [carve(128, F16) for _ in range(2)]
        assert KC * CW <= 3 * NH * FD
        qh = [kf.rearrange("p t f -> p (t f)")[:, h * KC * CW // 2:(h + 1) * KC * CW // 2].bitcast(F16)
              .rearrange("p (m t) -> p m t", m=KC) for h in range(2)]
        qf = [big[:, h * NPAIR * TP // 2:(h + 1) * NPAIR * TP // 2].bitcast(F16)
              .rearrange("p (m t) -> p m t", m=NPAIR) for h in range(2)]
        stage = [big[:, i * KC * D:(i + 1) * KC * D].rearrange("p (k n) -> p k n", k=KC) for i in range(2)]
        bd_f = [big[:, 2 * KC * D + 256 * i:2 * KC * D + 256 * (i + 1)] for i in range(2)]

        used[0] = shared_end
        k1 = [[carve(NG * SK // 2, F16, "p (g s) -> p g s", g=NG) for _ in range(2)] for _ in range(2)]
        q1 = [[carve(NH * S // 2, F16, "p (h s) -> p h s", h=NH) for _ in range(2)] for _ in range(2)]
        v1 = [carve(3 * P, F32, "p (t c) -> p t c", t=3) for _ in range(2)]
        pr = [carve(3 * P, F32) for _ in range(NS)]
        pT = [carve(3 * S, F32, "p (t s) -> p t s", t=3) for _ in range(2)]
        mask8 = carve(B * SK // 4, U8, "p (b s) -> p b s", rows=slice(MASKED, MASKED + NMASK), b=B)
        q1T = [big[:, h * KC * TP // 2:(h + 1) * KC * TP // 2].bitcast(F16).rearrange("p (m t) -> p m t", m=KC) for h in range(2)]
        mask16 = big[MASKED:MASKED + NMASK, KC * TP:KC * TP + B * SK // 2].bitcast(F16).rearrange("p (b s) -> p b s", b=B)
        stage1 = [big[:, KC * TP + i * KC * D:KC * TP + (i + 1) * KC * D].rearrange("p (k n) -> p k n", k=KC)
                  for i in range(2)]

        hT = [big[:, h * IH * TP // 2:(h + 1) * IH * TP // 2].bitcast(F16)
              .rearrange("p (m t) -> p m t", m=IH) for h in range(2)]
        sil = [big[:, IH * TP + i * CW:IH * TP + (i + 1) * CW] for i in range(2)]
        h32 = [big[:, IH * TP + (2 + i) * CW:IH * TP + (3 + i) * CW] for i in range(2)]
        used[0] = 0
        GN = KC * I
        WN = 2 * GN + IH * D
        wst = carve(WN, F32)
        wsp = [[carve(WN // 2, F16) for h in range(2)] for s in range(2)]

        sems = {}

        def sem(name):
            sems[name] = ctx.enter_context(nc.semaphore(name))
            return sems[name]

        psum_full = [Count(sem(f"psum_full{b}")) for b in range(8)]
        psum_free = [Count(sem(f"psum_free{b}"), 1) for b in range(8)]
        hi_done = Count(sem("hi_done"))
        att_hi = Count(sem("att_hi"))
        x_loaded, const_loaded = sem("x_loaded"), sem("const_loaded")
        stage_full = [sem(f"stage_full{i}") for i in range(2)]
        stage_hi, stage_used = sem("stage_hi"), sem("stage_used")
        dve_chain = Count(sem("dve_chain"))
        gates_ready = sem("gates_ready")
        phase = sem("phase")
        stats_ready, rstd_ready = sem("stats_ready"), sem("rstd_ready")
        norm_ready = Count(sem("norm_ready"))
        q_split = sem("q_split")
        ctx_loaded, ctx_hi = sem("ctx_loaded"), sem("ctx_hi")
        ctx_split = sem("ctx_split")
        kT_ready, va_ready, kf_ready = sem("kT_ready"), sem("va_ready"), sem("kf_ready")
        kv32_ready, kv_hi, kv_ready = sem("kv32_ready"), sem("kv_hi"), sem("kv_ready")
        den_ready, rden_ready = sem("den_ready"), sem("rden_ready")
        w_loaded, w_hi, w_split = sem("w_loaded"), sem("w_hi"), sem("w_split")
        sil_ready, h_ready, h_hi, hT_ready = sem("sil_ready"), sem("h_ready"), sem("h_hi"), sem("hT_ready")
        logits_ready, top_ready, route_exp = sem("logits_ready"), sem("top_ready"), sem("route_exp")
        mask_loaded, aug_zero, nmax_ready = sem("mask_loaded"), sem("aug_zero"), sem("nmax_ready")
        kv1_ready, v1_ready = sem("kv1_ready"), sem("v1_ready")
        q1_ready = sem("q1_ready")
        copied = sem("copied")
        q1T_ready, mask_ready = sem("q1T_ready"), sem("mask_ready")
        exp_done, pT_ready = sem("exp_done"), sem("pT_ready")
        x_ready = sem("x_ready")
        stored = sem("stored")

        def banks(uses, times, other=()):
            return Banks(psum_full, psum_free, uses, times, other)

        def pair_banks(name):
            return [banks([(name, par)], PAIRS + 1 - par) for par in range(2)]

        plan = {}
        LINEAR = ([(f"kT{m}", m % 2) for m in range(KC)] + [("v0", 2), ("v1", 3), ("v2", 2)]
                  + [(f"kf{t}{h}", 4 + h) for t in range(3) for h in range(2)]
                  + [("kv0", 6), ("kv1", 7), ("o0", 6), ("o1", 7), ("oT", 6)])
        SOFTMAX = ([(f"s{h}", h % NS) for h in range(NH)] + [(f"pT{h}", (3, 6)[h % 2]) for h in range(NH)]
                   + [("k", 7), ("v", 7), ("o", 4), ("oT", 5)])
        BLOCK = ([(f"{w}{u}", 2 * (u % 2) + n) for u in range(UNITS) for n, w in enumerate("gu")]
                 + [(f"d{t}", 4 + t % 4) for t in range(TT)])
        for layer in range(2):
            plan["ln", 2 * layer] = pair_banks("n")
            plan["q", layer] = banks([(f"q{m}", m) for m in range(KC)]
                                     + [(f"f{p}", 4 + p % 4) for p in range(NPAIR)] * (layer == 0), NCH)
            plan["att", layer] = banks((LINEAR, SOFTMAX)[layer], B, other=((), (0, 1, 2, 3, 4, 6))[layer])
            plan["out", layer] = pair_banks("w")
            plan["ln", 2 * layer + 1] = pair_banks("n")
            plan["route", layer] = banks([("l", 7)], 1)
            plan["ffn", layer] = banks(BLOCK, NBLK[layer], other=range(4))
        hi = {}
        for layer in range(2):
            hi["ln", 2 * layer] = hi_done.span(TT)
            hi["q", layer] = hi_done.span(NCH, KC + NPAIR * (layer == 0))
            hi["kT", layer] = hi_done.span(B, (KC, NG)[layer])
            hi["oT", layer] = att_hi.span(B)
            hi["ln", 2 * layer + 1] = hi_done.span(TT)
        norms = {}
        for layer in range(2):
            norms["ln", 2 * layer] = norm_ready.span(TT)
            norms["att", layer] = norm_ready.span(B)
            norms["ln", 2 * layer + 1] = norm_ready.span(TT)

        def col(v, t, n=P):
            return v[:, :, bass.ds(t * n, n)]

        def row(v, t):
            return v[:, bass.ds(t, 1), :].rearrange("p o d -> p (o d)")

        def at1(v, t):
            return v[:, bass.ds(t, 1)]

        def in_pairs(eng, body):
            with eng.Fori(0, PAIRS) as j:
                body(j * 2, j, 0)
                body(j * 2 + 1, j, 1)
            body(TT - 1, PAIRS, 0)

        block = ctx.enter_context(nc.Block())
        CONSTS = [(ident[:], a["ident"]), (bq, a["bq"]), (bk, a["bk"]), (gate_in, a["gates"]),
                  (mask_c[:], a["mask_f"]), (iota8[:], a["iota8"]), (bias_gu[:], a["bias_gu"]),
                  (bias_v[:], a["bv"].partition_broadcast(P)), (bias_o[:], a["bo"].partition_broadcast(P)),
                  (bias_d[:], a["bd"].partition_broadcast(P)),
                  (route_s[0][:, :, 0:E + 1], a["route0"]), (route_s[1][:, :, 0:E], a["route1"])]
        N_CONST = len(CONSTS) + 2 * 4

        @block.sync
        def _(sp):
            for n in range(4):
                if n >= 2:
                    sp.wait_ge(stage_used, n - 1)
                sp.dma_start(stage[n % 2], a["w_attn0"][n]).then_inc(stage_full[n % 2], 16)
                if n == 1:
                    sp.dma_start(x[:, 0:TT - 1, :], a["x"][0:(TT - 1) * P, :].rearrange("(t p) d -> p t d", p=P)).then_inc(x_loaded, 16)
                    sp.wait_ge(phase, 1)
                    sp.dma_start(x[0:LAST, TT - 1, :], a["x"][(TT - 1) * P:T, :]).then_inc(x_loaded, 16)
            sp.dma_start(ctx_f, a["ctxT"][0]).then_inc(ctx_loaded, 16)
            with sp.Fori(1, B) as b:
                sp.wait_ge(ctx_split, b)
                sp.dma_start(ctx_f, a["ctxT"][b]).then_inc(ctx_loaded, 16)

            def ffn_loads(layer):
                sp.wait_ge(phase, (3, 7)[layer])
                first = NBLK[0] * layer
                sp.dma_start(wst, a[f"w_blk{layer}"][0]).then_inc(w_loaded, 16)
                with sp.Fori(1, NBLK[layer]) as k:
                    sp.wait_ge(w_split, k + first)
                    sp.dma_start(wst, a[f"w_blk{layer}"][k]).then_inc(w_loaded, 16)

            if stop >= 2:
                ffn_loads(0)
            if stop >= 3:
                sp.wait_ge(phase, 5)
                sp.dma_start(stage1[0], a["w_attn1"][0]).then_inc(stage_full[0], 16)
                sp.dma_start(stage1[1], a["w_attn1"][1]).then_inc(stage_full[1], 16)
                sp.dma_start(mask8, a["mask_b"]).then_inc(mask_loaded, 16)
                sp.wait_ge(stage_used, 6)
                sp.dma_start(stage1[0][:, :, 0:2 * P], a["w_kv1"]).then_inc(stage_full[0], 16)
                sp.dma_start(ctx_f, a["ctxT"][0]).then_inc(ctx_loaded, 16)
                sp.wait_ge(aug_zero, 1)
                for par in range(2):
                    for h in range(2):
                        sp.dma_start(q1[par][h][ALIBI:ALIBI + 2], a["q_aug"][h]).then_inc(mask_loaded, 16)
                    sp.dma_start(k1[par][0][ALIBI:ALIBI + 2], a["k_aug"]).then_inc(mask_loaded, 16)
                with sp.Fori(1, B) as b:
                    sp.wait_ge(ctx_split, b + B)
                    sp.dma_start(ctx_f, a["ctxT"][b]).then_inc(ctx_loaded, 16)
            if stop >= 4:
                ffn_loads(1)
            sp.wait_ge(phase, {1: 3, 2: 5, 3: 7, 4: 9}[stop])
            sp.dma_start(out[0:(TT - 1) * P, :].rearrange("(t p) d -> p t d", p=P), x[:, 0:TT - 1, :]).then_inc(stored, 16)
            sp.dma_start(out[(TT - 1) * P:T, :], x[0:LAST, TT - 1, :]).then_inc(stored, 16)
            sp.wait_ge(stored, 32)

        @block.gpsimd
        def _(pool):
            pool.wait_ge(phase, 1)
            for dst, src in CONSTS:
                pool.dma_start(dst, src).then_inc(const_loaded, 16)
            for n, w in enumerate(("wkf", "wqf")):
                for j in range(4):
                    pool.dma_start(bd_f[n][HD * j:HD * (j + 1), FD * j:FD * (j + 1)], a[w]).then_inc(const_loaded, 16)

            def power(n):
                pool.wait_ge(stats_ready, n + 1)
                nc.gpsimd.tensor_tensor(rstd[:], rstd[:], mhalf[:], ALU.pow).then_inc(rstd_ready, 1)

            power(0)
            with pool.Fori(0, B) as b:
                pool.wait_ge(ctx_hi, b + 1)
                nc.gpsimd.tensor_tensor(ctx_s[1], ctx_f, ctx_s[0], ALU.subtract).then_inc(ctx_split, 1)
            for n in range(1, min(stop, 3)):
                power(n)
            if stop >= 3:
                pool.wait_ge(mask_loaded, 16 * 7)
                pool.wait_ge(rstd_ready, 3)
                pool.wait_ge(stage_used, 8)
                nc.gpsimd.tensor_scalar(mask16, mask8, -1.0, FAR, ALU.add, ALU.mult).then_inc(mask_ready, 1)
                pool.wait_ge(mask_ready, 1)
                pool.wait_ge(q1T_ready, 1)

                def context1(b):
                    if not isinstance(b, int) or b:
                        pool.wait_ge(q1_ready, b)
                    pool.wait_ge(ctx_hi, b + B + 1)
                    nc.gpsimd.tensor_tensor(ctx_s[1], ctx_f, ctx_s[0], ALU.subtract).then_inc(ctx_split, 1)

                def queries(b, par):
                    pool.wait_ge(ctx_split, b + B + 1)
                    for h in range(2):
                        for g in range(NG):
                            nc.gpsimd.tensor_copy(q1[par][h][0:HD].rearrange("p (m j) s -> p m j s", j=4)[:, :, g, :],
                                                  col(q1T[h], b, S)[HD * g:HD * (g + 1)]).then_inc(copied, 1)
                            pool.wait_ge(copied, b * (2 * NG) + (h * NG + g + 1))
                    nc.gpsimd.tensor_copy(k1[par][0][MASKED:MASKED + NMASK],
                                          row(mask16, b).unsqueeze(1).to_broadcast([NMASK, NG, SK])).then_inc(q1_ready, 1)

                context1(0)
                queries(0, 0)
                context1(1)
                queries(1, 1)
                with pool.Fori(0, B // 2 - 1) as j:
                    for par in range(2):
                        context1(j * 2 + (2 + par))
                        pool.wait_ge(exp_done, j * (2 * NH) + (par + 1) * NH)
                        queries(j * 2 + (2 + par), par)
            if stop >= 4:
                power(3)

        @block.scalar
        def _(act):
            def layernorm_hi(n):
                def tile(t, j, par):
                    pl = plan["ln", n][par]
                    pl.written(act, "n", j)
                    nc.scalar.activation(col(nT[0], t), psum[:, par, :].rearrange("p (k t) -> p k t", k=KC),
                                         ACT.Copy).then_inc(hi_done.sem, 1)
                in_pairs(act, tile)

            def stage_split_hi(n, dst):
                act.wait_ge(stage_full[n % 2], 16 * (n // 2 + 1))
                nc.scalar.activation(dst[0][:], stage[n % 2], ACT.Copy, scale=WS).then_inc(stage_hi, 1)

            stage_split_hi(0, wq)
            stage_split_hi(1, wk)
            act.wait_ge(const_loaded, 16 * N_CONST)
            nc.scalar.activation(gate, gate_in, ACT.Tanh).then_inc(gates_ready, 1)
            stage_split_hi(2, wv)
            stage_split_hi(3, wo)
            for n, dst in enumerate((bd_k, bd_q)):
                nc.scalar.activation(dst[0], bd_f[n], ACT.Copy).then_inc(stage_hi, 1)
            for n in range(2):
                nc.scalar.activation(route_w[n][0][:], route_s[n][:], ACT.Copy, scale=WS).then_inc(stage_hi, 1)

            layernorm_hi(0)

            pl = plan["q", 0]
            with act.Fori(0, NCH) as c:
                act.wait_ge(phase, 2)
                for m in range(KC):
                    pl.written(act, f"q{m}", c)
                    nc.scalar.activation(qh[0][:, m, :], psum[:, m, 0:CW], ACT.Identity, bias=bq[:, m:m + 1]).then_inc(hi_done.sem, 1)
                for p in range(NPAIR):
                    pl.written(act, f"f{p}", c)
                    nc.scalar.activation(col(qf[0], c, CW)[:, p, :], psum[:, pl.bank(f"f{p}"), 0:CW], ACT.Relu).then_inc(hi_done.sem, 1)

            pl = plan["att", 0]

            def context(b):
                act.wait_ge(ctx_loaded, b * 16 + 16)
                nc.scalar.activation(ctx_s[0], ctx_f, ACT.Copy).then_inc(ctx_hi, 1)

            def keys(b):
                for m in range(KC):
                    pl.written(act, f"kT{m}", b)
                    nc.scalar.activation(kT[0][:, m, :], psum[:, m % 2, 0:SK], ACT.Identity, bias=bk[:, m:m + 1]).then_inc(hi_done.sem, 1)

            def split_kv(b):
                act.wait_ge(kv32_ready, b + 1)
                nc.scalar.activation(kvb[0], kv32, ACT.Copy).then_inc(kv_hi, 1)

            def att_columns(pl, b):
                pl.written(act, "oT", b)
                nc.scalar.activation(col(nT[0], b, S), psum[:, pl.bank("oT"), 0:KC * S].rearrange("p (k t) -> p k t", k=KC),
                                     ACT.Copy).then_inc(att_hi.sem, 1)

            act.wait_ge(phase, 3 - 1)
            context(0)
            keys(0)
            pl.written(act, "v2", 0)
            context(1)
            split_kv(0)
            with act.Fori(0, B - 2) as b:
                keys(b + 1)
                pl.written(act, "v2", b + 1)
                context(b + 2)
                att_columns(pl, b)
                split_kv(b + 1)
            keys(B - 1)
            att_columns(pl, B - 2)
            split_kv(B - 1)
            att_columns(pl, B - 1)

            def ffn(layer):
                layernorm_hi(2 * layer + 1)
                pl = plan["ffn", layer]
                first = NBLK[0] * layer
                act.wait_ge(top_ready, layer + 1)
                nc.scalar.activation(rt[:, 1, :], rt[:, 0, :], ACT.Exp, scale=1.0 / WS).then_inc(route_exp, 1)
                if layer == 0:
                    nc.scalar.activation(rt[:, 5, :], rt[:, 4, :], ACT.Sigmoid, scale=1.0 / WS).then_inc(route_exp, 1)

                def split_hi(k, par, reuse=None):
                    act.wait_ge(w_loaded, (k + first) * 16 + 16)
                    if reuse is not None:
                        pl.written(act, f"d{TT - 1}", reuse)
                    nc.scalar.activation(wsp[par][0], wst, ACT.Copy, scale=WS).then_inc(w_hi, 1)

                def units(k, par):
                    def unit_hi(u):
                        s, (c, m) = u % 2, divmod(u, IH)
                        mn = IT[m][1]
                        act.wait_ge(h_ready, (k + first) * UNITS + u + 1)
                        nc.scalar.activation(hT[0][0:mn, m, c * CW:(c + 1) * CW], h32[s][0:mn, :], ACT.Copy).then_inc(h_hi, 1)

                    for u in range(UNITS):
                        s, m = u % 2, u % IH
                        mn = IT[m][1]
                        pl.written(act, f"g{u}", k)
                        bias = bias_now[0:mn, par, m, 0:1] if layer else 0.0
                        nc.scalar.activation(sil[s][0:mn, :], psum[0:mn, 2 * s, 0:CW], ACT.Silu, bias=bias,
                                             scale=1.0 / WS).then_inc(sil_ready, 1)
                        if u:
                            unit_hi(u - 1)
                    unit_hi(UNITS - 1)

                split_hi(0, 0)
                units(0, 0)
                split_hi(1, 1)
                with act.Fori(0, NBLK[layer] // 2 - 1) as j:
                    for par in range(2):
                        k = j * 2 + 1 + par
                        units(k, 1 - par)
                        split_hi(k + 1, par, k - 1)
                units(NBLK[layer] - 1, 1)

            if stop >= 2:
                ffn(0)
            if stop >= 3:
                for n, dst in enumerate((wq, wo)):
                    act.wait_ge(stage_full[n], 16 * 3)
                    nc.scalar.activation(dst[0][:], stage1[n], ACT.Copy, scale=WS).then_inc(stage_hi, 1)
                act.wait_ge(stage_full[0], 16 * 4)
                nc.scalar.activation(wk[0][:, :, 0:2 * P], stage1[0][:, :, 0:2 * P], ACT.Copy, scale=WS).then_inc(stage_hi, 1)
                layernorm_hi(2)
                pl = plan["q", 1]
                with act.Fori(0, NCH) as c:
                    for m in range(KC):
                        pl.written(act, f"q{m}", c)
                        nc.scalar.activation(col(q1T[0], c, CW)[:, m, :], psum[:, m, 0:CW], ACT.Copy, scale=QS).then_inc(hi_done.sem, 1)
                pl = plan["att", 1]

                def context1(b):
                    act.wait_ge(ctx_loaded, b * 16 + (16 + 16 * B))
                    nc.scalar.activation(ctx_s[0], ctx_f, ACT.Copy).then_inc(ctx_hi, 1)

                def keys1(b, par, g):
                    if g == 0:
                        pl.written(act, "k", b)
                    nc.scalar.activation(k1[par][0][0:HD, g, :], psum[HD * g:HD * (g + 1), 7, 0:SK], ACT.Copy, scale=1.0 / WS).then_inc(hi_done.sem, 1)

                def values1(b, par):
                    pl.written(act, "v", b)
                    nc.scalar.activation(v1[par][:, 0:2, :], psum[:, 7, 0:2 * P].rearrange("p (t c) -> p t c", t=2), ACT.Copy, scale=1.0 / WS)
                    nc.scalar.activation(v1[par][0:KT[2][1], 2, :], psum[0:KT[2][1], 7, 2 * P:3 * P], ACT.Copy,
                                         scale=1.0 / WS).then_inc(psum_free[7].sem, 1)

                def heads(b, par, before, after):
                    for h in range(NH):
                        act.wait_ge(nmax_ready, b * NH + h + 1)
                        if h >= NS:
                            pl.written(act, f"pT{h - NS}", b)
                        nc.scalar.activation(pr[h % NS][0:S, 0:SK], psum[0:S, pl.bank(f"s{h}"), 0:SK], ACT.Exp,
                                             bias=nmax[0:S, h % NS:h % NS + 1], accum_out=den1[par][0:S, h:h + 1]).then_inc(exp_done, 1)
                        if before and h == 4:
                            att_columns(pl, b - 1)
                        if after and K_AT < h <= K_AT + NG:
                            keys1(b + 1, 1 - par, h - K_AT - 1)
                        if after and h == V_AT + 1:
                            values1(b + 1, 1 - par)
                        if after == 2 and h == V_AT + 2:
                            context1(b + 2)

                context1(0)
                for g in range(NG):
                    keys1(0, 0, g)
                values1(0, 0)
                context1(1)
                heads(0, 0, False, 2)
                with act.Fori(0, B // 2 - 2) as j:
                    heads(j * 2 + 1, 1, True, 2)
                    heads(j * 2 + 2, 0, True, 2)
                heads(B - 3, 1, True, 2)
                heads(B - 2, 0, True, 1)
                heads(B - 1, 1, True, 0)
                att_columns(pl, B - 1)
            if stop >= 4:
                ffn(1)

        @block.vector
        def _(dve):
            chained = [0]

            def link(ins):
                chained[0] += 1
                ins.then_inc(dve_chain.sem, 1)
                dve.wait_ge(dve_chain.sem, chained[0])

            def end_phase():
                nc.vector.engine_nop().then_inc(phase, 1)

            for v in (x[:, TT - 1, :], bd_f[0], bd_f[1], route_s[0][:], route_s[1][:]):
                nc.vector.memset(v, 0.0)
            nc.vector.memset(mhalf[:], -0.5)
            for c in psum_free:
                nc.vector.engine_nop().then_inc(c.sem, 1)
            link(nc.vector.memset(comb[:], 1.0))
            end_phase()
            def layernorm(n):
                for t in range(TT):
                    ins = nc.vector.bn_stats(stats[:, t, :], x[:, t, :])
                link(ins)
                for t in range(TT):
                    ins = nc.vector.bn_aggr(mv[:, t, :], stats[:, t, :])
                link(ins)
                nc.vector.tensor_scalar(rstd[:], mv[:, :, 1:2].rearrange("p t o -> p (t o)"), EPS_LN, None, ALU.add).then_inc(stats_ready, 1)
                dve.wait_ge(rstd_ready, n + 1)

                def normalise(t, j, par, reuse=True):
                    if reuse:
                        plan["ln", n][par].written(dve, "n", j - 1)
                    nc.vector.tensor_scalar(norm[par][:], row(x, t), mv[:, bass.ds(t, 1), 0:1].rearrange("p o s -> p (o s)"),
                                            at1(rstd, t), ALU.subtract, ALU.mult).then_inc(norm_ready.sem, 1)

                def low(t, j, par):
                    dve.wait_ge(hi_done.sem, hi["ln", n].at(t))
                    nc.vector.tensor_tensor(col(nT[1], t), psum[:, par, :].rearrange("p (k t) -> p k t", k=KC),
                                            col(nT[0], t), ALU.subtract).then_inc(psum_free[par].sem, 1)

                normalise(0, 0, 0, False)
                normalise(1, 0, 1, False)
                with dve.Fori(0, PAIRS - 1) as j:
                    normalise(j * 2 + 2, j + 1, 0)
                    low(j * 2, j, 0)
                    normalise(j * 2 + 3, j + 1, 1)
                    low(j * 2 + 1, j, 1)
                normalise(TT - 1, PAIRS, 0)
                for t in range(TT - 3, TT):
                    low(t, t // 2, t % 2)
                end_phase()

            def stage_split_low(n, dst):
                dve.wait_ge(stage_hi, n + 1)
                nc.vector.scalar_tensor_tensor(out=dst[1][:], in0=stage[n % 2], scalar=WS, in1=dst[0][:],
                                               op0=ALU.mult, op1=ALU.subtract).then_inc(stage_used, 1)

            stage_split_low(0, wq)
            stage_split_low(1, wk)
            dve.wait_ge(const_loaded, 16 * N_CONST)
            for v in (bq, bk, bias_v[:]):
                link(nc.vector.tensor_scalar(v, v, WS, None, ALU.mult))
            link(nc.vector.tensor_scalar(mask_c[:], mask_c[:], 1.0 / WS, None, ALU.mult))
            dve.wait_ge(gates_ready, 1)
            link(nc.vector.tensor_scalar(gate_s[:, 0:2], gate[:, 0:2], 1.0 / WS, None, ALU.mult))
            link(nc.vector.tensor_scalar(gate_s[:, 2:4], gate[:, 2:4], 1.0 / (WS * WS), None, ALU.mult))
            dve.wait_ge(x_loaded, 32)
            layernorm(0)
            stage_split_low(2, wv)
            stage_split_low(3, wo)
            dve.wait_ge(stage_hi, 8)
            for n, dst in enumerate((bd_k, bd_q)):
                nc.vector.tensor_tensor(dst[1], bd_f[n], dst[0], ALU.subtract)
            for n in range(2):
                ins = nc.vector.scalar_tensor_tensor(out=route_w[n][1][:], in0=route_s[n][:], scalar=WS, in1=route_w[n][0][:],
                                                     op0=ALU.mult, op1=ALU.subtract)
            ins.then_inc(stage_used, 1)
            nc.vector.memset(kv32, 0.0)

            pl = plan["q", 0]
            with dve.Fori(0, NCH) as c:
                for m in range(KC):
                    dve.wait_ge(hi_done.sem, hi["q", 0].at(c, m))
                    nc.vector.scalar_tensor_tensor(out=qh[1][:, m, :], in0=psum[:, m, 0:CW], scalar=bq[:, m:m + 1],
                                                   in1=qh[0][:, m, :], op0=ALU.add, op1=ALU.subtract).then_inc(psum_free[m].sem, 1)
                for p in range(NPAIR):
                    dve.wait_ge(hi_done.sem, hi["q", 0].at(c, KC + p))
                    nc.vector.scalar_tensor_tensor(out=col(qf[1], c, CW)[:, p, :], in0=psum[:, pl.bank(f"f{p}"), 0:CW], scalar=0.0,
                                                   in1=col(qf[0], c, CW)[:, p, :], op0=ALU.max, op1=ALU.subtract).then_inc(pl.free_sem(f"f{p}"), 1)
            nc.vector.memset(va, WS).then_inc(q_split, 1)
            dve.wait_ge(q_split, 1)

            pl = plan["att", 0]

            def keys(b):
                for m in range(KC):
                    dve.wait_ge(hi_done.sem, hi["kT", 0].at(b, m))
                    nc.vector.scalar_tensor_tensor(out=kT[1][:, m, :], in0=psum[:, m % 2, 0:SK], scalar=bk[:, m:m + 1],
                                                   in1=kT[0][:, m, :], op0=ALU.add, op1=ALU.subtract).then_inc(psum_free[m % 2].sem, 1)

            def values(b):
                for t, (t0, tn) in enumerate(KT):
                    pl.written(dve, f"v{t}", b)
                    nc.vector.tensor_tensor(va[0:tn, t, :, 0:HD], psum[0:tn, pl.bank(f"v{t}"), :].rearrange("p (h c) -> p h c", h=NH),
                                            bias_v[0:tn, :].rearrange("p (h c) -> p h c", h=NH), ALU.add).then_inc(pl.free_sem(f"v{t}"), 1)

            def features(b):
                for t, (t0, tn) in enumerate(KT):
                    for half in range(2):
                        pl.written(dve, f"kf{t}{half}", b)
                        nc.vector.tensor_scalar(kf[0:tn, t, half * 512:(half + 1) * 512], psum[0:tn, 4 + half, :], 0.0,
                                                mask_c[0:tn, bass.ds(b, 1), t:t + 1].rearrange("p a c -> p (a c)"),
                                                ALU.max, ALU.mult).then_inc(psum_free[4 + half].sem, 1)

            def diagonal(b):
                for q in range(2):
                    pl.written(dve, f"kv{q}", b)
                    src = psum[:, 6 + q, 0:4 * 2 * VW].rearrange("p (a c) -> p a c", a=4)
                    nc.vector.tensor_scalar(kv32[0:64, 4 * q:4 * q + 4, 0:VW], src[0:64, :, 0:VW], 1.0 / KVS, None, ALU.mult)
                    nc.vector.tensor_scalar(kv32[64:128, 4 * q:4 * q + 4, VW:2 * VW], src[64:128, :, VW:2 * VW],
                                            1.0 / KVS, None, ALU.mult).then_inc(psum_free[6 + q].sem, 1)
                nc.vector.engine_nop().then_inc(kv32_ready, 1)
                dve.wait_ge(kv_hi, b + 1)
                nc.vector.tensor_tensor(kvb[1], kv32, kvb[0], ALU.subtract).then_inc(kv_ready, 1)

            def quotient(b, reuse=None):
                for q in range(2):
                    pl.written(dve, f"o{q}", b)
                    src = psum[0:S, 6 + q, 0:8 * VW].rearrange("p (h c) -> p h c", h=8)
                    ins = nc.vector.tensor_scalar(den[0:S, 8 * q:8 * q + 8], src[:, :, HD:VW].rearrange("p h c -> p (h c)"),
                                                  EPS_DEN * WS * WS * WS / (KVS * WS), None, ALU.add)
                ins.then_inc(den_ready, 1)
                dve.wait_ge(den_ready, b + 1)
                nc.vector.reciprocal(rden[0:S, :], den[0:S, :]).then_inc(rden_ready, 1)
                dve.wait_ge(rden_ready, b + 1)
                for q in range(2):
                    src = psum[0:S, 6 + q, 0:8 * VW].rearrange("p (h c) -> p h c", h=8)
                    ins = nc.vector.tensor_tensor(norm[0][0:S, 256 * q:256 * (q + 1)].rearrange("p (h c) -> p h c", h=8), src[:, :, 0:HD],
                                                  rden[0:S, 8 * q:8 * q + 8].unsqueeze(2).to_broadcast([S, 8, HD]), ALU.mult)
                    ins.then_inc(psum_free[6 + q].sem, 1)
                nc.vector.engine_nop().then_inc(norm_ready.sem, 1)

            def att_columns(layer, pl, b):
                dve.wait_ge(att_hi.sem, hi["oT", layer].at(b))
                nc.vector.tensor_tensor(col(nT[1], b, S), psum[:, pl.bank("oT"), 0:KC * S].rearrange("p (k t) -> p k t", k=KC),
                                        col(nT[0], b, S), ALU.subtract).then_inc(pl.free_sem("oT"), 1)

            keys(0)
            values(0)
            features(0)
            diagonal(0)
            with dve.Fori(0, B - 1) as b:
                keys(b + 1)
                values(b + 1)
                quotient(b)
                features(b + 1)
                att_columns(0, pl, b)
                diagonal(b + 1)
            quotient(B - 1)
            att_columns(0, pl, B - 1)

            def project_out(layer):
                if layer == 0:
                    link(nc.vector.scalar_tensor_tensor(out=x[:], in0=bias_o[:].unsqueeze(1).to_broadcast([P, TT, D]), scalar=gate[:, 0:1],
                                                        in1=x[:], op0=ALU.mult, op1=ALU.add))
                nc.vector.engine_nop().then_inc(x_ready, 1)

                def tile(t, j, par):
                    pl = plan["out", layer][par]
                    pl.written(dve, "w", j)
                    nc.vector.scalar_tensor_tensor(out=row(x, t), in0=psum[:, par, :], scalar=gate_s[:, layer:layer + 1], in1=row(x, t),
                                                   op0=ALU.mult, op1=ALU.add).then_inc(psum_free[par].sem, 1)
                in_pairs(dve, tile)
                link(nc.vector.engine_nop())
                end_phase()

            project_out(0)

            def ffn(layer):
                layernorm(2 * layer + 1)
                first = NBLK[0] * layer
                plan["route", layer].written(dve, "l")
                link(nc.vector.tensor_copy(logit[:], psum[:, 7, 0:TT * 16].rearrange("p (t e) -> p t e", t=TT)))
                psum_free_tick = nc.vector.engine_nop().then_inc(psum_free[7].sem, 1)
                for t in range(TT):
                    ins = nc.vector.max(top[:, t, :], logit[:, t, 0:E])
                link(ins)
                for t in range(TT):
                    ins = nc.vector.max_index(topi[:, t, :], top[:, t, :], logit[:, t, 0:E])
                link(ins)

                def pick(v, n):
                    return v[:, :, n:n + 1].rearrange("p t o -> p (t o)")
                if layer == 0:
                    link(nc.vector.tensor_copy(rt[:, 4, :], pick(logit, E)))
                nc.vector.tensor_tensor(rt[:, 0, :], pick(top, 1), pick(top, 0), ALU.subtract).then_inc(top_ready, 1)
                nc.vector.tensor_copy(rt[:, 6, :], pick(topi, 0))
                link(nc.vector.tensor_copy(rt[:, 7, :], pick(topi, 1)))
                dve.wait_ge(route_exp, (2, 3)[layer])
                link(nc.vector.tensor_scalar(rt[:, 2, :], rt[:, 1, :], 1.0, None, ALU.add))
                link(nc.vector.reciprocal(rt[:, 2, :], rt[:, 2, :]))
                link(nc.vector.tensor_tensor(rt[:, 3, :], rt[:, 1, :], rt[:, 2, :], ALU.mult))
                ids = iota8[:].unsqueeze(1).to_broadcast([P, TT, E])
                for n in range(2):
                    link(nc.vector.tensor_tensor(oh[:, n], ids, rt[:, 6 + n, :].unsqueeze(2).to_broadcast([P, TT, E]), ALU.is_equal))
                    link(nc.vector.tensor_tensor(oh[:, n], oh[:, n], rt[:, 2 + n, :].unsqueeze(2).to_broadcast([P, TT, E]), ALU.mult))
                link(nc.vector.tensor_tensor(comb[:, :, 0:E], oh[:, 0], oh[:, 1], ALU.add))
                if layer == 0:
                    link(nc.vector.tensor_copy(comb[:, :, E:12], rt[:, 5, :].unsqueeze(2).to_broadcast([P, TT, 4])))
                else:
                    link(nc.vector.memset(comb[:, :, E:12], 1.0))
                    link(nc.vector.scalar_tensor_tensor(out=x[:], in0=bias_d[:].unsqueeze(1).to_broadcast([P, TT, D]), scalar=gate[:, 3:4],
                                                        in1=x[:], op0=ALU.mult, op1=ALU.add))
                link(nc.vector.tensor_scalar(comb[:], comb[:], gate_s[:, 2 + layer:3 + layer], None, ALU.mult))

                pl = plan["ffn", layer]

                def split_low(k, par):
                    dve.wait_ge(w_hi, k + first + 1)
                    if layer:
                        nc.vector.tensor_copy(bias_now[:, par], bias_gu[:, bass.ds(k, 1)].rearrange("p o m n -> p (o m) n"))
                    nc.vector.scalar_tensor_tensor(out=wsp[par][1], in0=wst, scalar=WS, in1=wsp[par][0],
                                                   op0=ALU.mult, op1=ALU.subtract).then_inc(w_split, 1)

                def units(k, par):
                    def unit_low(u):
                        s, (c, m) = u % 2, divmod(u, IH)
                        mn = IT[m][1]
                        dve.wait_ge(h_hi, (k + first) * UNITS + u + 1)
                        nc.vector.tensor_tensor(hT[1][0:mn, m, c * CW:(c + 1) * CW], h32[s][0:mn, :],
                                                hT[0][0:mn, m, c * CW:(c + 1) * CW], ALU.subtract).then_inc(hT_ready, 1)

                    for u in range(UNITS):
                        s, m = u % 2, u % IH
                        mn = IT[m][1]
                        pl.written(dve, f"u{u}", k)
                        dve.wait_ge(sil_ready, (k + first) * UNITS + u + 1)
                        if u >= 2 or not isinstance(k, int) or k > 0:
                            dve.wait_ge(hT_ready, (k + first) * UNITS + u - 1)
                        up = psum[0:mn, 2 * s + 1, 0:CW]
                        if layer:
                            ins = nc.vector.scalar_tensor_tensor(out=h32[s][0:mn, :], in0=up,
                                                                 scalar=bias_now[0:mn, par, m, 1:2],
                                                                 in1=sil[s][0:mn, :], op0=ALU.add, op1=ALU.mult)
                        else:
                            ins = nc.vector.tensor_tensor(h32[s][0:mn, :], up, sil[s][0:mn, :], ALU.mult)
                        ins.then_inc(h_ready, 1)
                        if u:
                            unit_low(u - 1)
                    unit_low(UNITS - 1)

                def combine(k):
                    for t in range(TT):
                        pl.written(dve, f"d{t}", k)
                        nc.vector.scalar_tensor_tensor(out=x[:, t, :], in0=psum[:, 4 + t % 4, :],
                                                       scalar=comb[:, t, bass.ds(k, 1)], in1=x[:, t, :],
                                                       op0=ALU.mult, op1=ALU.add).then_inc(psum_free[4 + t % 4].sem, 1)

                split_low(0, 0)
                units(0, 0)
                split_low(1, 1)
                combine(0)
                with dve.Fori(0, NBLK[layer] // 2 - 1) as j:
                    for par in range(2):
                        k = j * 2 + 1 + par
                        units(k, 1 - par)
                        split_low(k + 1, par)
                        combine(k)
                units(NBLK[layer] - 1, 1)
                combine(NBLK[layer] - 1)
                link(nc.vector.engine_nop())
                end_phase()

            if stop >= 2:
                ffn(0)
            if stop >= 3:
                for n, dst in enumerate((wq, wo)):
                    dve.wait_ge(stage_hi, 9 + n)
                    nc.vector.scalar_tensor_tensor(out=dst[1][:], in0=stage1[n], scalar=WS, in1=dst[0][:],
                                                   op0=ALU.mult, op1=ALU.subtract).then_inc(stage_used, 1)
                dve.wait_ge(stage_hi, 11)
                nc.vector.scalar_tensor_tensor(out=wk[1][:, :, 0:2 * P], in0=stage1[0][:, :, 0:2 * P], scalar=WS, in1=wk[0][:, :, 0:2 * P],
                                               op0=ALU.mult, op1=ALU.subtract).then_inc(stage_used, 1)
                link(nc.vector.tensor_scalar(bias_gu[:, :, :, 1:2], bias_gu[:, :, :, 1:2], WS, None, ALU.mult))
                for v in pr + [t for pair in k1 + q1 for t in pair]:
                    ins = nc.vector.memset(v, 0.0)
                link(ins)
                for par in range(2):
                    link(nc.vector.memset(q1[par][0][MASKED:MASKED + NMASK], FAR))
                nc.vector.engine_nop().then_inc(aug_zero, 1)
                layernorm(2)
                pl = plan["q", 1]
                with dve.Fori(0, NCH) as c:
                    for m in range(KC):
                        dve.wait_ge(hi_done.sem, hi["q", 1].at(c, m))
                        nc.vector.scalar_tensor_tensor(out=col(q1T[1], c, CW)[:, m, :], in0=psum[:, m, 0:CW], scalar=QS,
                                                       in1=col(q1T[0], c, CW)[:, m, :], op0=ALU.mult, op1=ALU.subtract).then_inc(psum_free[m].sem, 1)
                nc.vector.engine_nop().then_inc(q1T_ready, 1)
                pl = plan["att", 1]

                def keys1(b, par, g):
                    dve.wait_ge(hi_done.sem, hi["kT", 1].at(b, g))
                    ins = nc.vector.scalar_tensor_tensor(out=k1[par][1][0:HD, g, :], in0=psum[HD * g:HD * (g + 1), 7, 0:SK], scalar=1.0 / WS,
                                                         in1=k1[par][0][0:HD, g, :], op0=ALU.mult, op1=ALU.subtract)
                    if g == NG - 1:
                        ins.then_inc(psum_free[7].sem, 1)

                def quotient1(b, par):
                    dve.wait_ge(exp_done, b * NH + NH)
                    nc.vector.reciprocal(rden[0:S, :], den1[par][0:S, :]).then_inc(rden_ready, 1)
                    dve.wait_ge(rden_ready, b + B + 1)
                    pl.written(dve, "o", b)
                    nc.vector.tensor_tensor(norm[0][0:S, :].rearrange("p (h c) -> p h c", h=NH), psum[0:S, 4, :].rearrange("p (h c) -> p h c", h=NH),
                                            rden[0:S, :].unsqueeze(2).to_broadcast([S, NH, HD]), ALU.mult).then_inc(norm_ready.sem, 1)

                def heads(b, par, before, after):
                    def transposed(h):
                        pl.written(dve, f"pT{h}", b)
                        nc.vector.tensor_copy(pT[h % 2], psum[:, pl.bank(f"pT{h}"), 0:3 * S].rearrange("p (t s) -> p t s", t=3)).then_inc(pT_ready, 1)

                    for h in range(NH):
                        pl.written(dve, f"s{h}", b)
                        if h >= NS:
                            dve.wait_ge(exp_done, b * NH + h + 1 - NS)
                        elif before:
                            dve.wait_ge(exp_done, b * NH + h + 1 - NS)
                        nc.vector.reduce_max(nmax[0:S, h % NS:h % NS + 1], psum[0:S, h % NS, 0:SK], AX_X, negate=True).then_inc(nmax_ready, 1)
                        if h >= 2:
                            transposed(h - 2)
                        if before and h == 1:
                            quotient1(b - 1, 1 - par)
                        if before and h == 5:
                            att_columns(1, pl, b - 1)
                        if after and K_AT + 1 < h <= K_AT + 1 + NG:
                            keys1(b + 1, 1 - par, h - K_AT - 2)
                    transposed(NH - 2)
                    transposed(NH - 1)

                for g in range(NG):
                    keys1(0, 0, g)
                heads(0, 0, False, True)
                with dve.Fori(0, B // 2 - 1) as j:
                    heads(j * 2 + 1, 1, True, True)
                    heads(j * 2 + 2, 0, True, True)
                heads(B - 1, 1, True, False)
                quotient1(B - 1, 1)
                att_columns(1, pl, B - 1)
                project_out(1)
            if stop >= 4:
                ffn(1)

        @block.tensor
        def _(pe):
            def product(dst, stationary, moving, last=None):
                n, total = 0, 3 * KC
                for sh, mh in PASSES:
                    for k in range(KC):
                        ins = nc.tensor.matmul(dst, stationary(sh, k), moving(mh, k), start=n == 0, stop=n == total - 1)
                        n += 1
                if last is not None:
                    ins.then_inc(last, 1)
                return ins

            def transposes(n):
                def tile(t, j, par):
                    pl = plan["ln", n][par]
                    pe.wait_ge(norm_ready.sem, norms["ln", n].at(t))
                    pl.free(pe, "n", j)
                    for k in range(KC):
                        ins = nc.tensor.transpose(psum[:, par, k * P:(k + 1) * P], norm[par][:, k * P:(k + 1) * P], ident[:])
                    ins.then_inc(psum_full[par].sem, 1)
                in_pairs(pe, tile)

            def att_transposes(layer, pl, b):
                pe.wait_ge(norm_ready.sem, norms["att", layer].at(b))
                pl.free(pe, "oT", b)
                for k in range(KC):
                    ins = nc.tensor.transpose(psum[:, pl.bank("oT"), k * S:(k + 1) * S], norm[0][0:S, k * P:(k + 1) * P], ident[0:S, 0:S])
                ins.then_inc(pl.full_sem("oT"), 1)

            def project_out(layer):
                pe.wait_ge(x_ready, layer + 1)

                def tile(t, j, par):
                    pl = plan["out", layer][par]
                    pl.free(pe, "w", j)
                    product(psum[:, par, :], lambda h, k: col(nT[h], t)[:, k, :], lambda h, k: wo[h][:, k, :], psum_full[par].sem)
                in_pairs(pe, tile)

            transposes(0)
            pe.wait_ge(stage_used, 5)
            pe.wait_ge(phase, 2)
            pl = plan["q", 0]
            with pe.Fori(0, NCH) as c:
                for m in range(KC):
                    pl.free(pe, f"q{m}", c)
                    product(psum[:, m, 0:CW], lambda h, k: wq[h][:, k, m * P:(m + 1) * P], lambda h, k: col(nT[h], c, CW)[:, k, :],
                            psum_full[m].sem)
                for p in range(NPAIR):
                    m, half = divmod(p, 2)
                    pl.free(pe, f"f{p}", c)
                    if half == 0:
                        pe.wait_ge(psum_free[m].sem, pl.r[m].before(c + 1))
                    for n, (sh, mh) in enumerate(PASSES):
                        ins = nc.tensor.matmul(psum[:, 4 + p % 4, 0:CW], bd_q[sh][:, half * P:(half + 1) * P], qh[mh][:, m, :],
                                               start=n == 0, stop=n == 2)
                    ins.then_inc(pl.full_sem(f"f{p}"), 1)

            pl = plan["att", 0]

            def keys(b):
                pe.wait_ge(ctx_split, b + 1)
                for m in range(KC):
                    pl.free(pe, f"kT{m}", b)
                    product(psum[:, m % 2, 0:SK], lambda h, k: wk[h][:, k, m * P:(m + 1) * P], lambda h, k: ctx_s[h][:, k, :],
                            psum_full[m % 2].sem)

            def values(b):
                for t, (t0, tn) in enumerate(KT):
                    pl.free(pe, f"v{t}", b)
                    product(psum[0:tn, pl.bank(f"v{t}"), :], lambda h, k: ctx_s[h][:, k, t0:t0 + tn], lambda h, k: wv[h][:, k, :],
                            pl.full_sem(f"v{t}"))

            def features(b):
                pe.wait_ge(psum_free[0].sem, pl.r[0].before(b + 1))
                pe.wait_ge(psum_free[1].sem, pl.r[1].before(b + 1))
                for t, (t0, tn) in enumerate(KT):
                    for half in range(2):
                        pl.free(pe, f"kf{t}{half}", b)
                        for m in (2 * half, 2 * half + 1):
                            for n, (sh, mh) in enumerate(PASSES):
                                ins = nc.tensor.matmul(psum[0:tn, 4 + half, (m % 2) * 256:(m % 2 + 1) * 256], kT[sh][:, m, t0:t0 + tn],
                                                       bd_k[mh], start=n == 0, stop=n == 2)
                        ins.then_inc(psum_full[4 + half].sem, 1)

            def sums(b):
                for bank in (2, 3, 4, 5):
                    pe.wait_ge(psum_free[bank].sem, pl.r[bank].before(b + 1))
                for q in range(2):
                    pl.free(pe, f"kv{q}", b)
                    for p in range(4 * q, 4 * q + 4):
                        for t, (t0, tn) in enumerate(KT):
                            ins = nc.tensor.matmul(psum[:, 6 + q, (p % 4) * 2 * VW:(p % 4 + 1) * 2 * VW], kf[0:tn, t, p * P:(p + 1) * P],
                                                   va[0:tn, t, 2 * p:2 * p + 2, :].rearrange("p h c -> p (h c)"),
                                                   start=t == 0, stop=t == len(KT) - 1)
                    ins.then_inc(psum_full[6 + q].sem, 1)

            def outputs(b):
                pe.wait_ge(kv_ready, b + 1)
                for q in range(2):
                    pl.free(pe, f"o{q}", b)
                    for p in range(4 * q, 4 * q + 4):
                        for n, (sh, mh) in enumerate(PASSES):
                            ins = nc.tensor.matmul(psum[0:S, 6 + q, (p % 4) * 2 * VW:(p % 4 + 1) * 2 * VW], col(qf[sh], b, S)[:, p, :],
                                                   kvb[mh][:, p, :], start=n == 0, stop=n == 2)
                    ins.then_inc(psum_full[6 + q].sem, 1)

            for bank in (4, 5, 6, 7):
                pe.wait_ge(psum_free[bank].sem, plan["q", 0].r[bank].before(NCH))
            pe.wait_ge(q_split, 1)
            keys(0)
            values(0)
            features(0)
            sums(0)
            with pe.Fori(0, B - 1) as b:
                keys(b + 1)
                values(b + 1)
                outputs(b)
                features(b + 1)
                att_transposes(0, pl, b)
                sums(b + 1)
            outputs(B - 1)
            att_transposes(0, pl, B - 1)
            project_out(0)

            def ffn(layer):
                transposes(2 * layer + 1)
                pe.wait_ge(phase, (4, 8)[layer])
                plan["route", layer].free(pe, "l")
                for t in range(TT):
                    for n, (sh, mh) in enumerate(PASSES):
                        for k in range(KC):
                            ins = nc.tensor.matmul(psum[:, 7, t * 16:(t + 1) * 16], nT[sh][:, k, t * P:(t + 1) * P], route_w[layer][mh][:, k, :],
                                                   start=n == 0 and k == 0, stop=n == 2 and k == KC - 1)
                ins.then_inc(psum_full[7].sem, 1)
                pl = plan["ffn", layer]
                first = NBLK[0] * layer

                def blk(k, par):
                    pe.wait_ge(w_split, k + first + 1)
                    for u in range(UNITS):
                        c, m = divmod(u, IH)
                        m0, mn = IT[m]
                        if u >= 2 or not isinstance(k, int) or k > 0:
                            pe.wait_ge(h_ready, (k + first) * UNITS + u - 1)
                        for n, w in enumerate("gu"):
                            product(psum[0:mn, 2 * (u % 2) + n, 0:CW],
                                    lambda h, kc: wsp[par][h][:, n * GN + kc * I + m0:n * GN + kc * I + m0 + mn],
                                    lambda h, kc: nT[h][:, kc, c * CW:(c + 1) * CW], pl.full_sem(f"{w}{u}"))
                    for t in range(TT):
                        c = (t * P + P - 1) // CW
                        pe.wait_ge(hT_ready, (k + first) * UNITS + IH * (c + 1))
                        pl.free(pe, f"d{t}", k)
                        n = 0
                        for sh, mh in PASSES:
                            for m, (m0, mn) in enumerate(IT):
                                ins = nc.tensor.matmul(psum[:, 4 + t % 4, :], hT[sh][0:mn, m, t * P:(t + 1) * P],
                                                       wsp[par][mh][0:mn, 2 * GN + m * D:2 * GN + (m + 1) * D],
                                                       start=n == 0, stop=n == 3 * IH - 1)
                                n += 1
                        ins.then_inc(pl.full_sem(f"d{t}"), 1)

                blk(0, 0)
                with pe.Fori(0, NBLK[layer] // 2 - 1) as j:
                    for par in range(2):
                        blk(j * 2 + 1 + par, (1 + par) % 2)
                blk(NBLK[layer] - 1, 1)

            if stop >= 2:
                ffn(0)
            if stop >= 3:
                pe.wait_ge(stage_used, 8)
                transposes(2)
                pe.wait_ge(phase, 6)
                pl = plan["q", 1]
                with pe.Fori(0, NCH) as c:
                    for m in range(KC):
                        pl.free(pe, f"q{m}", c)
                        product(psum[:, m, 0:CW], lambda h, k: wq[h][:, k, m * P:(m + 1) * P], lambda h, k: col(nT[h], c, CW)[:, k, :],
                                psum_full[m].sem)
                pl = plan["att", 1]

                def keys1(b):
                    pe.wait_ge(ctx_split, b + B + 1)
                    pl.free(pe, "k", b)
                    product(psum[:, 7, 0:SK], lambda h, k: wk[h][:, k, 0:P], lambda h, k: ctx_s[h][:, k, :], psum_full[7].sem)

                def values1(b):
                    pl.free(pe, "v", b)
                    for t, (t0, tn) in enumerate(KT):
                        product(psum[0:tn, 7, t * P:(t + 1) * P], lambda h, k: ctx_s[h][:, k, t0:t0 + tn], lambda h, k: wk[h][:, k, P:2 * P],
                                psum_full[7].sem if t == 2 else None)

                def heads(b, par, before, after):
                    pl.free(pe, "k", b + 1)
                    pe.wait_ge(q1_ready, b + 1)

                    def scores(h):
                        if h >= NS:
                            pe.wait_ge(exp_done, b * NH + h + 1 - NS)
                        elif before:
                            pe.wait_ge(exp_done, b * NH + h + 1 - NS)
                        for n, (sh, mh) in enumerate(PASSES):
                            ins = nc.tensor.matmul(psum[0:S, h % NS, 0:SK], q1[par][sh][:, h, :], k1[par][mh][:, h // 4, :], start=n == 0, stop=n == 2)
                        ins.then_inc(psum_full[h % NS].sem, 1)

                    def turn(h):
                        pe.wait_ge(exp_done, b * NH + h + 1)
                        for t in range(3):
                            ins = nc.tensor.transpose(psum[:, pl.bank(f"pT{h}"), t * S:(t + 1) * S], pr[h % NS][0:S, t * P:(t + 1) * P], ident[0:S, 0:S])
                        ins.then_inc(pl.full_sem(f"pT{h}"), 1)

                    def weigh(h):
                        pe.wait_ge(pT_ready, b * NH + h + 1)
                        if h == 0 and before:
                            pe.wait_ge(norm_ready.sem, norms["att", 1].at(b - 1))
                        for t, (t0, tn) in enumerate(KT):
                            ins = nc.tensor.matmul(psum[0:S, 4, h * HD:(h + 1) * HD], pT[h % 2][0:tn, t, :], v1[par][0:tn, t, (h // 4) * HD:(h // 4 + 1) * HD],
                                                   start=t == 0, stop=t == 2)
                        if h == NH - 1:
                            ins.then_inc(psum_full[4].sem, 1)

                    scores(0)
                    scores(1)
                    for h in range(NH):
                        if h + 2 < NH:
                            scores(h + 2)
                        turn(h)
                        if before and h == 2:
                            att_transposes(1, pl, b - 1)
                        if h:
                            weigh(h - 1)
                        if after and h == K_AT:
                            keys1(b + 1)
                        if after and h == V_AT:
                            values1(b + 1)
                    weigh(NH - 1)

                keys1(0)
                values1(0)
                heads(0, 0, False, True)
                with pe.Fori(0, B // 2 - 1) as j:
                    heads(j * 2 + 1, 1, True, True)
                    heads(j * 2 + 2, 0, True, True)
                heads(B - 1, 1, True, False)
                att_transposes(1, pl, B - 1)
                project_out(1)
            if stop >= 4:
                ffn(1)


STOP = 4


def kernel(**inputs):
    import numpy as np
    import concourse.bacc as bacc
    from concourse.bass_utils import run_bass_kernel_spmd

    v = {k: np.asarray(t) for k, t in inputs.items()}

    def chunks(w):
        return w.reshape(KC, P, -1).transpose(1, 0, 2)

    def per_part(b):
        return b.reshape(KC, P).T

    def block_weights(gate, up, down):
        n = gate.shape[0]
        g, u = (w.reshape(n, KC, P, I).transpose(0, 2, 1, 3).reshape(n, P, KC * I) for w in (gate, up))
        d = np.zeros((n, IH * P, D), np.float32)
        d[:, 0:I] = down
        d = d.reshape(n, IH, P, D).transpose(0, 2, 1, 3).reshape(n, P, IH * D)
        return np.concatenate([g, u, d], axis=2)

    def cut(w, axis):
        n = w.shape[axis] // I
        return w.reshape(n, I, D) if axis == 0 else w.reshape(D, n, I).transpose(1, 0, 2)

    mask_f = np.zeros((P, B, 3), np.float32)
    mask_t = v["mask_BxS2_ff1"].T
    for t, (t0, tn) in enumerate(KT):
        mask_f[0:tn, :, t] = mask_t[t0:t0 + tn]
    bias_gu = np.zeros((P, NBLK[1], IH, 2), np.float32)
    for n, name in enumerate(("L1_ffn_s_gate_b", "L1_ffn_s_up_b")):
        for k in range(NBLK[1] - E):
            for m, (m0, mn) in enumerate(IT):
                bias_gu[0:mn, E + k, m, n] = v[name][k * I + m0:k * I + m0 + mn]
    slopes = (2.0 ** (-8.0 / NH)) ** np.arange(1, NH + 1, dtype=np.float32)
    slopes = slopes.astype(np.float32)
    q_aug = np.stack([np.repeat(slopes[:, None], S, 1), -slopes[:, None] * np.arange(S, dtype=np.float32)[None, :]])
    q_aug = np.stack([q_aug.astype(np.float16), (q_aug - q_aug.astype(np.float16)).astype(np.float16)])
    k_aug = np.stack([np.repeat(np.arange(SK, dtype=np.float16)[None], NG, 0), np.ones((NG, SK), np.float16)])
    arrays = {
        "x": v["x"].reshape(T, D),
        "ctxT": v["ctx_2048"].transpose(0, 2, 1).reshape(B, KC, P, SK).transpose(0, 2, 1, 3),
        "mask_f": mask_f,
        "mask_b": v["mask_BxS2_bf1"].view(np.uint8).reshape(1, B, SK).repeat(NMASK, 0),
        "gates": np.concatenate([v["g_xattn"], v["g_ffn"]])[None].repeat(P, 0),
        "w_attn0": np.stack([chunks(v[f"L0_xattn_{w}"].T) for w in ("Wq", "Wk", "Wv", "Wo")]),
        "w_attn1": np.stack([chunks(v[f"L1_xattn_{w}"]) for w in ("Wq", "Wo")]),
        "w_kv1": chunks(np.concatenate([v["L1_xattn_Wk"], v["L1_xattn_Wv"]], axis=1)),
        "wqf": v["L0_xattn_Wqf"].T, "wkf": v["L0_xattn_Wkf"].T,
        "bq": per_part(v["L0_xattn_bq"]), "bk": per_part(v["L0_xattn_bk"]),
        "bv": v["L0_xattn_bv"], "bo": v["L0_xattn_bo"], "bd": v["L1_ffn_s_down_b"],
        "route0": chunks(np.concatenate([v["L0_ffn_gate_w"].T, v["L0_ffn_shared_gate_w"]], axis=1)),
        "route1": chunks(v["L1_ffn_router_w"].T),
        "w_blk0": block_weights(np.concatenate([v["L0_ffn_w_gate"], cut(v["L0_ffn_sw_gate"], 1)]),
                                np.concatenate([v["L0_ffn_w_up"], cut(v["L0_ffn_sw_up"], 1)]),
                                np.concatenate([v["L0_ffn_w_down"], cut(v["L0_ffn_sw_down"], 0)])),
        "w_blk1": block_weights(np.concatenate([v["L1_ffn_gate_w"], cut(v["L1_ffn_s_gate_w"], 1)]),
                                np.concatenate([v["L1_ffn_up_w"], cut(v["L1_ffn_s_up_w"], 1)]),
                                np.concatenate([v["L1_ffn_down_w"], cut(v["L1_ffn_s_down_w"], 0)])),
        "bias_gu": bias_gu,
        "ident": np.eye(P, dtype=np.float32),
        "iota8": np.arange(E, dtype=np.float32)[None].repeat(P, 0),
        "q_aug": q_aug, "k_aug": k_aug,
    }
    arrays = {f"in_{k}": np.ascontiguousarray(t) for k, t in arrays.items()}
    nc = bacc.Bacc("TRN2", target_bir_lowering=False, num_devices=1)
    aps = {k[3:]: nc.dram_tensor(k, t.shape, mybir.dt.from_np(t.dtype), kind="ExternalInput").ap() for k, t in arrays.items()}
    out = nc.dram_tensor("out", (T, D), F32, kind="ExternalOutput").ap()
    build(nc, aps, out, STOP)
    r = run_bass_kernel_spmd(nc, [arrays], core_ids=[0])
    return r.results[0]["out"].reshape(B, S, D)
```

```python
from contextlib import ExitStack

import concourse.bass as bass
from concourse import mybir

F32 = mybir.dt.float32
F16 = mybir.dt.float16
U8 = mybir.dt.uint8
U32 = mybir.dt.uint32
ALU = mybir.AluOpType
ACT = mybir.ActivationFunctionType
AX_X = mybir.AxisListType.X

P = 128
B, S, D = 16, 100, 512
SK = 361
KC = D // P
T = B * S
TT = (T + P - 1) // P
TP = TT * P
LAST = T - (TT - 1) * P
PAIRS = TT // 2
NCH = 4
CW = TP // NCH
KT = [(0, P), (P, P), (2 * P, SK - 2 * P)]
NH, HD, FD = 16, 32, 64
NG = 4
NPAIR = NH // 2
VW = HD + 1
E = 8
I = 352
IT = [(0, P), (P, P), (2 * P, I - 2 * P)]
IH = len(IT)
UNITS = NCH * IH
NBLK = (4, 2)
SLOTS = 256
HALVES = SLOTS // P
NTILE = (2 * T - E) // SLOTS + E
NHALF = NTILE * HALVES
MAX_TILES = (T + SLOTS - 1) // SLOTS
WS = 64.0
KVS = 256.0
PASSES = ((0, 0), (0, 1), (1, 0))
EPS_LN = 1e-5
EPS_DEN = 1e-8
ALIBI, MASKED, NMASK, FAR = HD, 64, 32, 60000.0
QS = 1.0 / (WS * HD ** 0.5)
K_AT, V_AT = 4, 11
PREFETCH = (3, 6, 9)
RANKS_AT = 3
NS = 3


class Count:

    def __init__(self, sem, first=0):
        self.sem, self.base, self.first, self.per = sem, 0, first, 0
        self.total = 0

    def span(self, times, per=1):
        new = Count(self.sem, self.first)
        new.base, new.per = self.total, per
        self.total += times * per
        return new

    def at(self, n=0, k=0):
        return n * self.per + (self.base + k + 1)

    def before(self, n=0, k=0):
        return n * self.per + (self.base + k + self.first)


class Banks:

    def __init__(self, full, free, uses, times, other=()):
        per = {}
        self.place = {}
        for name, bank in uses:
            self.place[name] = (bank, per.get(bank, 0))
            per[bank] = per.get(bank, 0) + 1
        self.f = {b: full[b].span(times, n) for b, n in per.items()}
        self.r = {b: free[b].span(times, n) for b, n in per.items() if b not in other}

    def bank(self, name):
        return self.place[name][0]

    def written(self, eng, name, n=0):
        b, k = self.place[name]
        eng.wait_ge(self.f[b].sem, self.f[b].at(n, k))

    def free(self, eng, name, n=0):
        b, k = self.place[name]
        eng.wait_ge(self.r[b].sem, self.r[b].before(n, k))

    def free_after(self, eng, name, n=0):
        b, k = self.place[name]
        eng.wait_ge(self.r[b].sem, self.r[b].before(n, k + 1))

    def full_sem(self, name):
        return self.f[self.place[name][0]].sem

    def free_sem(self, name):
        return self.r[self.place[name][0]].sem


def build(nc, a, out, stop=4):
    with ExitStack() as ctx:
        def sb(name, shape, dt=F32):
            return ctx.enter_context(nc.sbuf_tensor(name, shape, dt))

        x = sb("x", [P, TT, D])
        nT = [sb("nT_hi", [P, KC, TP], F16), sb("nT_lo", [P, KC, TP], F16)]
        big = sb("big", [P, NPAIR * TP])
        work_words = 3 * (2 * KC * I + IH * D)
        work = sb("work", [P, work_words])
        wproj = sb("wproj", [P, 4 * KC * D])
        wq, wk, wv, wo = ([wproj[:, (2 * i + h) * KC * D // 2:(2 * i + h + 1) * KC * D // 2].bitcast(F16)
                           .rearrange("p (k n) -> p k n", k=KC) for h in range(2)] for i in range(4))
        norm = [sb(f"norm{i}", [P, D]) for i in range(2)]
        ident = sb("ident", [P, P])
        cols = sb("cols", [P, 80])
        stats = sb("stats", [P, TT, 6])
        mv = sb("mv", [P, TT, 2])
        rstd = sb("rstd", [P, TT])
        mhalf = sb("mhalf", [P, TT])
        mask_c = sb("mask_c", [P, B, 3])
        route_s = [sb(f"route_s{i}", [P, KC, 16]) for i in range(2)]
        route_w = [[sb(f"route_w{i}{h}", [P, KC, 16], F16) for h in range(2)] for i in range(2)]
        logit = sb("logit", [P, TT, 16])
        top = sb("top", [P, TT, 8])
        topi = sb("topi", [P, TT, 8], U32)
        shared = sb("shared", [P, TT])
        iota = sb("iota", [P, P])
        token = sb("token", [P, 2 * TT])
        ones16, before16 = sb("ones16", [P, P], F16), sb("before16", [P, P], F16)
        oh_sum = sb("oh_sum", [P, TT, E], F16)
        tiles = sb("tiles", [P, E])
        ends = sb("ends", [P, E])
        slot = sb("slot", [P, 2 * TT])
        low = sb("low", [P, 2 * TT])
        slot_u = sb("slot_u", [P, TT, 2], U32)
        source = sb("source", [P, NHALF], U32)
        expert = sb("expert", [P, NTILE])
        expert_u = sb("expert_u", [P, NTILE], U32)
        offset = sb("offset", [P, 2, HALVES], U32)
        rt = sb("rt", [P, 8, TT])
        oh = sb("oh", [P, 2, TT, E])
        bias_gu = sb("bias_gu", [P, NBLK[1], IH, 2])
        bias_v = sb("bias_v", [P, D])
        bias_o = sb("bias_o", [P, D])
        bias_d = sb("bias_d", [P, D])
        psum = ctx.enter_context(nc.psum_tensor("psum", [P, 8, 512], F32))

        bq, bk = cols[:, 0:4], cols[:, 4:8]
        gate, gate_in = cols[:, 8:12], cols[:, 12:16]
        den, rden = cols[:, 16:32], cols[:, 32:48]
        gate_s = cols[:, 48:52]
        tick = cols[:, 52:53]
        nmax = cols[:, 53:53 + NS]
        den1 = [cols[:, 16:32], cols[:, 56:72]]

        used = [0]

        def carve(n, dt, pattern=None, rows=slice(0, P), **dims):
            v = work[rows, used[0]:used[0] + n]
            used[0] += n
            if dt != F32:
                v = v.bitcast(dt)
            return v.rearrange(pattern, **dims) if pattern else v

        CT = KC * SK
        ctx_f = carve(CT, F32, "p (k s) -> p k s", k=KC)
        ctx_s = [carve(CT // 2, F16, "p (k s) -> p k s", k=KC) for _ in range(2)]
        shared_end = used[0]
        kT = [carve(CT // 2, F16, "p (k s) -> p k s", k=KC) for _ in range(2)]
        kf = carve(3 * NH * FD, F32, "p (t f) -> p t f", t=3)
        va = carve(3 * NH * VW, F32, "p (t h c) -> p t h c", t=3, h=NH)
        kv32 = carve(NH * VW, F32, "p (a c) -> p a c", a=NPAIR)
        kvb = [carve(NH * VW // 2, F16, "p (a c) -> p a c", a=NPAIR) for _ in range(2)]
        bd_k = [carve(128, F16) for _ in range(2)]
        bd_q = [carve(128, F16) for _ in range(2)]
        assert KC * CW <= 3 * NH * FD
        qh = [kf.rearrange("p t f -> p (t f)")[:, h * KC * CW // 2:(h + 1) * KC * CW // 2].bitcast(F16)
              .rearrange("p (m t) -> p m t", m=KC) for h in range(2)]
        qf = [big[:, h * NPAIR * TP // 2:(h + 1) * NPAIR * TP // 2].bitcast(F16)
              .rearrange("p (m t) -> p m t", m=NPAIR) for h in range(2)]
        stage = [big[:, i * KC * D:(i + 1) * KC * D].rearrange("p (k n) -> p k n", k=KC) for i in range(4)]
        bd_f = [big[:, 4 * KC * D + 256 * i:4 * KC * D + 256 * (i + 1)] for i in range(2)]

        used[0] = shared_end
        k1 = [[carve(NG * SK // 2, F16, "p (g s) -> p g s", g=NG) for _ in range(2)] for _ in range(2)]
        q1 = [[carve(NH * S // 2, F16, "p (h s) -> p h s", h=NH) for _ in range(2)] for _ in range(2)]
        v1 = [carve(3 * P, F32, "p (t c) -> p t c", t=3) for _ in range(2)]
        pr = [carve(3 * P, F32) for _ in range(NS)]
        pT = [carve(3 * S, F32, "p (t s) -> p t s", t=3) for _ in range(2)]
        mask8 = carve(B * SK // 4, U8, "p (b s) -> p b s", rows=slice(MASKED, MASKED + NMASK), b=B)
        q1T = [big[:, h * KC * TP // 2:(h + 1) * KC * TP // 2].bitcast(F16).rearrange("p (m t) -> p m t", m=KC) for h in range(2)]
        mask16 = big[MASKED:MASKED + NMASK, KC * TP:KC * TP + B * SK // 2].bitcast(F16).rearrange("p (b s) -> p b s", b=B)

        hT = [big[:, h * IH * TP // 2:(h + 1) * IH * TP // 2].bitcast(F16)
              .rearrange("p (m t) -> p m t", m=IH) for h in range(2)]
        sil = [big[:, IH * TP + i * CW:IH * TP + (i + 1) * CW] for i in range(2)]
        h32 = [big[:, IH * TP + (2 + i) * CW:IH * TP + (3 + i) * CW] for i in range(2)]
        FF = IH * TP + 4 * CW
        rows = [big[:, FF + i * HALVES * D:FF + (i + 1) * HALVES * D].rearrange("p (q d) -> p q d", q=HALVES) for i in range(2)]
        FF += 2 * HALVES * D
        stage1 = [big[:, at:at + KC * D].rearrange("p (k n) -> p k n", k=KC) for at in (FF, NPAIR * TP - KC * D)]
        assert FF + 2 * KC * D <= NPAIR * TP and KC * D <= 2 * HALVES * D
        y = [big[:, FF + i * HALVES * D:FF + (i + 1) * HALVES * D].rearrange("p (q d) -> p q d", q=HALVES) for i in range(2)]
        FF += 2 * HALVES * D
        xg = [big[:, FF + h * KC * SLOTS // 2:FF + (h + 1) * KC * SLOTS // 2].bitcast(F16)
              .rearrange("p (k t) -> p k t", k=KC) for h in range(2)]
        FF += KC * SLOTS
        hg = [big[:, FF + h * IH * SLOTS // 2:FF + (h + 1) * IH * SLOTS // 2].bitcast(F16)
              .rearrange("p (m t) -> p m t", m=IH) for h in range(2)]
        FF += IH * SLOTS
        assert FF <= NPAIR * TP and 2 * IH * SLOTS <= 4 * CW
        silg = [big[:, IH * TP + i * SLOTS:IH * TP + (i + 1) * SLOTS] for i in range(IH)]
        hg32 = [big[:, IH * TP + (IH + i) * SLOTS:IH * TP + (IH + i + 1) * SLOTS] for i in range(IH)]
        plan_at = [IH * TP + 4 * CW]

        def table(words, dt, pattern, **dims):
            v = big[:, plan_at[0]:plan_at[0] + words]
            plan_at[0] += words
            return (v if dt == F32 else v.bitcast(dt)).rearrange(pattern, **dims)

        NC2 = 2 * TT
        ge = table(NC2 * (NHALF + 1), F32, "p (n j) -> p n j", n=NC2)
        diff = table(NC2 * NHALF, F32, "p (n j) -> p n j", n=NC2)
        oh_high = table(NC2 * NHALF // 2, F16, "p (n j) -> p n j", n=NC2)
        oh_low = table(NC2 * P // 2, F16, "p (n j) -> p n j", n=NC2)
        slot_all = table(TT * E, F32, "p (t e) -> p t e", t=TT)
        chosen = table(2 * TT * E, F32, "p (n t e) -> p n t e", n=2, t=TT)
        ge_tile = table(NTILE * E, F32, "p (i e) -> p i e", i=NTILE)
        assert plan_at[0] <= NPAIR * TP
        xn_d = nc.dram_tensor("xn_d", (TP, D), F32, kind="Internal").ap()
        ys_d = nc.dram_tensor("ys_d", (NTILE * SLOTS, D), F32, kind="Internal").ap()
        used[0] = 0
        GN = KC * I
        WN = 2 * GN + IH * D
        wst = carve(WN, F32)
        wsp = [[carve(WN // 2, F16) for h in range(2)] for s in range(2)]
        wstage = [wproj[:, 0:WN], wst]
        PIECE = [(0, GN), (GN, 2 * GN), (2 * GN, WN)]

        sems = {}

        def sem(name):
            sems[name] = ctx.enter_context(nc.semaphore(name))
            return sems[name]

        psum_full = [Count(sem(f"psum_full{b}")) for b in range(8)]
        psum_free = [Count(sem(f"psum_free{b}"), 1) for b in range(8)]
        hi_done = Count(sem("hi_done"))
        att_hi = Count(sem("att_hi"))
        x_loaded, const_loaded = [sem(f"x_loaded{i}") for i in range(2)], sem("const_loaded")
        stage_full = [sem(f"stage_full{i}") for i in range(4)]
        small_split = sem("small_split")
        stage_hi, stage_used = sem("stage_hi"), sem("stage_used")
        dve_chain = Count(sem("dve_chain"))
        gates_ready = sem("gates_ready")
        phase = sem("phase")
        stats_ready, rstd_ready = sem("stats_ready"), sem("rstd_ready")
        norm_ready = Count(sem("norm_ready"))
        q_split = sem("q_split")
        ctx_loaded, ctx_hi = sem("ctx_loaded"), sem("ctx_hi")
        ctx_split = sem("ctx_split")
        kv32_ready, kv_hi, kv_ready = sem("kv32_ready"), sem("kv_hi"), sem("kv_ready")
        den_ready, rden_ready = sem("den_ready"), sem("rden_ready")
        w_scaled = sem("w_scaled")
        w_loaded, w_hi, w_split = sem("w_loaded"), sem("w_hi"), sem("w_split")
        sil_ready, h_ready, h_hi, hT_ready = sem("sil_ready"), sem("h_ready"), sem("h_hi"), sem("hT_ready")
        logits_ready, top_ready, route_exp = sem("logits_ready"), sem("top_ready"), sem("route_exp")
        mask_loaded, aug_zero, nmax_ready = sem("mask_loaded"), sem("aug_zero"), sem("nmax_ready")
        q1_ready = sem("q1_ready")
        copied = sem("copied")
        q1T_ready, mask_ready = sem("q1T_ready"), sem("mask_ready")
        exp_done, pT_ready = sem("exp_done"), sem("pT_ready")
        x_ready = sem("x_ready")
        xn_stored = [sem(f"xn_stored{i}") for i in range(2)]
        picks_ready = sem("picks_ready")
        experts_ready = sem("experts_ready")
        tables_ready = sem("tables_ready")
        slots_ready = sem("slots_ready")
        offset_ready = sem("offset_ready")
        gathered = [sem(f"gathered{i}") for i in range(2)]
        y_used = sem("y_used")
        gw_loaded = [sem(f"gw_loaded{i}") for i in range(2)]
        gw_hi, gw_split = sem("gw_hi"), sem("gw_split")
        gsil_ready, gh_ready, gh_hi, gh_split = sem("gsil_ready"), sem("gh_ready"), sem("gh_hi"), sem("gh_split")
        xg_hi = sem("xg_hi")
        y_stored = [sem(f"y_stored{i}") for i in range(2)]
        stored = sem("stored")

        def banks(uses, times, other=()):
            return Banks(psum_full, psum_free, uses, times, other)

        def pair_banks(name):
            return [banks([(name, par)], PAIRS + 1 - par) for par in range(2)]

        plan = {}
        LINEAR = ([(f"kT{m}", m % 2) for m in range(KC)] + [("v0", 2), ("v1", 3), ("v2", 2)]
                  + [(f"kf{t}{h}", (3, 1, 0, 2, 3, 1)[2 * t + h]) for t in range(3) for h in range(2)]
                  + [("kv0", 4), ("kv1", 5), ("o0", 6), ("o1", 7), ("oT", 6)])
        SOFTMAX = ([(f"s{h}", h % NS) for h in range(NH)] + [(f"pT{h}", (3, 6)[h % 2]) for h in range(NH)]
                   + [("k", 7), ("v", 7), ("o", 4), ("oT", 5)])
        BLOCK = ([(f"{w}{u}", 2 * (u % 2) + n) for u in range(UNITS) for n, w in enumerate("gu")]
                 + [(f"d{t}", 4 + t % 4) for t in range(TT)])
        for layer in range(2):
            plan["ln", 2 * layer] = pair_banks("n")
            plan["q", layer] = banks([(f"q{m}", m) for m in range(KC)]
                                     + [(f"f{p}", 4 + p % 4) for p in range(NPAIR)] * (layer == 0), NCH)
            plan["att", layer] = banks((LINEAR, SOFTMAX)[layer], B, other=((), (0, 1, 2, 3, 4, 6))[layer])
            plan["out", layer] = pair_banks("w")
            plan["ln", 2 * layer + 1] = pair_banks("n")
            plan["route", layer] = banks([("l", 7)], 1)
            plan["slots", layer] = banks([("r", 6), ("i", 5)], 1)
            plan["first", layer] = banks(BLOCK, 1, other=range(4))
            plan["tile", layer] = banks([(f"u{m}", m) for m in range(IH)] + [("x0", 6), ("x1", 7), ("y0", 4), ("y1", 5)], NTILE,
                                        other=range(3))
            plan["ffn", layer] = banks(BLOCK, NBLK[layer] - 1, other=range(4))
        hi = {}
        for layer in range(2):
            hi["ln", 2 * layer] = hi_done.span(TT)
            hi["q", layer] = hi_done.span(NCH, KC + NPAIR * (layer == 0))
            hi["kT", layer] = hi_done.span(B, (KC, NG)[layer])
            hi["oT", layer] = att_hi.span(B)
            hi["ln", 2 * layer + 1] = hi_done.span(TT)
        norms = {}
        for layer in range(2):
            norms["ln", 2 * layer] = norm_ready.span(TT)
            norms["att", layer] = norm_ready.span(B)
            norms["ln", 2 * layer + 1] = norm_ready.span(TT)

        def col(v, t, n=P):
            return v[:, :, bass.ds(t * n, n)]

        def row(v, t):
            return v[:, bass.ds(t, 1), :].rearrange("p o d -> p (o d)")

        def at1(v, t):
            return v[:, bass.ds(t, 1)]

        def of_block(layer, k):
            return (plan["first", layer], 0) if isinstance(k, int) and k == 0 else (plan["ffn", layer], k - 1)

        assert NTILE % 2 == 0

        def in_pairs(eng, body):
            with eng.Fori(0, PAIRS) as j:
                body(j * 2, j, 0)
                body(j * 2 + 1, j, 1)
            body(TT - 1, PAIRS, 0)

        block = ctx.enter_context(nc.Block())
        CONSTS = [(ident[:], a["ident"]), (bq, a["bq"]), (bk, a["bk"]), (gate_in, a["gates"]),
                  (mask_c[:], a["mask_f"]), (iota[:], a["iota"]), (bias_gu[:], a["bias_gu"]),
                  (token[:], a["token"]), (ones16[:], a["ones16"]), (before16[:], a["before16"]),
                  (bias_v[:], a["bv"].partition_broadcast(P)), (bias_o[:], a["bo"].partition_broadcast(P)),
                  (bias_d[:], a["bd"].partition_broadcast(P)),
                  (route_s[0][:, :, 0:E + 1], a["route0"]), (route_s[1][:, :, 0:E], a["route1"])]
        N_CONST = len(CONSTS) + 2 * 4
        ZEROED = pr + [v for pair in k1 + q1 for v in pair]
        N_ZERO = len(ZEROED) + 2

        @block.sync
        def _(sp):
            half = TT // 2
            for n, (t0, t1) in enumerate(((0, half), (half, TT - 1))):
                sp.dma_start(x[:, t0:t1, :], a["x"][t0 * P:t1 * P, :].rearrange("(t p) d -> p t d", p=P)).then_inc(x_loaded[n], 16)
            sp.wait_ge(phase, 1)
            sp.dma_start(x[0:LAST, TT - 1, :], a["x"][(TT - 1) * P:T, :]).then_inc(x_loaded[1], 16)
            for n in range(4):
                sp.dma_start(stage[n], a["w_attn0"][n]).then_inc(stage_full[n], 16)
            sp.dma_start(ctx_f, a["ctxT"][0]).then_inc(ctx_loaded, 16)
            with sp.Fori(1, B) as b:
                sp.wait_ge(ctx_split, b)
                sp.dma_start(ctx_f, a["ctxT"][b]).then_inc(ctx_loaded, 16)

            def ffn_loads(layer):
                first = NBLK[0] * layer
                sp.wait_ge(x_ready, layer + 1)
                sp.dma_start(wst, a[f"w_shared{layer}"][0]).then_inc(w_loaded, 16)

                def store_rows(t, j, par):
                    sp.wait_ge(norm_ready.sem, norms["ln", 2 * layer + 1].at(t))
                    sp.dma_start(xn_d[bass.ds(t * P, P), :], norm[par][:]).then_inc(xn_stored[par], 16)
                in_pairs(sp, store_rows)
                sp.wait_ge(experts_ready, layer + 1)

                def load(i, par, wait=True):
                    e = sp.value_load(expert_u[0:1, bass.ds(i, 1)], min_val=0, max_val=E - 1)
                    if wait:
                        sp.wait_ge(gw_split, (i - 1) * len(PIECE) + layer * NTILE * len(PIECE))
                    sp.dma_start(wstage[par], a[f"w_expert{layer}"][bass.ds(e, 1)].rearrange("o p n -> (o p) n")).then_inc(gw_loaded[par], 16)

                load(0, 0, False)
                sp.wait_ge(w_split, first + 1)
                load(1, 1, False)
                with sp.Fori(1, NTILE // 2) as j:
                    for par in range(2):
                        load(j * 2 + par, par)
                sp.wait_ge(gw_split, NTILE * len(PIECE) * (layer + 1))
                sp.dma_start(wst, a[f"w_shared{layer}"][1]).then_inc(w_loaded, 16)
                for k in range(2, NBLK[layer]):
                    sp.wait_ge(w_split, k + first)
                    sp.dma_start(wst, a[f"w_shared{layer}"][k]).then_inc(w_loaded, 16)

                if layer == 0 and stop >= 3:
                    for par in range(2):
                        sp.wait_ge(y_stored[par], 16 * (NTILE // 2))
                    sp.wait_ge(w_split, 3)
                    sp.dma_start(stage1[0], a["w_attn1"][0]).then_inc(stage_full[0], 16)
                    sp.dma_start(stage1[1], a["w_attn1"][1]).then_inc(stage_full[1], 16)
                    sp.wait_ge(stage_used, 5)
                    sp.dma_start(stage1[0][:, :, 0:2 * P], a["w_kv1"]).then_inc(stage_full[0], 16)
                    sp.wait_ge(w_split, NBLK[0])

            if stop >= 2:
                ffn_loads(0)
            if stop >= 3:
                sp.dma_start(ctx_f, a["ctxT"][0]).then_inc(ctx_loaded, 16)
                sp.wait_ge(phase, 5)
                sp.dma_start(mask8, a["mask_b"]).then_inc(mask_loaded, 16)
                sp.wait_ge(aug_zero, N_ZERO)
                for par in range(2):
                    for h in range(2):
                        sp.dma_start(q1[par][h][ALIBI:ALIBI + 2], a["q_aug"][h]).then_inc(mask_loaded, 16)
                    sp.dma_start(k1[par][0][ALIBI:ALIBI + 2], a["k_aug"]).then_inc(mask_loaded, 16)
                with sp.Fori(1, B) as b:
                    sp.wait_ge(ctx_split, b + B)
                    sp.dma_start(ctx_f, a["ctxT"][b]).then_inc(ctx_loaded, 16)
            if stop >= 4:
                ffn_loads(1)
            sp.wait_ge(phase, {1: 3, 2: 5, 3: 7, 4: 9}[stop])
            sp.dma_start(out[0:(TT - 1) * P, :].rearrange("(t p) d -> p t d", p=P), x[:, 0:TT - 1, :]).then_inc(stored, 16)
            sp.dma_start(out[(TT - 1) * P:T, :], x[0:LAST, TT - 1, :]).then_inc(stored, 16)
            sp.wait_ge(stored, 32)

        @block.gpsimd
        def _(pool):
            def power(n):
                pool.wait_ge(stats_ready, n + 1)
                nc.gpsimd.tensor_tensor(rstd[:], rstd[:], mhalf[:], ALU.pow).then_inc(rstd_ready, 1)

            def experts(layer):
                rounds = (NTILE + TT) * layer
                pool.wait_ge(slots_ready, layer + 1)
                for par in range(2):
                    pool.wait_ge(xn_stored[par], 16 * (PAIRS + 1 - par) * (layer + 1))

                def fetch(numbers, par, src, count):
                    nc.gpsimd.tensor_copy(offset[:, par, :], numbers).then_inc(offset_ready, 1)
                    pool.wait_ge(offset_ready, count)
                    nc.gpsimd.tensor_tensor(tick, iota[:, 0:1], iota[:, 1:2], ALU.add)
                    for n in range(2):
                        nc.gpsimd.indirect_dma_start(rows[par][:, n, :], None, src, bass.IndirectOffsetOnAxis(offset[:, par, n:n + 1], 0)).then_inc(gathered[par], 16)

                def gather(i, j, par, reuse=True):
                    if reuse:
                        for q in range(HALVES):
                            plan["tile", layer].written(pool, f"x{q}", i - 2)
                    fetch(source[:, bass.ds(i * HALVES, HALVES)], par, xn_d, i + (1 + rounds))

                gather(0, 0, 0, False)
                gather(1, 0, 1, False)
                with pool.Fori(1, NTILE // 2) as j:
                    gather(j * 2, j, 0)
                    gather(j * 2 + 1, j, 1)
                for par in range(2):
                    pool.wait_ge(y_stored[par], 16 * (NTILE // 2) * (layer + 1))
                    for q in range(HALVES):
                        plan["tile", layer].written(pool, f"x{q}", NTILE - 2 + par)

                def gather_y(t, j, par, reuse=True):
                    if reuse:
                        pool.wait_ge(y_used, t + (TT * layer - 1))
                    fetch(slot_u[:, bass.ds(t, 1), :].rearrange("p o n -> p (o n)"), par, ys_d, t + (1 + rounds + NTILE))

                gather_y(0, 0, 0, False)
                gather_y(1, 0, 1, False)
                with pool.Fori(1, PAIRS) as j:
                    gather_y(j * 2, j, 0)
                    gather_y(j * 2 + 1, j, 1)
                gather_y(TT - 1, PAIRS, 0)

            power(0)
            with pool.Fori(0, B) as b:
                pool.wait_ge(ctx_hi, b + 1)
                nc.gpsimd.tensor_tensor(ctx_s[1], ctx_f, ctx_s[0], ALU.subtract).then_inc(ctx_split, 1)
            def first_split(layer):
                pool.wait_ge(w_hi, NBLK[0] * layer + 1)
                nc.gpsimd.tensor_scalar(wst, wst, WS, None, ALU.mult).then_inc(w_scaled, 1)
                pool.wait_ge(w_scaled, layer + 1)
                nc.gpsimd.tensor_tensor(wsp[0][1], wst, wsp[0][0], ALU.subtract).then_inc(w_split, 1)

            if stop >= 2:
                first_split(0)
                power(1)
                experts(0)
            if stop >= 3:
                power(2)
                for v in ZEROED:
                    nc.gpsimd.memset(v, 0.0).then_inc(aug_zero, 1)
                pool.wait_ge(aug_zero, len(ZEROED))
                for par in range(2):
                    nc.gpsimd.memset(q1[par][0][MASKED:MASKED + NMASK], FAR).then_inc(aug_zero, 1)
            if stop >= 3:
                pool.wait_ge(mask_loaded, 16 * 7)
                pool.wait_ge(rstd_ready, 3)
                pool.wait_ge(stage_used, 7)
                nc.gpsimd.tensor_scalar(mask16, mask8, -1.0, FAR, ALU.add, ALU.mult).then_inc(mask_ready, 1)
                pool.wait_ge(mask_ready, 1)
                pool.wait_ge(q1T_ready, 1)

                def context1(b):
                    if not isinstance(b, int) or b:
                        pool.wait_ge(q1_ready, b)
                    pool.wait_ge(ctx_hi, b + B + 1)
                    nc.gpsimd.tensor_tensor(ctx_s[1], ctx_f, ctx_s[0], ALU.subtract).then_inc(ctx_split, 1)

                def queries(b, par):
                    pool.wait_ge(ctx_split, b + B + 1)
                    for h in range(2):
                        for g in range(NG):
                            nc.gpsimd.tensor_copy(q1[par][h][0:HD].rearrange("p (m j) s -> p m j s", j=4)[:, :, g, :],
                                                  col(q1T[h], b, S)[HD * g:HD * (g + 1)]).then_inc(copied, 1)
                            pool.wait_ge(copied, b * (2 * NG) + (h * NG + g + 1))
                    nc.gpsimd.tensor_copy(k1[par][0][MASKED:MASKED + NMASK],
                                          row(mask16, b).unsqueeze(1).to_broadcast([NMASK, NG, SK])).then_inc(q1_ready, 1)

                context1(0)
                queries(0, 0)
                context1(1)
                queries(1, 1)
                with pool.Fori(0, B // 2 - 1) as j:
                    for par in range(2):
                        context1(j * 2 + (2 + par))
                        pool.wait_ge(exp_done, j * (2 * NH) + (par + 1) * NH)
                        queries(j * 2 + (2 + par), par)
            if stop >= 4:
                first_split(1)
                power(3)
                experts(1)

        @block.scalar
        def _(act):
            def layernorm_hi(n):
                def tile(t, j, par):
                    pl = plan["ln", n][par]
                    pl.written(act, "n", j)
                    nc.scalar.activation(col(nT[0], t), psum[:, par, :].rearrange("p (k t) -> p k t", k=KC),
                                         ACT.Copy).then_inc(hi_done.sem, 1)
                in_pairs(act, tile)

            def stage_split_hi(n, dst):
                act.wait_ge(stage_full[n], 16)
                nc.scalar.activation(dst[0][:], stage[n], ACT.Copy, scale=WS).then_inc(stage_hi, 1)

            act.wait_ge(phase, 1)
            for dst, src in CONSTS:
                act.dma_start(dst, src).then_inc(const_loaded, 16)
            for n, w in enumerate(("wkf", "wqf")):
                for j in range(4):
                    act.dma_start(bd_f[n][HD * j:HD * (j + 1), FD * j:FD * (j + 1)], a[w]).then_inc(const_loaded, 16)
            for n, dst in enumerate((wq, wk, wv, wo)):
                stage_split_hi(n, dst)
            act.wait_ge(const_loaded, 16 * N_CONST)
            nc.scalar.activation(gate, gate_in, ACT.Tanh).then_inc(gates_ready, 1)
            for n, dst in enumerate((bd_k, bd_q)):
                nc.scalar.activation(dst[0], bd_f[n], ACT.Copy).then_inc(stage_hi, 1)
            for n in range(2):
                nc.scalar.activation(route_w[n][0][:], route_s[n][:], ACT.Copy, scale=WS).then_inc(stage_hi, 1)

            layernorm_hi(0)

            act.wait_ge(small_split, 1)
            pl = plan["q", 0]
            with act.Fori(0, NCH) as c:
                act.wait_ge(phase, 2)
                for m in range(KC):
                    pl.written(act, f"q{m}", c)
                    nc.scalar.activation(qh[0][:, m, :], psum[:, m, 0:CW], ACT.Identity, bias=bq[:, m:m + 1]).then_inc(hi_done.sem, 1)
                act.wait_ge(stage_used, 4)
                for p in range(NPAIR):
                    pl.written(act, f"f{p}", c)
                    nc.scalar.activation(col(qf[0], c, CW)[:, p, :], psum[:, pl.bank(f"f{p}"), 0:CW], ACT.Relu).then_inc(hi_done.sem, 1)

            pl = plan["att", 0]

            def context(b):
                act.wait_ge(ctx_loaded, b * 16 + 16)
                nc.scalar.activation(ctx_s[0], ctx_f, ACT.Copy).then_inc(ctx_hi, 1)

            def keys(b):
                for m in range(KC):
                    pl.written(act, f"kT{m}", b)
                    nc.scalar.activation(kT[0][:, m, :], psum[:, m % 2, 0:SK], ACT.Identity, bias=bk[:, m:m + 1]).then_inc(hi_done.sem, 1)

            def split_kv(b):
                act.wait_ge(kv32_ready, b + 1)
                nc.scalar.activation(kvb[0], kv32, ACT.Copy).then_inc(kv_hi, 1)

            def att_columns(pl, b):
                pl.written(act, "oT", b)
                nc.scalar.activation(col(nT[0], b, S), psum[:, pl.bank("oT"), 0:KC * S].rearrange("p (k t) -> p k t", k=KC),
                                     ACT.Copy).then_inc(att_hi.sem, 1)

            context(0)
            keys(0)
            pl.written(act, "v2", 0)
            context(1)
            split_kv(0)
            with act.Fori(0, B - 2) as b:
                keys(b + 1)
                pl.written(act, "v2", b + 1)
                context(b + 2)
                split_kv(b + 1)
                att_columns(pl, b)
            keys(B - 1)
            split_kv(B - 1)
            att_columns(pl, B - 2)
            att_columns(pl, B - 1)

            def ffn(layer):
                first = NBLK[0] * layer
                act.wait_ge(w_loaded, first * 16 + 16)
                nc.scalar.activation(wsp[0][0], wst, ACT.Copy, scale=WS).then_inc(w_hi, 1)
                layernorm_hi(2 * layer + 1)

                def route_weights():
                    act.wait_ge(top_ready, layer + 1)
                    nc.scalar.activation(rt[:, 1, :], rt[:, 0, :], ACT.Exp, scale=1.0 / WS).then_inc(route_exp, 1)
                    if layer == 0:
                        nc.scalar.activation(rt[:, 5, :], rt[:, 4, :], ACT.Sigmoid, scale=1.0 / WS).then_inc(route_exp, 1)

                def attention_weights(n):
                    dst, src = ((wq[0], stage1[0]), (wo[0], stage1[1]), (wk[0][:, :, 0:2 * P], stage1[0][:, :, 0:2 * P]))[n]
                    act.wait_ge(stage_full[n % 2], 16 * (2 + n // 2))
                    nc.scalar.activation(dst, src, ACT.Copy, scale=WS).then_inc(stage_hi, 1)

                def split_hi(k, par, reuse=None):
                    act.wait_ge(w_loaded, (k + first) * 16 + 16)
                    if reuse is not None:
                        pl, n = of_block(layer, reuse)
                        pl.written(act, f"d{TT - 1}", n)
                    nc.scalar.activation(wsp[par][0], wst, ACT.Copy, scale=WS).then_inc(w_hi, 1)

                def units(k, par):
                    pl, n = of_block(layer, k)

                    def unit_hi(u):
                        s, (c, m) = u % 2, divmod(u, IH)
                        mn = IT[m][1]
                        act.wait_ge(h_ready, (k + first) * UNITS + u + 1)
                        nc.scalar.activation(hT[0][0:mn, m, c * CW:(c + 1) * CW], h32[s][0:mn, :], ACT.Copy).then_inc(h_hi, 1)

                    for u in range(UNITS):
                        s, m = u % 2, u % IH
                        mn = IT[m][1]
                        pl.written(act, f"g{u}", n)
                        bias = bias_gu[0:mn, k, m, 0:1] if layer else 0.0
                        nc.scalar.activation(sil[s][0:mn, :], psum[0:mn, 2 * s, 0:CW], ACT.Silu, bias=bias,
                                             scale=1.0 / WS).then_inc(sil_ready, 1)
                        if u:
                            unit_hi(u - 1)
                        if k == 0 and u == 2:
                            route_weights()
                        if stop >= 3 and layer == 0 and k == NBLK[0] - 1 and u in PREFETCH:
                            attention_weights(PREFETCH.index(u))
                    unit_hi(UNITS - 1)

                tl = plan["tile", layer]
                tile0 = NTILE * layer

                def piece_hi(par, staged, n):
                    p0, p1 = PIECE[n]
                    nc.scalar.activation(wsp[par][0][:, p0:p1], wstage[staged][:, p0:p1], ACT.Copy, scale=WS).then_inc(gw_hi, 1)

                def rows_hi(i):
                    for q in range(HALVES):
                        tl.written(act, f"x{q}", i)
                        nc.scalar.activation(xg[0][:, :, q * P:(q + 1) * P], psum[:, 6 + q, :].rearrange("p (k t) -> p k t", k=KC),
                                             ACT.Copy).then_inc(xg_hi, 1)

                def tile(i, j, par, following=True):
                    def unit_hi(m):
                        mn = IT[m][1]
                        act.wait_ge(gh_ready, i * IH + (tile0 * IH + m + 1))
                        nc.scalar.activation(hg[0][0:mn, m, :], hg32[m][0:mn, :], ACT.Copy).then_inc(gh_hi, 1)

                    piece_hi(1 - par, par, 2)
                    for m in range(IH):
                        mn = IT[m][1]
                        tl.written(act, f"u{m}", i)
                        nc.scalar.activation(silg[m][0:mn, :], psum[0:mn, m, 0:SLOTS], ACT.Silu, scale=1.0 / WS).then_inc(gsil_ready, 1)
                        if m:
                            unit_hi(m - 1)
                        if following and m == 0:
                            act.wait_ge(gw_loaded[1 - par], j * 16 + 16 * (1 + par + NTILE // 2 * layer))
                            piece_hi(par, 1 - par, 0)
                    unit_hi(IH - 1)
                    if following:
                        rows_hi(i + 1)
                        piece_hi(par, 1 - par, 1)
                    for q in range(HALVES):
                        tl.written(act, f"y{q}", i)
                        if q == 0 and (not isinstance(i, int) or i >= 2):
                            act.wait_ge(y_stored[par], j * 16 + 16 * (NTILE // 2) * layer)
                        ins = nc.scalar.activation(y[par][:, q, :], psum[:, 4 + q, :], ACT.Copy)
                        ins.then_inc(tl.free_sem(f"y{q}"), 1)
                    tl.free_after(act, "y0", i)
                    tl.free_after(act, "y1", i)
                    act.dma_start(ys_d[bass.ds(i * SLOTS, SLOTS), :].rearrange("(q p) d -> p q d", p=P), y[par]).then_inc(y_stored[par], 16)

                units(0, 0)
                act.wait_ge(gw_loaded[0], 16 + 16 * (NTILE // 2) * layer)
                for n in range(2):
                    piece_hi(1, 0, n)
                rows_hi(0)
                tile(0, 0, 0)
                tile(1, 0, 1)
                with act.Fori(1, NTILE // 2 - 1) as j:
                    tile(j * 2, j, 0)
                    tile(j * 2 + 1, j, 1)
                tile(NTILE - 2, NTILE // 2 - 1, 0)
                tile(NTILE - 1, NTILE // 2 - 1, 1, False)
                split_hi(1, 1)
                for k in range(1, NBLK[layer] - 1):
                    units(k, k % 2)
                    split_hi(k + 1, (k + 1) % 2, k - 1)
                units(NBLK[layer] - 1, 1)

            if stop >= 2:
                ffn(0)
            if stop >= 3:
                layernorm_hi(2)
                pl = plan["q", 1]
                with act.Fori(0, NCH) as c:
                    for m in range(KC):
                        pl.written(act, f"q{m}", c)
                        nc.scalar.activation(col(q1T[0], c, CW)[:, m, :], psum[:, m, 0:CW], ACT.Copy, scale=QS).then_inc(hi_done.sem, 1)
                pl = plan["att", 1]

                def context1(b):
                    act.wait_ge(ctx_loaded, b * 16 + (16 + 16 * B))
                    nc.scalar.activation(ctx_s[0], ctx_f, ACT.Copy).then_inc(ctx_hi, 1)

                def keys1(b, par, g):
                    if g == 0:
                        pl.written(act, "k", b)
                    nc.scalar.activation(k1[par][0][0:HD, g, :], psum[HD * g:HD * (g + 1), 7, 0:SK], ACT.Copy, scale=1.0 / WS).then_inc(hi_done.sem, 1)

                def values1(b, par):
                    pl.written(act, "v", b)
                    nc.scalar.activation(v1[par][:, 0:2, :], psum[:, 7, 0:2 * P].rearrange("p (t c) -> p t c", t=2), ACT.Copy, scale=1.0 / WS)
                    nc.scalar.activation(v1[par][0:KT[2][1], 2, :], psum[0:KT[2][1], 7, 2 * P:3 * P], ACT.Copy,
                                         scale=1.0 / WS).then_inc(psum_free[7].sem, 1)

                def heads(b, par, before, after):
                    for h in range(NH):
                        act.wait_ge(nmax_ready, b * NH + h + 1)
                        if h >= NS:
                            pl.written(act, f"pT{h - NS}", b)
                        nc.scalar.activation(pr[h % NS][0:S, 0:SK], psum[0:S, pl.bank(f"s{h}"), 0:SK], ACT.Exp,
                                             bias=nmax[0:S, h % NS:h % NS + 1], accum_out=den1[par][0:S, h:h + 1]).then_inc(exp_done, 1)
                        if before and h == 4:
                            att_columns(pl, b - 1)
                        if after and K_AT < h <= K_AT + NG:
                            keys1(b + 1, 1 - par, h - K_AT - 1)
                        if after and h == V_AT + 1:
                            values1(b + 1, 1 - par)
                        if after == 2 and h == V_AT + 2:
                            context1(b + 2)

                context1(0)
                act.wait_ge(aug_zero, N_ZERO)
                for g in range(NG):
                    keys1(0, 0, g)
                values1(0, 0)
                context1(1)
                heads(0, 0, False, 2)
                with act.Fori(0, B // 2 - 2) as j:
                    heads(j * 2 + 1, 1, True, 2)
                    heads(j * 2 + 2, 0, True, 2)
                heads(B - 3, 1, True, 2)
                heads(B - 2, 0, True, 1)
                heads(B - 1, 1, True, 0)
                att_columns(pl, B - 1)
            if stop >= 4:
                ffn(1)

        @block.vector
        def _(dve):
            chained = [0]

            def link(ins):
                chained[0] += 1
                ins.then_inc(dve_chain.sem, 1)
                dve.wait_ge(dve_chain.sem, chained[0])

            def end_phase():
                nc.vector.engine_nop().then_inc(phase, 1)

            for v in (x[:, TT - 1, :], bd_f[0], bd_f[1], route_s[0][:], route_s[1][:]):
                nc.vector.memset(v, 0.0)
            nc.vector.memset(mhalf[:], -0.5)
            for c in psum_free:
                nc.vector.engine_nop().then_inc(c.sem, 1)
            link(nc.vector.memset(shared[:], 1.0))
            end_phase()

            def stage_split_low(n, dst):
                dve.wait_ge(stage_hi, n + 1)
                nc.vector.scalar_tensor_tensor(out=dst[1][:], in0=stage[n], scalar=WS, in1=dst[0][:],
                                               op0=ALU.mult, op1=ALU.subtract).then_inc(stage_used, 1)

            def layernorm(n):
                if n == 0:
                    for t in range(TT):
                        if t == 0:
                            dve.wait_ge(x_loaded[0], 16)
                        elif t == TT // 2:
                            dve.wait_ge(x_loaded[1], 32)
                        ins = nc.vector.bn_stats(stats[:, t, :], x[:, t, :])
                    link(ins)
                for t in range(TT):
                    ins = nc.vector.bn_aggr(mv[:, t, :], stats[:, t, :])
                link(ins)
                nc.vector.tensor_scalar(rstd[:], mv[:, :, 1:2].rearrange("p t o -> p (t o)"), EPS_LN, None, ALU.add).then_inc(stats_ready, 1)
                if n == 0:
                    stage_split_low(0, wq)
                dve.wait_ge(rstd_ready, n + 1)

                def normalise(t, j, par, reuse=True):
                    if reuse:
                        plan["ln", n][par].written(dve, "n", j - 1)
                        if n % 2:
                            dve.wait_ge(xn_stored[par], j * 16 + 16 * (PAIRS + 1 - par) * (n // 2))
                    nc.vector.tensor_scalar(norm[par][:], row(x, t), mv[:, bass.ds(t, 1), 0:1].rearrange("p o s -> p (o s)"),
                                            at1(rstd, t), ALU.subtract, ALU.mult).then_inc(norm_ready.sem, 1)

                def low(t, j, par):
                    dve.wait_ge(hi_done.sem, hi["ln", n].at(t))
                    nc.vector.tensor_tensor(col(nT[1], t), psum[:, par, :].rearrange("p (k t) -> p k t", k=KC),
                                            col(nT[0], t), ALU.subtract).then_inc(psum_free[par].sem, 1)

                normalise(0, 0, 0, False)
                normalise(1, 0, 1, False)
                with dve.Fori(0, PAIRS - 1) as j:
                    normalise(j * 2 + 2, j + 1, 0)
                    low(j * 2, j, 0)
                    normalise(j * 2 + 3, j + 1, 1)
                    low(j * 2 + 1, j, 1)
                normalise(TT - 1, PAIRS, 0)
                for t in range(TT - 3, TT):
                    low(t, t // 2, t % 2)
                end_phase()

            layernorm(0)
            for n, dst in enumerate((wk, wv, wo)):
                stage_split_low(n + 1, dst)
            dve.wait_ge(const_loaded, 16 * N_CONST)
            for v in (bq, bk, bias_v[:]):
                link(nc.vector.tensor_scalar(v, v, WS, None, ALU.mult))
            link(nc.vector.tensor_scalar(mask_c[:], mask_c[:], 1.0 / WS, None, ALU.mult))
            dve.wait_ge(gates_ready, 1)
            link(nc.vector.tensor_scalar(gate_s[:, 0:2], gate[:, 0:2], 1.0 / WS, None, ALU.mult))
            link(nc.vector.tensor_scalar(gate_s[:, 2:4], gate[:, 2:4], 1.0 / (WS * WS), None, ALU.mult))
            dve.wait_ge(stage_hi, 8)
            for n, dst in enumerate((bd_k, bd_q)):
                nc.vector.tensor_tensor(dst[1], bd_f[n], dst[0], ALU.subtract)
            for n in range(2):
                ins = nc.vector.scalar_tensor_tensor(out=route_w[n][1][:], in0=route_s[n][:], scalar=WS, in1=route_w[n][0][:],
                                                     op0=ALU.mult, op1=ALU.subtract)
            ins.then_inc(small_split, 1)
            nc.vector.memset(kv32, 0.0)

            pl = plan["q", 0]
            with dve.Fori(0, NCH) as c:
                for m in range(KC):
                    dve.wait_ge(hi_done.sem, hi["q", 0].at(c, m))
                    nc.vector.scalar_tensor_tensor(out=qh[1][:, m, :], in0=psum[:, m, 0:CW], scalar=bq[:, m:m + 1],
                                                   in1=qh[0][:, m, :], op0=ALU.add, op1=ALU.subtract).then_inc(psum_free[m].sem, 1)
                for p in range(NPAIR):
                    dve.wait_ge(hi_done.sem, hi["q", 0].at(c, KC + p))
                    nc.vector.scalar_tensor_tensor(out=col(qf[1], c, CW)[:, p, :], in0=psum[:, pl.bank(f"f{p}"), 0:CW], scalar=0.0,
                                                   in1=col(qf[0], c, CW)[:, p, :], op0=ALU.max, op1=ALU.subtract).then_inc(pl.free_sem(f"f{p}"), 1)
            nc.vector.memset(va, WS).then_inc(q_split, 1)
            dve.wait_ge(q_split, 1)

            pl = plan["att", 0]

            def keys(b):
                for m in range(KC):
                    dve.wait_ge(hi_done.sem, hi["kT", 0].at(b, m))
                    nc.vector.scalar_tensor_tensor(out=kT[1][:, m, :], in0=psum[:, m % 2, 0:SK], scalar=bk[:, m:m + 1],
                                                   in1=kT[0][:, m, :], op0=ALU.add, op1=ALU.subtract).then_inc(psum_free[m % 2].sem, 1)

            def values(b):
                for t, (t0, tn) in enumerate(KT):
                    pl.written(dve, f"v{t}", b)
                    nc.vector.tensor_tensor(va[0:tn, t, :, 0:HD], psum[0:tn, pl.bank(f"v{t}"), :].rearrange("p (h c) -> p h c", h=NH),
                                            bias_v[0:tn, :].rearrange("p (h c) -> p h c", h=NH), ALU.add).then_inc(pl.free_sem(f"v{t}"), 1)

            def features(b):
                for t, (t0, tn) in enumerate(KT):
                    for half in range(2):
                        pl.written(dve, f"kf{t}{half}", b)
                        nc.vector.tensor_scalar(kf[0:tn, t, half * 512:(half + 1) * 512], psum[0:tn, pl.bank(f"kf{t}{half}"), :], 0.0,
                                                mask_c[0:tn, bass.ds(b, 1), t:t + 1].rearrange("p a c -> p (a c)"),
                                                ALU.max, ALU.mult).then_inc(pl.free_sem(f"kf{t}{half}"), 1)

            def diagonal(b):
                for q in range(2):
                    pl.written(dve, f"kv{q}", b)
                    src = psum[:, pl.bank(f"kv{q}"), 0:4 * 2 * VW].rearrange("p (a c) -> p a c", a=4)
                    nc.vector.tensor_scalar(kv32[0:64, 4 * q:4 * q + 4, 0:VW], src[0:64, :, 0:VW], 1.0 / KVS, None, ALU.mult)
                    nc.vector.tensor_scalar(kv32[64:128, 4 * q:4 * q + 4, VW:2 * VW], src[64:128, :, VW:2 * VW],
                                            1.0 / KVS, None, ALU.mult).then_inc(pl.free_sem(f"kv{q}"), 1)
                nc.vector.engine_nop().then_inc(kv32_ready, 1)
                dve.wait_ge(kv_hi, b + 1)
                nc.vector.tensor_tensor(kvb[1], kv32, kvb[0], ALU.subtract).then_inc(kv_ready, 1)

            def quotient(b, reuse=None):
                for q in range(2):
                    pl.written(dve, f"o{q}", b)
                    src = psum[0:S, 6 + q, 0:8 * VW].rearrange("p (h c) -> p h c", h=8)
                    ins = nc.vector.tensor_scalar(den[0:S, 8 * q:8 * q + 8], src[:, :, HD:VW].rearrange("p h c -> p (h c)"),
                                                  EPS_DEN * WS * WS * WS / (KVS * WS), None, ALU.add)
                ins.then_inc(den_ready, 1)
                dve.wait_ge(den_ready, b + 1)
                nc.vector.reciprocal(rden[0:S, :], den[0:S, :]).then_inc(rden_ready, 1)
                dve.wait_ge(rden_ready, b + 1)
                for q in range(2):
                    src = psum[0:S, 6 + q, 0:8 * VW].rearrange("p (h c) -> p h c", h=8)
                    ins = nc.vector.tensor_tensor(norm[0][0:S, 256 * q:256 * (q + 1)].rearrange("p (h c) -> p h c", h=8), src[:, :, 0:HD],
                                                  rden[0:S, 8 * q:8 * q + 8].unsqueeze(2).to_broadcast([S, 8, HD]), ALU.mult)
                    ins.then_inc(psum_free[6 + q].sem, 1)
                nc.vector.engine_nop().then_inc(norm_ready.sem, 1)

            def att_columns(layer, pl, b):
                dve.wait_ge(att_hi.sem, hi["oT", layer].at(b))
                nc.vector.tensor_tensor(col(nT[1], b, S), psum[:, pl.bank("oT"), 0:KC * S].rearrange("p (k t) -> p k t", k=KC),
                                        col(nT[0], b, S), ALU.subtract).then_inc(pl.free_sem("oT"), 1)

            keys(0)
            values(0)
            features(0)
            diagonal(0)
            with dve.Fori(0, B - 1) as b:
                keys(b + 1)
                values(b + 1)
                features(b + 1)
                quotient(b)
                diagonal(b + 1)
                att_columns(0, pl, b)
            quotient(B - 1)
            att_columns(0, pl, B - 1)

            def project_out(layer):
                if layer == 0:
                    link(nc.vector.scalar_tensor_tensor(out=x[:], in0=bias_o[:].unsqueeze(1).to_broadcast([P, TT, D]), scalar=gate[:, 0:1],
                                                        in1=x[:], op0=ALU.mult, op1=ALU.add))
                nc.vector.engine_nop().then_inc(x_ready, 1)

                def tile(t, j, par):
                    pl = plan["out", layer][par]
                    pl.written(dve, "w", j)
                    nc.vector.scalar_tensor_tensor(out=row(x, t), in0=psum[:, par, :], scalar=gate_s[:, layer:layer + 1], in1=row(x, t),
                                                   op0=ALU.mult, op1=ALU.add).then_inc(psum_free[par].sem, 1)

                def measure(t, j, par):
                    plan["out", layer][par].free_after(dve, "w", j)
                    nc.vector.bn_stats(stats[:, bass.ds(t, 1), :].rearrange("p o s -> p (o s)"), row(x, t))

                tile(0, 0, 0)
                tile(1, 0, 1)
                measure(0, 0, 0)
                with dve.Fori(1, PAIRS) as j:
                    tile(j * 2, j, 0)
                    measure(j * 2 - 1, j - 1, 1)
                    tile(j * 2 + 1, j, 1)
                    measure(j * 2, j, 0)
                tile(TT - 1, PAIRS, 0)
                measure(TT - 2, PAIRS - 1, 1)
                measure(TT - 1, PAIRS, 0)
                link(nc.vector.engine_nop())
                end_phase()

            project_out(0)

            def ffn(layer):
                layernorm(2 * layer + 1)
                first = NBLK[0] * layer
                sl = plan["slots", layer]
                ranks = psum[:, 6, 0:TT * E].rearrange("p (t e) -> p t e", t=TT)
                number = psum[:, 6, TT * E:(TT + 1) * E]

                def pick(v, n):
                    return v[:, :, n:n + 1].rearrange("p t o -> p (t o)")

                def two_largest():
                    plan["route", layer].written(dve, "l")
                    link(nc.vector.tensor_copy(logit[:], psum[:, 7, 0:TT * 16].rearrange("p (t e) -> p t e", t=TT)))
                    nc.vector.engine_nop().then_inc(psum_free[7].sem, 1)
                    for t in range(TT):
                        ins = nc.vector.max(top[:, t, :], logit[:, t, 0:E])
                    link(ins)
                    for t in range(TT):
                        ins = nc.vector.max_index(topi[:, t, :], top[:, t, :], logit[:, t, 0:E])
                    link(ins)

                def one_hot_rows():
                    if layer == 0:
                        link(nc.vector.tensor_copy(rt[:, 4, :], pick(logit, E)))
                    nc.vector.tensor_tensor(rt[:, 0, :], pick(top, 1), pick(top, 0), ALU.subtract).then_inc(top_ready, 1)
                    nc.vector.tensor_copy(rt[:, 6, :], pick(topi, 0))
                    link(nc.vector.tensor_copy(rt[:, 7, :], pick(topi, 1)))
                    ids = iota[:, 0:E].unsqueeze(1).to_broadcast([P, TT, E])
                    for n in range(2):
                        ins = nc.vector.tensor_tensor(oh[:, n], ids, rt[:, 6 + n, :].unsqueeze(2).to_broadcast([P, TT, E]), ALU.is_equal)
                    link(ins)
                    link(nc.vector.memset(oh[LAST:P, :, TT - 1, :], 0.0))
                    nc.vector.tensor_tensor(oh_sum[:], oh[:, 0], oh[:, 1], ALU.add).then_inc(picks_ready, 1)

                def weights():
                    dve.wait_ge(route_exp, (2, 3)[layer])
                    link(nc.vector.tensor_scalar(rt[:, 2, :], rt[:, 1, :], 1.0, None, ALU.add))
                    link(nc.vector.reciprocal(rt[:, 2, :], rt[:, 2, :]))
                    link(nc.vector.tensor_tensor(rt[:, 3, :], rt[:, 1, :], rt[:, 2, :], ALU.mult))
                    link(nc.vector.tensor_scalar(rt[:, 2:4, :], rt[:, 2:4, :], gate_s[:, 2 + layer:3 + layer], None, ALU.mult))
                    if layer == 0:
                        link(nc.vector.tensor_scalar(shared[:], rt[:, 5, :], gate_s[:, 2:3], None, ALU.mult))
                    else:
                        link(nc.vector.memset(shared[:], 1.0))
                        link(nc.vector.tensor_scalar(shared[:], shared[:], gate_s[:, 3:4], None, ALU.mult))

                def tiles_of_experts():
                    sl.written(dve, "r")
                    link(nc.vector.tensor_scalar(tiles[:], number, 0.0, None, ALU.is_gt))
                    for k in range(1, MAX_TILES):
                        link(nc.vector.scalar_tensor_tensor(out=tiles[:], in0=number, scalar=float(SLOTS * k), in1=tiles[:], op0=ALU.is_gt, op1=ALU.add))
                    link(nc.vector.tensor_copy(ends[:], tiles[:]))
                    for e in range(1, E):
                        link(nc.vector.tensor_tensor(ends[:, e:e + 1], ends[:, e - 1:e], ends[:, e:e + 1], ALU.add))

                def expert_of_tiles():
                    link(nc.vector.tensor_tensor(ge_tile, iota[:, 0:NTILE].unsqueeze(2).to_broadcast([P, NTILE, E]),
                                                 ends[:].unsqueeze(1).to_broadcast([P, NTILE, E]), ALU.is_ge))
                    link(nc.vector.reduce_sum(expert[:], ge_tile, AX_X))
                    nc.vector.tensor_scalar(expert_u[:], expert[:], float(E - 1), None, ALU.min).then_inc(experts_ready, 1)

                def slots_of_choices():
                    link(nc.vector.tensor_tensor(tiles[:], ends[:], tiles[:], ALU.subtract))
                    link(nc.vector.scalar_tensor_tensor(out=slot_all, in0=tiles[:].unsqueeze(1).to_broadcast([P, TT, E]), scalar=float(SLOTS),
                                                        in1=ranks, op0=ALU.mult, op1=ALU.add))
                    nc.vector.engine_nop().then_inc(psum_free[6].sem, 1)
                    for n in range(2):
                        ins = nc.vector.tensor_tensor(chosen[:, n], oh[:, n], slot_all, ALU.mult)
                    link(ins)
                    link(nc.vector.reduce_sum(slot[:].rearrange("p (n t) -> p n t", n=2), chosen, AX_X))
                    nc.vector.tensor_copy(slot_u[:].rearrange("p t n -> p n t"), slot[:].rearrange("p (n t) -> p n t", n=2))
                    link(nc.vector.tensor_scalar(low[:], slot[:], 1.0 / P, None, ALU.mult))

                def high_tables():
                    link(nc.vector.tensor_tensor(ge, low[:].unsqueeze(2).to_broadcast([P, NC2, NHALF + 1]),
                                                 iota[:, 0:NHALF + 1].unsqueeze(1).to_broadcast([P, NC2, NHALF + 1]), ALU.is_ge))

                def high_rows():
                    nc.vector.tensor_tensor(diff, ge[:, :, 0:NHALF], ge[:, :, 1:NHALF + 1], ALU.subtract)
                    link(nc.vector.reduce_sum(low[:], ge[:, :, 1:NHALF + 1], AX_X))

                def low_number():
                    nc.vector.tensor_tensor(oh_high, diff, token[:].unsqueeze(2).to_broadcast([P, NC2, NHALF]), ALU.mult)
                    link(nc.vector.scalar_tensor_tensor(out=low[:], in0=low[:], scalar=-float(P), in1=slot[:], op0=ALU.mult, op1=ALU.add))

                def low_rows(n):
                    part = slice(n * TT, (n + 1) * TT)
                    ins = nc.vector.tensor_tensor(oh_low[:, part, :], iota[:].unsqueeze(1).to_broadcast([P, TT, P]),
                                                  low[:, part].unsqueeze(2).to_broadcast([P, TT, P]), ALU.is_equal)
                    if n == 1:
                        ins.then_inc(tables_ready, 1)

                def slots_done():
                    sl.written(dve, "i")
                    nc.vector.tensor_copy(source[:], psum[:, 5, 0:NHALF]).then_inc(psum_free[5].sem, 1)
                    nc.vector.engine_nop().then_inc(slots_ready, 1)

                def plan_step(u):
                    if u == 0:
                        two_largest()
                    elif u == 1:
                        one_hot_rows()
                    elif u == RANKS_AT:
                        weights()
                    elif u == RANKS_AT + 1:
                        tiles_of_experts()
                    elif u == RANKS_AT + 2:
                        expert_of_tiles()
                        slots_of_choices()
                    elif u == RANKS_AT + 3:
                        high_tables()
                    elif u == RANKS_AT + 4:
                        high_rows()
                    elif u == RANKS_AT + 5:
                        low_number()
                    elif u == RANKS_AT + 6:
                        low_rows(0)
                    elif u == RANKS_AT + 7:
                        low_rows(1)

                def add_experts(t):
                    par = t % 2
                    done = NTILE // 2 * (layer + 1) + t // 2 + 1 + (PAIRS + 1 - par) * layer
                    dve.wait_ge(gathered[par], 32 * done)
                    for c in range(2):
                        link(nc.vector.scalar_tensor_tensor(out=x[:, t, :], in0=rows[par][:, c, :], scalar=rt[:, 2 + c, t:t + 1],
                                                            in1=x[:, t, :], op0=ALU.mult, op1=ALU.add))
                    nc.vector.engine_nop().then_inc(y_used, 1)

                def attention_weights(n):
                    part = slice(0, (D, D, 2 * P)[n])
                    dst, src = ((wq, stage1[0]), (wo, stage1[1]), (wk, stage1[0]))[n]
                    dve.wait_ge(stage_hi, 9 + n)
                    nc.vector.scalar_tensor_tensor(out=dst[1][:, :, part], in0=src[:, :, part], scalar=WS, in1=dst[0][:, :, part],
                                                   op0=ALU.mult, op1=ALU.subtract).then_inc(stage_used, 1)

                last = NBLK[layer] - 1

                def split_low(k, par):
                    dve.wait_ge(w_hi, k + first + 1)
                    nc.vector.scalar_tensor_tensor(out=wsp[par][1], in0=wst, scalar=WS, in1=wsp[par][0],
                                                   op0=ALU.mult, op1=ALU.subtract).then_inc(w_split, 1)

                def units(k, par):
                    pl, n = of_block(layer, k)

                    def unit_low(u):
                        s, (c, m) = u % 2, divmod(u, IH)
                        mn = IT[m][1]
                        dve.wait_ge(h_hi, (k + first) * UNITS + u + 1)
                        nc.vector.tensor_tensor(hT[1][0:mn, m, c * CW:(c + 1) * CW], h32[s][0:mn, :],
                                                hT[0][0:mn, m, c * CW:(c + 1) * CW], ALU.subtract).then_inc(hT_ready, 1)

                    for u in range(UNITS):
                        s, m = u % 2, u % IH
                        mn = IT[m][1]
                        pl.written(dve, f"u{u}", n)
                        dve.wait_ge(sil_ready, (k + first) * UNITS + u + 1)
                        if u >= 2 or k > 0:
                            dve.wait_ge(hT_ready, (k + first) * UNITS + u - 1)
                        up = psum[0:mn, 2 * s + 1, 0:CW]
                        if layer:
                            ins = nc.vector.scalar_tensor_tensor(out=h32[s][0:mn, :], in0=up,
                                                                 scalar=bias_gu[0:mn, k, m, 1:2],
                                                                 in1=sil[s][0:mn, :], op0=ALU.add, op1=ALU.mult)
                        else:
                            ins = nc.vector.tensor_tensor(h32[s][0:mn, :], up, sil[s][0:mn, :], ALU.mult)
                        ins.then_inc(h_ready, 1)
                        if u:
                            unit_low(u - 1)
                        if k == 0:
                            plan_step(u)
                        if k == last and u >= 2:
                            for t in (u - 2,) if u < 9 else (2 * u - 11, 2 * u - 10):
                                add_experts(t)
                        if stop >= 3 and layer == 0 and k == last and u in PREFETCH:
                            attention_weights(PREFETCH.index(u))
                    unit_low(UNITS - 1)

                def combine(k):
                    pl, n = of_block(layer, k)
                    for t in range(TT):
                        pl.written(dve, f"d{t}", n)
                        nc.vector.scalar_tensor_tensor(out=x[:, t, :], in0=psum[:, 4 + t % 4, :],
                                                       scalar=shared[:, t:t + 1], in1=x[:, t, :],
                                                       op0=ALU.mult, op1=ALU.add).then_inc(psum_free[4 + t % 4].sem, 1)
                        if layer == 0 and k == last and t:
                            pl.free_after(dve, f"d{t - 1}", n)
                            nc.vector.bn_stats(stats[:, t - 1, :], x[:, t - 1, :])
                    if layer == 0 and k == last:
                        pl.free_after(dve, f"d{TT - 1}", n)
                        nc.vector.bn_stats(stats[:, TT - 1, :], x[:, TT - 1, :])

                tl = plan["tile", layer]
                tile0 = NTILE * layer

                def piece_low(i, par, staged, n):
                    p0, p1 = PIECE[n]
                    dve.wait_ge(gw_hi, i * len(PIECE) + (tile0 * len(PIECE) + n + 1))
                    nc.vector.scalar_tensor_tensor(out=wsp[par][1][:, p0:p1], in0=wstage[staged][:, p0:p1], scalar=WS,
                                                   in1=wsp[par][0][:, p0:p1], op0=ALU.mult, op1=ALU.subtract).then_inc(gw_split, 1)

                def rows_low(i):
                    for q in range(HALVES):
                        dve.wait_ge(xg_hi, i * HALVES + (tile0 * HALVES + q + 1))
                        nc.vector.tensor_tensor(xg[1][:, :, q * P:(q + 1) * P], psum[:, 6 + q, :].rearrange("p (k t) -> p k t", k=KC),
                                                xg[0][:, :, q * P:(q + 1) * P], ALU.subtract).then_inc(psum_free[6 + q].sem, 1)

                def tile(i, j, par, following=True):
                    def unit_low(m):
                        mn = IT[m][1]
                        dve.wait_ge(gh_hi, i * IH + (tile0 * IH + m + 1))
                        nc.vector.tensor_tensor(hg[1][0:mn, m, :], hg32[m][0:mn, :], hg[0][0:mn, m, :], ALU.subtract).then_inc(gh_split, 1)

                    piece_low(i, 1 - par, par, 2)
                    for m in range(IH):
                        mn = IT[m][1]
                        dve.wait_ge(gsil_ready, i * IH + (tile0 * IH + m + 1))
                        if not isinstance(i, int) or i or layer:
                            dve.wait_ge(gh_split, i * IH + (tile0 * IH + m - IH + 1))
                        nc.vector.tensor_tensor(hg32[m][0:mn, :], psum[0:mn, m, SLOTS:2 * SLOTS], silg[m][0:mn, :], ALU.mult).then_inc(gh_ready, 1)
                        if m:
                            unit_low(m - 1)
                        if following and m == 0:
                            piece_low(i + 1, par, 1 - par, 0)
                    unit_low(IH - 1)
                    if following:
                        rows_low(i + 1)
                        piece_low(i + 1, par, 1 - par, 1)

                units(0, 0)
                slots_done()
                for n in range(2):
                    piece_low(0, 1, 0, n)
                if layer:
                    link(nc.vector.scalar_tensor_tensor(out=x[:], in0=bias_d[:].unsqueeze(1).to_broadcast([P, TT, D]), scalar=gate[:, 3:4],
                                                        in1=x[:], op0=ALU.mult, op1=ALU.add))
                combine(0)
                rows_low(0)
                tile(0, 0, 0)
                tile(1, 0, 1)
                with dve.Fori(1, NTILE // 2 - 1) as j:
                    tile(j * 2, j, 0)
                    tile(j * 2 + 1, j, 1)
                tile(NTILE - 2, NTILE // 2 - 1, 0)
                tile(NTILE - 1, NTILE // 2 - 1, 1, False)
                split_low(1, 1)
                for k in range(1, NBLK[layer] - 1):
                    units(k, k % 2)
                    split_low(k + 1, (k + 1) % 2)
                    combine(k)
                units(NBLK[layer] - 1, 1)
                combine(NBLK[layer] - 1)
                link(nc.vector.engine_nop())
                end_phase()

            if stop >= 2:
                ffn(0)
            if stop >= 3:
                link(nc.vector.tensor_scalar(bias_gu[:, :, :, 1:2], bias_gu[:, :, :, 1:2], WS, None, ALU.mult))
                layernorm(2)
                pl = plan["q", 1]
                with dve.Fori(0, NCH) as c:
                    for m in range(KC):
                        dve.wait_ge(hi_done.sem, hi["q", 1].at(c, m))
                        nc.vector.scalar_tensor_tensor(out=col(q1T[1], c, CW)[:, m, :], in0=psum[:, m, 0:CW], scalar=QS,
                                                       in1=col(q1T[0], c, CW)[:, m, :], op0=ALU.mult, op1=ALU.subtract).then_inc(psum_free[m].sem, 1)
                nc.vector.engine_nop().then_inc(q1T_ready, 1)
                pl = plan["att", 1]

                def keys1(b, par, g):
                    dve.wait_ge(hi_done.sem, hi["kT", 1].at(b, g))
                    ins = nc.vector.scalar_tensor_tensor(out=k1[par][1][0:HD, g, :], in0=psum[HD * g:HD * (g + 1), 7, 0:SK], scalar=1.0 / WS,
                                                         in1=k1[par][0][0:HD, g, :], op0=ALU.mult, op1=ALU.subtract)
                    if g == NG - 1:
                        ins.then_inc(psum_free[7].sem, 1)

                def quotient1(b, par):
                    dve.wait_ge(exp_done, b * NH + NH)
                    nc.vector.reciprocal(rden[0:S, :], den1[par][0:S, :]).then_inc(rden_ready, 1)
                    dve.wait_ge(rden_ready, b + B + 1)
                    pl.written(dve, "o", b)
                    nc.vector.tensor_tensor(norm[0][0:S, :].rearrange("p (h c) -> p h c", h=NH), psum[0:S, 4, :].rearrange("p (h c) -> p h c", h=NH),
                                            rden[0:S, :].unsqueeze(2).to_broadcast([S, NH, HD]), ALU.mult).then_inc(norm_ready.sem, 1)

                def heads(b, par, before, after):
                    def transposed(h):
                        pl.written(dve, f"pT{h}", b)
                        nc.vector.tensor_copy(pT[h % 2], psum[:, pl.bank(f"pT{h}"), 0:3 * S].rearrange("p (t s) -> p t s", t=3)).then_inc(pT_ready, 1)

                    for h in range(NH):
                        pl.written(dve, f"s{h}", b)
                        if h >= NS:
                            dve.wait_ge(exp_done, b * NH + h + 1 - NS)
                        elif before:
                            dve.wait_ge(exp_done, b * NH + h + 1 - NS)
                        nc.vector.reduce_max(nmax[0:S, h % NS:h % NS + 1], psum[0:S, h % NS, 0:SK], AX_X, negate=True).then_inc(nmax_ready, 1)
                        if h >= 2:
                            transposed(h - 2)
                        if before and h == 1:
                            quotient1(b - 1, 1 - par)
                        if before and h == 5:
                            att_columns(1, pl, b - 1)
                        if after and K_AT + 1 < h <= K_AT + 1 + NG:
                            keys1(b + 1, 1 - par, h - K_AT - 2)
                    transposed(NH - 2)
                    transposed(NH - 1)

                dve.wait_ge(aug_zero, N_ZERO)
                for g in range(NG):
                    keys1(0, 0, g)
                heads(0, 0, False, True)
                with dve.Fori(0, B // 2 - 1) as j:
                    heads(j * 2 + 1, 1, True, True)
                    heads(j * 2 + 2, 0, True, True)
                heads(B - 1, 1, True, False)
                quotient1(B - 1, 1)
                att_columns(1, pl, B - 1)
                project_out(1)
            if stop >= 4:
                ffn(1)

        @block.tensor
        def _(pe):
            def product(dst, stationary, moving, last=None):
                n, total = 0, 3 * KC
                for sh, mh in PASSES:
                    for k in range(KC):
                        ins = nc.tensor.matmul(dst, stationary(sh, k), moving(mh, k), start=n == 0, stop=n == total - 1)
                        n += 1
                if last is not None:
                    ins.then_inc(last, 1)
                return ins

            def transposes(n):
                def tile(t, j, par):
                    pl = plan["ln", n][par]
                    pe.wait_ge(norm_ready.sem, norms["ln", n].at(t))
                    pl.free(pe, "n", j)
                    for k in range(KC):
                        ins = nc.tensor.transpose(psum[:, par, k * P:(k + 1) * P], norm[par][:, k * P:(k + 1) * P], ident[:])
                    ins.then_inc(psum_full[par].sem, 1)
                in_pairs(pe, tile)

            def att_transposes(layer, pl, b):
                pe.wait_ge(norm_ready.sem, norms["att", layer].at(b))
                pl.free(pe, "oT", b)
                for k in range(KC):
                    ins = nc.tensor.transpose(psum[:, pl.bank("oT"), k * S:(k + 1) * S], norm[0][0:S, k * P:(k + 1) * P], ident[0:S, 0:S])
                ins.then_inc(pl.full_sem("oT"), 1)

            def project_out(layer):
                pe.wait_ge(x_ready, layer + 1)

                def tile(t, j, par):
                    pl = plan["out", layer][par]
                    pl.free(pe, "w", j)
                    product(psum[:, par, :], lambda h, k: col(nT[h], t)[:, k, :], lambda h, k: wo[h][:, k, :], psum_full[par].sem)
                in_pairs(pe, tile)

            pe.wait_ge(const_loaded, 16 * N_CONST)
            transposes(0)
            pe.wait_ge(stage_used, 1)
            pe.wait_ge(phase, 2)
            pl = plan["q", 0]
            with pe.Fori(0, NCH) as c:
                for m in range(KC):
                    pl.free(pe, f"q{m}", c)
                    product(psum[:, m, 0:CW], lambda h, k: wq[h][:, k, m * P:(m + 1) * P], lambda h, k: col(nT[h], c, CW)[:, k, :],
                            psum_full[m].sem)
                for p in range(NPAIR):
                    m, half = divmod(p, 2)
                    pl.free(pe, f"f{p}", c)
                    if half == 0:
                        pe.wait_ge(psum_free[m].sem, pl.r[m].before(c + 1))
                    for n, (sh, mh) in enumerate(PASSES):
                        ins = nc.tensor.matmul(psum[:, 4 + p % 4, 0:CW], bd_q[sh][:, half * P:(half + 1) * P], qh[mh][:, m, :],
                                               start=n == 0, stop=n == 2)
                    ins.then_inc(pl.full_sem(f"f{p}"), 1)

            pl = plan["att", 0]

            def keys(b):
                pe.wait_ge(ctx_split, b + 1)
                for m in range(KC):
                    pl.free(pe, f"kT{m}", b)
                    product(psum[:, m % 2, 0:SK], lambda h, k: wk[h][:, k, m * P:(m + 1) * P], lambda h, k: ctx_s[h][:, k, :],
                            psum_full[m % 2].sem)

            def values(b):
                for t, (t0, tn) in enumerate(KT):
                    pl.free(pe, f"v{t}", b)
                    product(psum[0:tn, pl.bank(f"v{t}"), :], lambda h, k: ctx_s[h][:, k, t0:t0 + tn], lambda h, k: wv[h][:, k, :],
                            pl.full_sem(f"v{t}"))

            def features(b):
                pl.free_after(pe, f"kT{KC - 2}", b)
                pl.free_after(pe, f"kT{KC - 1}", b)
                for t, (t0, tn) in enumerate(KT):
                    for half in range(2):
                        pl.free(pe, f"kf{t}{half}", b)
                        for m in (2 * half, 2 * half + 1):
                            for n, (sh, mh) in enumerate(PASSES):
                                ins = nc.tensor.matmul(psum[0:tn, pl.bank(f"kf{t}{half}"), (m % 2) * 256:(m % 2 + 1) * 256], kT[sh][:, m, t0:t0 + tn],
                                                       bd_k[mh], start=n == 0, stop=n == 2)
                        ins.then_inc(pl.full_sem(f"kf{t}{half}"), 1)

            def sums(b):
                for bank in range(4):
                    pe.wait_ge(psum_free[bank].sem, pl.r[bank].before(b + 1))
                for q in range(2):
                    pl.free(pe, f"kv{q}", b)
                    for p in range(4 * q, 4 * q + 4):
                        for t, (t0, tn) in enumerate(KT):
                            ins = nc.tensor.matmul(psum[:, 4 + q, (p % 4) * 2 * VW:(p % 4 + 1) * 2 * VW], kf[0:tn, t, p * P:(p + 1) * P],
                                                   va[0:tn, t, 2 * p:2 * p + 2, :].rearrange("p h c -> p (h c)"),
                                                   start=t == 0, stop=t == len(KT) - 1)
                    ins.then_inc(pl.full_sem(f"kv{q}"), 1)

            def outputs(b):
                pe.wait_ge(kv_ready, b + 1)
                for q in range(2):
                    pl.free(pe, f"o{q}", b)
                    for p in range(4 * q, 4 * q + 4):
                        for n, (sh, mh) in enumerate(PASSES):
                            ins = nc.tensor.matmul(psum[0:S, 6 + q, (p % 4) * 2 * VW:(p % 4 + 1) * 2 * VW], col(qf[sh], b, S)[:, p, :],
                                                   kvb[mh][:, p, :], start=n == 0, stop=n == 2)
                    ins.then_inc(psum_full[6 + q].sem, 1)

            pe.wait_ge(stage_used, 4)
            for bank in (4, 5, 6, 7):
                pe.wait_ge(psum_free[bank].sem, plan["q", 0].r[bank].before(NCH))
            pe.wait_ge(q_split, 1)
            keys(0)
            values(0)
            features(0)
            sums(0)
            with pe.Fori(0, B - 1) as b:
                keys(b + 1)
                values(b + 1)
                features(b + 1)
                outputs(b)
                sums(b + 1)
                att_transposes(0, pl, b)
            outputs(B - 1)
            att_transposes(0, pl, B - 1)
            project_out(0)

            def ffn(layer):
                transposes(2 * layer + 1)
                pe.wait_ge(phase, (4, 8)[layer])
                plan["route", layer].free(pe, "l")
                for t in range(TT):
                    for n, (sh, mh) in enumerate(PASSES):
                        for k in range(KC):
                            ins = nc.tensor.matmul(psum[:, 7, t * 16:(t + 1) * 16], nT[sh][:, k, t * P:(t + 1) * P], route_w[layer][mh][:, k, :],
                                                   start=n == 0 and k == 0, stop=n == 2 and k == KC - 1)
                ins.then_inc(psum_full[7].sem, 1)
                first = NBLK[0] * layer
                sl = plan["slots", layer]

                def count_tokens():
                    pe.wait_ge(picks_ready, layer + 1)
                    sl.free(pe, "r")
                    for t in range(TT + 1):
                        dst = psum[:, 6, t * E:(t + 1) * E]
                        if t < TT:
                            nc.tensor.matmul(dst, before16[:], oh_sum[:, t, :], start=True, stop=t == 0)
                        for b in range(t):
                            ins = nc.tensor.matmul(dst, ones16[:], oh_sum[:, b, :], start=t == TT and b == 0, stop=b == t - 1)
                    ins.then_inc(sl.full_sem("r"), 1)

                def fill_slots():
                    pe.wait_ge(tables_ready, layer + 1)
                    sl.free(pe, "i")
                    for n in range(NC2):
                        ins = nc.tensor.matmul(psum[:, 5, 0:NHALF], oh_low[:, n, :], oh_high[:, n, :], start=n == 0, stop=n == NC2 - 1)
                    ins.then_inc(sl.full_sem("i"), 1)

                def blk(k, par):
                    pl, rnd = of_block(layer, k)
                    pe.wait_ge(w_split, k + first + 1)
                    for u in range(UNITS):
                        c, m = divmod(u, IH)
                        m0, mn = IT[m]
                        if u >= 2 or k > 0:
                            pe.wait_ge(h_ready, (k + first) * UNITS + u - 1)
                        for n, w in enumerate("gu"):
                            product(psum[0:mn, 2 * (u % 2) + n, 0:CW],
                                    lambda h, kc: wsp[par][h][:, n * GN + kc * I + m0:n * GN + kc * I + m0 + mn],
                                    lambda h, kc: nT[h][:, kc, c * CW:(c + 1) * CW], pl.full_sem(f"{w}{u}"))
                        if k == 0 and u == RANKS_AT:
                            count_tokens()
                    if k == 0:
                        fill_slots()
                    for t in range(TT):
                        c = (t * P + P - 1) // CW
                        pe.wait_ge(hT_ready, (k + first) * UNITS + IH * (c + 1))
                        pl.free(pe, f"d{t}", rnd)
                        n = 0
                        for sh, mh in PASSES:
                            for m, (m0, mn) in enumerate(IT):
                                ins = nc.tensor.matmul(psum[:, 4 + t % 4, :], hT[sh][0:mn, m, t * P:(t + 1) * P],
                                                       wsp[par][mh][0:mn, 2 * GN + m * D:2 * GN + (m + 1) * D],
                                                       start=n == 0, stop=n == 3 * IH - 1)
                                n += 1
                        ins.then_inc(pl.full_sem(f"d{t}"), 1)

                tl = plan["tile", layer]
                tile0 = NTILE * layer

                def turn_rows(i, j, par):
                    pe.wait_ge(gathered[par], j * 32 + 32 * (1 + (NTILE // 2 + PAIRS + 1 - par) * layer))
                    for q in range(HALVES):
                        tl.free(pe, f"x{q}", i)
                        for k in range(KC):
                            ins = nc.tensor.transpose(psum[:, 6 + q, k * P:(k + 1) * P], rows[par][:, q, k * P:(k + 1) * P], ident[:])
                        ins.then_inc(tl.full_sem(f"x{q}"), 1)

                def tile(i, j, par, following=True):
                    w = wsp[1 - par]
                    for q in range(HALVES):
                        tl.free_after(pe, f"x{q}", i)
                    pe.wait_ge(gw_split, i * len(PIECE) + (tile0 * len(PIECE) + 2))
                    for m, (m0, mn) in enumerate(IT):
                        if not isinstance(i, int) or i or layer:
                            pe.wait_ge(gh_ready, i * IH + (tile0 * IH + m - IH + 1))
                        for n in range(2):
                            product(psum[0:mn, m, n * SLOTS:(n + 1) * SLOTS],
                                    lambda h, kc: w[h][:, n * GN + kc * I + m0:n * GN + kc * I + m0 + mn],
                                    lambda h, kc: xg[h][:, kc, :], tl.full_sem(f"u{m}") if n else None)
                    if following:
                        turn_rows(i + 1, j + par, 1 - par)
                    pe.wait_ge(gw_split, i * len(PIECE) + (tile0 * len(PIECE) + 3))
                    for q in range(HALVES):
                        tl.free(pe, f"y{q}", i)
                        n = 0
                        for m, (m0, mn) in enumerate(IT):
                            if q == 0:
                                pe.wait_ge(gh_split, i * IH + (tile0 * IH + m + 1))
                            for sh, mh in PASSES:
                                ins = nc.tensor.matmul(psum[:, 4 + q, :], hg[sh][0:mn, m, q * P:(q + 1) * P],
                                                       w[mh][0:mn, 2 * GN + m * D:2 * GN + (m + 1) * D], start=n == 0, stop=n == 3 * IH - 1)
                                n += 1
                        ins.then_inc(tl.full_sem(f"y{q}"), 1)

                blk(0, 0)
                pe.wait_ge(h_ready, (first + 1) * UNITS)
                turn_rows(0, 0, 0)
                tile(0, 0, 0)
                tile(1, 0, 1)
                with pe.Fori(1, NTILE // 2 - 1) as j:
                    tile(j * 2, j, 0)
                    tile(j * 2 + 1, j, 1)
                tile(NTILE - 2, NTILE // 2 - 1, 0)
                tile(NTILE - 1, NTILE // 2 - 1, 1, False)
                for k in range(1, NBLK[layer]):
                    blk(k, k % 2)

            if stop >= 2:
                ffn(0)
            if stop >= 3:
                pe.wait_ge(stage_used, 7)
                transposes(2)
                pe.wait_ge(phase, 6)
                pl = plan["q", 1]
                with pe.Fori(0, NCH) as c:
                    for m in range(KC):
                        pl.free(pe, f"q{m}", c)
                        product(psum[:, m, 0:CW], lambda h, k: wq[h][:, k, m * P:(m + 1) * P], lambda h, k: col(nT[h], c, CW)[:, k, :],
                                psum_full[m].sem)
                pl = plan["att", 1]

                def keys1(b):
                    pe.wait_ge(ctx_split, b + B + 1)
                    pl.free(pe, "k", b)
                    product(psum[:, 7, 0:SK], lambda h, k: wk[h][:, k, 0:P], lambda h, k: ctx_s[h][:, k, :], psum_full[7].sem)

                def values1(b):
                    pl.free(pe, "v", b)
                    for t, (t0, tn) in enumerate(KT):
                        product(psum[0:tn, 7, t * P:(t + 1) * P], lambda h, k: ctx_s[h][:, k, t0:t0 + tn], lambda h, k: wk[h][:, k, P:2 * P],
                                psum_full[7].sem if t == 2 else None)

                def heads(b, par, before, after):
                    pl.free(pe, "k", b + 1)
                    pe.wait_ge(q1_ready, b + 1)

                    def scores(h):
                        if h >= NS:
                            pe.wait_ge(exp_done, b * NH + h + 1 - NS)
                        elif before:
                            pe.wait_ge(exp_done, b * NH + h + 1 - NS)
                        for n, (sh, mh) in enumerate(PASSES):
                            ins = nc.tensor.matmul(psum[0:S, h % NS, 0:SK], q1[par][sh][:, h, :], k1[par][mh][:, h // 4, :], start=n == 0, stop=n == 2)
                        ins.then_inc(psum_full[h % NS].sem, 1)

                    def turn(h):
                        pe.wait_ge(exp_done, b * NH + h + 1)
                        for t in range(3):
                            ins = nc.tensor.transpose(psum[:, pl.bank(f"pT{h}"), t * S:(t + 1) * S], pr[h % NS][0:S, t * P:(t + 1) * P], ident[0:S, 0:S])
                        ins.then_inc(pl.full_sem(f"pT{h}"), 1)

                    def weigh(h):
                        pe.wait_ge(pT_ready, b * NH + h + 1)
                        if h == 0 and before:
                            pe.wait_ge(norm_ready.sem, norms["att", 1].at(b - 1))
                        for t, (t0, tn) in enumerate(KT):
                            ins = nc.tensor.matmul(psum[0:S, 4, h * HD:(h + 1) * HD], pT[h % 2][0:tn, t, :], v1[par][0:tn, t, (h // 4) * HD:(h // 4 + 1) * HD],
                                                   start=t == 0, stop=t == 2)
                        if h == NH - 1:
                            ins.then_inc(psum_full[4].sem, 1)

                    scores(0)
                    scores(1)
                    for h in range(NH):
                        if h + 2 < NH:
                            scores(h + 2)
                        if h >= 2:
                            weigh(h - 2)
                        turn(h)
                        if before and h == 2:
                            att_transposes(1, pl, b - 1)
                        if after and h == K_AT:
                            keys1(b + 1)
                        if after and h == V_AT:
                            values1(b + 1)
                    weigh(NH - 2)
                    weigh(NH - 1)

                keys1(0)
                values1(0)
                heads(0, 0, False, True)
                with pe.Fori(0, B // 2 - 1) as j:
                    heads(j * 2 + 1, 1, True, True)
                    heads(j * 2 + 2, 0, True, True)
                heads(B - 1, 1, True, False)
                att_transposes(1, pl, B - 1)
                project_out(1)
            if stop >= 4:
                ffn(1)


STOP = 4


def kernel(**inputs):
    import numpy as np
    import concourse.bacc as bacc
    from concourse.bass_utils import run_bass_kernel_spmd

    v = {k: np.asarray(t) for k, t in inputs.items()}

    def chunks(w):
        return w.reshape(KC, P, -1).transpose(1, 0, 2)

    def per_part(b):
        return b.reshape(KC, P).T

    def block_weights(gate, up, down):
        n = gate.shape[0]
        g, u = (w.reshape(n, KC, P, I).transpose(0, 2, 1, 3).reshape(n, P, KC * I) for w in (gate, up))
        d = np.zeros((n, IH * P, D), np.float32)
        d[:, 0:I] = down
        d = d.reshape(n, IH, P, D).transpose(0, 2, 1, 3).reshape(n, P, IH * D)
        return np.concatenate([g, u, d], axis=2)

    def cut(w, axis):
        n = w.shape[axis] // I
        return w.reshape(n, I, D) if axis == 0 else w.reshape(D, n, I).transpose(1, 0, 2)

    mask_f = np.zeros((P, B, 3), np.float32)
    mask_t = v["mask_BxS2_ff1"].T
    for t, (t0, tn) in enumerate(KT):
        mask_f[0:tn, :, t] = mask_t[t0:t0 + tn]
    bias_gu = np.zeros((P, NBLK[1], IH, 2), np.float32)
    tokens = np.arange(TP, dtype=np.float32)
    tokens[T:] = 0
    for n, name in enumerate(("L1_ffn_s_gate_b", "L1_ffn_s_up_b")):
        for k in range(NBLK[1]):
            for m, (m0, mn) in enumerate(IT):
                bias_gu[0:mn, k, m, n] = v[name][k * I + m0:k * I + m0 + mn]
    slopes = (2.0 ** (-8.0 / NH)) ** np.arange(1, NH + 1, dtype=np.float32)
    slopes = slopes.astype(np.float32)
    q_aug = np.stack([np.repeat(slopes[:, None], S, 1), -slopes[:, None] * np.arange(S, dtype=np.float32)[None, :]])
    q_aug = np.stack([q_aug.astype(np.float16), (q_aug - q_aug.astype(np.float16)).astype(np.float16)])
    k_aug = np.stack([np.repeat(np.arange(SK, dtype=np.float16)[None], NG, 0), np.ones((NG, SK), np.float16)])
    arrays = {
        "x": v["x"].reshape(T, D),
        "ctxT": v["ctx_2048"].transpose(0, 2, 1).reshape(B, KC, P, SK).transpose(0, 2, 1, 3),
        "mask_f": mask_f,
        "mask_b": v["mask_BxS2_bf1"].view(np.uint8).reshape(1, B, SK).repeat(NMASK, 0),
        "gates": np.concatenate([v["g_xattn"], v["g_ffn"]])[None].repeat(P, 0),
        "w_attn0": np.stack([chunks(v[f"L0_xattn_{w}"].T) for w in ("Wq", "Wk", "Wv", "Wo")]),
        "w_attn1": np.stack([chunks(v[f"L1_xattn_{w}"]) for w in ("Wq", "Wo")]),
        "w_kv1": chunks(np.concatenate([v["L1_xattn_Wk"], v["L1_xattn_Wv"]], axis=1)),
        "wqf": v["L0_xattn_Wqf"].T, "wkf": v["L0_xattn_Wkf"].T,
        "bq": per_part(v["L0_xattn_bq"]), "bk": per_part(v["L0_xattn_bk"]),
        "bv": v["L0_xattn_bv"], "bo": v["L0_xattn_bo"], "bd": v["L1_ffn_s_down_b"],
        "route0": chunks(np.concatenate([v["L0_ffn_gate_w"].T, v["L0_ffn_shared_gate_w"]], axis=1)),
        "route1": chunks(v["L1_ffn_router_w"].T),
        "w_expert0": block_weights(v["L0_ffn_w_gate"], v["L0_ffn_w_up"], v["L0_ffn_w_down"]),
        "w_shared0": block_weights(cut(v["L0_ffn_sw_gate"], 1), cut(v["L0_ffn_sw_up"], 1), cut(v["L0_ffn_sw_down"], 0)),
        "w_expert1": block_weights(v["L1_ffn_gate_w"], v["L1_ffn_up_w"], v["L1_ffn_down_w"]),
        "w_shared1": block_weights(cut(v["L1_ffn_s_gate_w"], 1), cut(v["L1_ffn_s_up_w"], 1), cut(v["L1_ffn_s_down_w"], 0)),
        "bias_gu": bias_gu,
        "ident": np.eye(P, dtype=np.float32),
        "iota": np.arange(P, dtype=np.float32)[None].repeat(P, 0),
        "token": np.tile(tokens.reshape(TT, P).T, (1, 2)),
        "ones16": np.ones((P, P), np.float16), "before16": np.triu(np.ones((P, P), np.float16), 1),
        "q_aug": q_aug, "k_aug": k_aug,
    }
    arrays = {f"in_{k}": np.ascontiguousarray(t) for k, t in arrays.items()}
    nc = bacc.Bacc("TRN2", target_bir_lowering=False, num_devices=1)
    aps = {k[3:]: nc.dram_tensor(k, t.shape, mybir.dt.from_np(t.dtype), kind="ExternalInput").ap() for k, t in arrays.items()}
    out = nc.dram_tensor("out", (T, D), F32, kind="ExternalOutput").ap()
    build(nc, aps, out, STOP)
    r = run_bass_kernel_spmd(nc, [arrays], core_ids=[0])
    return r.results[0]["out"].reshape(B, S, D)
```
